# Optimizing a Trainium2 kernel written in Bass

```python
import numpy as np
import jax
import jax.numpy as jnp

def _softmax(x, axis=-1):
    return jax.nn.softmax(x, axis=axis)

def _gelu(x):
    return jax.nn.gelu(x, approximate=True)

def _silu(x):
    return jax.nn.silu(x)

def _sigmoid(x):
    return jax.nn.sigmoid(x)

def _layernorm(x, axis=-1, eps=1e-05):
    m = jnp.mean(x, axis=axis, keepdims=True)
    v = jnp.var(x, axis=axis, keepdims=True)
    return (x - m) / jnp.sqrt(v + eps)

def _scatter_add(tgt, idx, src, axis=0):
    return tgt.at[idx].add(src)

def _segment_sum(src, seg, n):
    return jax.ops.segment_sum(src, seg, n)
kernel_name = 'mk_metaformer_d1_conv_nhwc128_r4_08de2f'

def setup_inputs(seed: int=0):
    np.random.seed(seed)
    _w = jnp.asarray

    def _rec_inputs():
        import jax
        import jax.numpy as jnp
        _gk = jax.random.key(seed)
        x = -0.0002091 + 1 * jax.random.normal(jax.random.fold_in(_gk, 1), (16, 56, 56, 32), jnp.float32)
        return x
    x = _rec_inputs()

    def _L0_conv_setup():
        import jax, jax.numpy as jnp
        import numpy as np
        WS, SHIFT, HEADS = (7, 3, 4)

        def _rel_index(ws):
            coords = np.stack(np.meshgrid(np.arange(ws), np.arange(ws), indexing='ij')).reshape(2, -1)
            rel = (coords[:, :, None] - coords[:, None, :]).transpose(1, 2, 0)
            rel[:, :, 0] += ws - 1
            rel[:, :, 1] += ws - 1
            rel[:, :, 0] *= 2 * ws - 1
            return rel.sum(-1)

        def _attn_mask(H, W, ws, shift):
            img = np.zeros((H, W))
            cnt = 0
            sl = (slice(0, -ws), slice(-ws, -shift), slice(-shift, None))
            for h in sl:
                for w in sl:
                    img[h, w] = cnt
                    cnt += 1
            mw = img.reshape(H // ws, ws, W // ws, ws).transpose(0, 2, 1, 3).reshape(-1, ws * ws)
            diff = mw[:, None, :] - mw[:, :, None]
            return np.where(diff != 0, -100.0, 0.0).astype(np.float32)
        key = jax.random.key(seed)
        ks = jax.random.split(key, 5)
        B, H, W, C = (16, 56, 56, 32)
        x = jax.random.normal(ks[0], (B, H, W, C), dtype=jnp.float32)
        w_qkv = jax.random.normal(ks[1], (C, 3 * C), dtype=jnp.float32) * 0.02
        b_qkv = jnp.zeros((3 * C,), dtype=jnp.float32)
        w_proj = jax.random.normal(ks[2], (C, C), dtype=jnp.float32) * 0.02
        b_proj = jnp.zeros((C,), dtype=jnp.float32)
        rel_table = jax.random.normal(ks[3], ((2 * WS - 1) ** 2, HEADS), dtype=jnp.float32) * 0.02
        return {'x': x, 'w_qkv': w_qkv, 'b_qkv': b_qkv, 'w_proj': w_proj, 'b_proj': b_proj, 'rel_table': rel_table}
    _L0_conv_all = _L0_conv_setup()
    _L0_conv_in = {k: v for k, v in _L0_conv_all.items() if k in ('w_qkv', 'b_qkv', 'w_proj', 'b_proj', 'rel_table')}
    del _L0_conv_all

    def _L0_ffn_setup():
        import jax, jax.numpy as jnp
        import numpy as np
        B, N, D, C, E, K = (8, 2048, 32, 32, 8, 2)
        key = jax.random.key(seed)
        k0, k1, k2 = jax.random.split(key, 3)
        x = jax.random.normal(k0, (B, N, D), dtype=jnp.float32)
        router_w = jax.random.normal(k1, (D, E), dtype=jnp.float32) * 0.05
        router_b = jnp.zeros((E,), dtype=jnp.float32)
        expert_w = jax.random.normal(k2, (E, D, C), dtype=jnp.float32) * (1.0 / np.sqrt(D))
        expert_b = jnp.zeros((E, C), dtype=jnp.float32)
        return {'x': x, 'router_w': router_w, 'router_b': router_b, 'expert_w': expert_w, 'expert_b': expert_b}
    _L0_ffn_all = _L0_ffn_setup()
    _L0_ffn_in = {k: v for k, v in _L0_ffn_all.items() if k in ('router_w', 'router_b', 'expert_w', 'expert_b')}
    del _L0_ffn_all
    return {'x': x, 'L0_conv_w_qkv': _L0_conv_in['w_qkv'], 'L0_conv_b_qkv': _L0_conv_in['b_qkv'], 'L0_conv_w_proj': _L0_conv_in['w_proj'], 'L0_conv_b_proj': _L0_conv_in['b_proj'], 'L0_conv_rel_table': _L0_conv_in['rel_table'], 'L0_ffn_router_w': _L0_ffn_in['router_w'], 'L0_ffn_router_b': _L0_ffn_in['router_b'], 'L0_ffn_expert_w': _L0_ffn_in['expert_w'], 'L0_ffn_expert_b': _L0_ffn_in['expert_b']}

def reference(x, L0_conv_w_qkv, L0_conv_b_qkv, L0_conv_w_proj, L0_conv_b_proj, L0_conv_rel_table, L0_ffn_router_w, L0_ffn_router_b, L0_ffn_expert_w, L0_ffn_expert_b):
    import jax
    import jax.numpy as jnp

    def _L0_conv_ref(x, w_qkv, b_qkv, w_proj, b_proj, rel_table):
        import jax, jax.numpy as jnp
        import numpy as np
        WS, SHIFT, HEADS = (7, 3, 4)

        def _rel_index(ws):
            coords = np.stack(np.meshgrid(np.arange(ws), np.arange(ws), indexing='ij')).reshape(2, -1)
            rel = (coords[:, :, None] - coords[:, None, :]).transpose(1, 2, 0)
            rel[:, :, 0] += ws - 1
            rel[:, :, 1] += ws - 1
            rel[:, :, 0] *= 2 * ws - 1
            return rel.sum(-1)

        def _attn_mask(H, W, ws, shift):
            img = np.zeros((H, W))
            cnt = 0
            sl = (slice(0, -ws), slice(-ws, -shift), slice(-shift, None))
            for h in sl:
                for w in sl:
                    img[h, w] = cnt
                    cnt += 1
            mw = img.reshape(H // ws, ws, W // ws, ws).transpose(0, 2, 1, 3).reshape(-1, ws * ws)
            diff = mw[:, None, :] - mw[:, :, None]
            return np.where(diff != 0, -100.0, 0.0).astype(np.float32)
        B, H, W, C = x.shape
        ws, shift, nh = (WS, SHIFT, HEADS)
        d = C // nh
        scale = d ** (-0.5)
        N = ws * ws
        mask = jnp.asarray(_attn_mask(H, W, ws, shift))
        rel_idx = _rel_index(ws).reshape(-1)
        xs = jnp.roll(x, (-shift, -shift), axis=(1, 2))
        xw = xs.reshape(B, H // ws, ws, W // ws, ws, C).transpose(0, 1, 3, 2, 4, 5).reshape(-1, N, C)
        Bn = xw.shape[0]
        qkv = (xw @ w_qkv + b_qkv).reshape(Bn, N, 3, nh, d).transpose(2, 0, 3, 1, 4)
        q, k, v = (qkv[0] * scale, qkv[1], qkv[2])
        attn = jax.nn.softmax(jnp.einsum('bhnd,bhmd->bhnm', q, k), axis=-1)
        bias = rel_table[rel_idx].reshape(N, N, nh).transpose(2, 0, 1)
        attn = attn + bias[None]
        nW = mask.shape[0]
        attn = (attn.reshape(Bn // nW, nW, nh, N, N) + mask[None, :, None]).reshape(Bn, nh, N, N)
        out = jnp.einsum('bhnm,bhmd->bhnd', attn, v).transpose(0, 2, 1, 3).reshape(Bn, N, C)
        out = out @ w_proj + b_proj
        out = out.reshape(B, H // ws, W // ws, ws, ws, C).transpose(0, 1, 3, 2, 4, 5).reshape(B, H, W, C)
        return jnp.roll(out, (shift, shift), axis=(1, 2))

    def _L0_ffn_ref(x, router_w, router_b, expert_w, expert_b):
        import jax, jax.numpy as jnp
        import numpy as np
        B, N, D, C, E, K = (8, 2048, 32, 32, 8, 2)
        router_probs = jax.nn.softmax(x @ router_w + router_b, axis=-1)
        top_p, top_i = jax.lax.top_k(router_probs, K)
        top_p = top_p / jnp.sum(top_p, axis=-1, keepdims=True)
        expert_out = jnp.einsum('bnd,edc->bnec', x, expert_w) + expert_b
        gathered = jnp.take_along_axis(expert_out, top_i[..., None], axis=2)
        return jnp.einsum('bnk,bnkc->bnc', top_p, gathered)

    def _gn(v, G=32, eps=1e-05):
        B_, H_, W_, C_ = v.shape
        g = v.reshape(B_, H_, W_, G, C_ // G)
        m = jnp.mean(g, axis=(1, 2, 4), keepdims=True)
        s = jnp.var(g, axis=(1, 2, 4), keepdims=True)
        return ((g - m) / jnp.sqrt(s + eps)).reshape(v.shape)

    def _ln_c(v, eps=1e-06):
        m = jnp.mean(v, axis=-1, keepdims=True)
        s = jnp.var(v, axis=-1, keepdims=True)
        return (v - m) / jnp.sqrt(s + eps)

    def _ln_t(v, eps=1e-05):
        m = jnp.mean(v, axis=-1, keepdims=True)
        s = jnp.var(v, axis=-1, keepdims=True)
        return (v - m) / jnp.sqrt(s + eps)

    def _to_tokens(v):
        B_, H_, W_, C_ = v.shape
        return v.reshape(B_, H_ * W_, C_)

    def _from_tokens(t, like):
        return t.reshape(like.shape)
    x = x + _L0_conv_ref(_ln_c(x), L0_conv_w_qkv, L0_conv_b_qkv, L0_conv_w_proj, L0_conv_b_proj, L0_conv_rel_table)
    t = _to_tokens(x)
    t = t + _L0_ffn_ref(_ln_t(t), L0_ffn_router_w, L0_ffn_router_b, L0_ffn_expert_w, L0_ffn_expert_b)
    x = _from_tokens(t, x)
    return x

_drawn_inputs = setup_inputs


def setup_inputs(seed=0):
    import zlib

    import numpy as np

    out = dict(_drawn_inputs(seed))
    spreads = {'L0_conv_b_qkv': (0.0, 0.1),
     'L0_conv_b_proj': (0.0, 0.716),
     'L0_ffn_router_b': (0.0, 0.44),
     'L0_ffn_expert_b': (0.0, 0.8)}
    factors = {'L0_conv_rel_table': 200.0}
    for name, (base, spread) in spreads.items():
        noise = np.random.default_rng([zlib.crc32(name.encode()), seed]).standard_normal(out[name].shape)
        drawn = base * np.exp(spread * noise) if base else spread * noise
        out[name] = jnp.asarray(drawn.astype(out[name].dtype))
    for name, factor in factors.items():
        out[name] = (out[name] * factor).astype(out[name].dtype)
    return out
```

```python
from contextlib import ExitStack

import numpy as np

import concourse.bass as bass
from concourse import mybir

F32 = mybir.dt.float32
BF16 = mybir.dt.bfloat16
ALU = mybir.AluOpType
ACT = mybir.ActivationFunctionType
AX = mybir.AxisListType.X

IMAGES, SIDE, C = 16, 56, 32
WS, SHIFT, HEADS = 7, 3, 4
D = C // HEADS
SCALE = float(D) ** -0.5
N = WS * WS
E = 8
UNITS = 16
ROWS = 2 * SIDE
A = 4
Q = 16
TOK = A * WS
COLS = Q * N
HALF = COLS // 2
PAD = 64
SLOT = 32
HN = HEADS * N
GROUPS = 4
LN1_EPS, LN2_EPS = 1e-6, 1e-5
BELOW_ALL = -3.0e38
ROW_CUTS = ((0, 48), (48, 53), (53, 56))
COL_CUTS = ((0, 25), (25, 28))
TRANSFERS = 2 * len(ROW_CUTS) * len(COL_CUTS)

PRE_FILLS = 12
ACC_FILLS = 4
RNG_FILLS = 24
AHEAD = 5
TOP2_STEPS = 22
GAP_STEP = 11

PRE_ORDER = ("load", "norm1_center", "norm1_scale", "xt", "xt", "qk", "qk", "qk", "qk", "place",
             "v", "v", "ob", "ob", "obt", "obt")
SIDE_TASKS = {
    (0, 0): [("y", 0)], (0, 1): [("y", 1)], (0, 2): [("back", 0)], (1, 0): [("back", 1)],
    (1, 1): [("load", 0)], (1, 2): [("norm2_center", 0)], (2, 2): [("norm2_scale", 0)],
    (3, 0): [("norm1_center", 0)], (4, 0): [("norm1_scale", 0)], (4, 1): [("x2t", 0)],
    (4, 2): [("x2t", 1)], (5, 0): [("router", 0)], (5, 1): [("xt", 0)],
    (5, 2): [("xt", 1), ("top2_pick", 0)], (6, 0): [("qk", 0)], (6, 1): [("qk", 1)],
    (6, 2): [("qk", 2), ("top2_exp", 0)], (7, 0): [("qk", 3), ("place", 0)],
    (7, 1): [("top2_weigh", 0)], (7, 2): [("v", 0)], (8, 0): [("wt", 0)], (8, 1): [("v", 1)],
    (8, 2): [("mix", 0)], (9, 0): [("ob", 0)], (9, 1): [("mix", 1)], (9, 2): [("mix", 2)],
    (10, 0): [("ob", 1)], (10, 1): [("mix", 3)], (10, 2): [("mix", 4)],
    (11, 0): [("obt", 0), ("mix", 5)], (11, 1): [("mix", 6)], (11, 2): [("mix", 7)],
    (12, 0): [("obt", 1), ("mix", 8), ("mix_drain", 0)], (12, 1): [("mix", 9)],
    (12, 2): [("mix", 10)], (13, 0): [("mix", 11)], (13, 1): [("mix", 12)],
    (13, 2): [("mix", 13)], (14, 0): [("mix", 14)], (14, 1): [("mix", 15)],
    (14, 2): [("mix", 16), ("mix_drain", 1)], (15, 0): [("final", 0)],
    (15, 1): [("final", 1)], (15, 2): [("store", 0)],
}


class Unit:

    def __init__(self, n, slab, par, number=None):
        self.n, self.slab, self.par = n, slab, par
        self.number = number

    def has_before(self, back):
        return self.number is None or self.number >= back

    def before(self, back):
        return Unit(self.n - back, None, None)


def fixed(n):
    return Unit(n, n // 2, n % 2, n)


def in_loop(it, offset):
    return Unit(it * 2 + offset, it + offset // 2, offset % 2)


def macro_step(att, pre, post, ahead):
    def side(place):
        for name, i in SIDE_TASKS.get(place, ()):
            unit = pre if name in PRE_ORDER else post
            if unit is not None:
                yield name, unit, i

    for s in range(Q):
        yield "scores", att, s
        yield from side((s, 0))
        unit, q = (att, s + AHEAD) if s + AHEAD < Q else (ahead, s + AHEAD - Q)
        if unit is not None:
            yield "maximum", unit, q
            if q % 4 == 3:
                yield "split", unit, q // 4
        if s % 4 == 0 and s:
            yield "normalise", att, s // 4 - 1
        yield from side((s, 1))
        yield "pv", att, s
        yield from side((s, 2))
        if s % 4 == 3:
            yield "pv_drain", att, s // 4
            g = (s // 4 + 1) % GROUPS
            if g or ahead is not None:
                yield "shift", att if g else ahead, g
    yield "normalise", att, GROUPS - 1


def program(eng):
    first, last = fixed(0), fixed(UNITS - 1)
    for k, name in enumerate(PRE_ORDER):
        yield name, first, PRE_ORDER[:k].count(name)
    for q in range(AHEAD):
        yield "maximum", first, q
        if q == 3:
            yield "split", first, 0
    yield "shift", first, 0
    yield from macro_step(fixed(0), fixed(1), None, fixed(1))
    yield from macro_step(fixed(1), fixed(2), fixed(0), fixed(2))
    with eng.Fori(0, (UNITS - 4) // 2) as it:
        u1, u2, u3, u4 = (in_loop(it, k) for k in (1, 2, 3, 4))
        yield from macro_step(u2, u3, u1, u3)
        yield from macro_step(u3, u4, u2, u4)
    yield from macro_step(fixed(UNITS - 2), last, fixed(UNITS - 3), last)
    yield from macro_step(last, None, fixed(UNITS - 2), None)
    for place in sorted(SIDE_TASKS):
        for name, i in SIDE_TASKS[place]:
            if name not in PRE_ORDER:
                yield name, last, i


def shape_constants():
    jj, ii = np.arange(N) // WS, np.arange(N) % WS
    late = lambda t: (t >= WS - SHIFT).astype(int)
    mask = np.zeros((128, 4, PAD), np.float32)
    for kind in range(4):
        for g in range(2):
            region = late(ii) * (kind & 1) + 2 * late(jj) * ((kind >> 1) & g)
            mask[PAD * g:PAD * g + N, kind, :N] = np.where(region[:, None] != region[None, :], -100.0, 0.0)
    shift_sel = np.zeros((128, 4, 2, 2, PAD), np.float32)
    for part in range(2):
        for q in range(4):
            for a in range(A):
                shift_sel[16 * part + 4 * q + a, q, a // 2, a % 2, :N] = 1.0
    z_sel = np.zeros((128, 128), np.float32)
    for h in range(HEADS):
        for s in range(16):
            z_sel[SLOT * h + 16 + s, SLOT * h + s] = 1.0
            z_sel[SLOT * h + 16 + s, SLOT * h + 16 + s] = 1.0
    weight_sel = np.zeros((96, E, A, C), np.float32)
    for part in range(3):
        for a in range(A):
            for e in range(E):
                weight_sel[32 * part + 8 * a + e, e, a, :] = 1.0
    first3 = np.zeros((128, 128), np.float32)
    first3[:3] = 1.0
    return {
        "c_ident": (np.eye(128, dtype=np.float32), False),
        "c_identb": (np.eye(128, dtype=np.float32), True),
        "c_mask": (mask.reshape(128, -1), False),
        "c_shift_sel": (shift_sel.reshape(128, -1), True),
        "c_z_sel": (z_sel, False),
        "c_weight_sel": (weight_sel.reshape(96, -1), True),
        "c_first3": (first3, True),
        "c_rank": (np.tile(np.arange(E, 0, -1, dtype=np.float32), (ROWS, 1)), False),
    }


def metaformer_block(nc, x, w_qkv, b_qkv, w_proj, b_proj, rel_table, router_w, router_b, expert_w,
                     expert_b, c_ident, c_identb, c_mask, c_shift_sel, c_z_sel, c_weight_sel,
                     c_first3, c_rank, out):
    with ExitStack() as ctx:
        def sb(name, shape, dt=F32):
            return ctx.enter_context(nc.sbuf_tensor(name, shape, dt))

        def bank(name):
            return ctx.enter_context(nc.psum_tensor(name, [128, 512], F32))

        ident, z_sel = sb("ident", [128, 128]), sb("z_sel", [128, 128])
        identb, first3 = sb("identb", [128, 128], BF16), sb("first3", [128, 128], BF16)
        shift_sel = sb("shift_sel", [128, 4, 2, 128], BF16)
        weight_sel = sb("weight_sel", [96, E, 128], BF16)
        rank = sb("rank", [ROWS, E])
        mask = sb("mask", [128, 4, PAD])
        wq, wk = sb("wq", [128, 128]), sb("wk", [128, 128])
        wv = sb("wv", [128, 2, 2, C])
        w_proj_o = sb("w_proj_o", [128, 2, C])
        w_proj_b = sb("w_proj_b", [128, 2, 2, A, C])
        wr = sb("wr", [128, A, E])
        we = sb("we", [128, E, A, C])
        biases = sb("biases", [128, 4])
        rb = sb("rb", [ROWS, E])
        rel_raw = sb("rel_raw", [128, N, HEADS])
        bt = sb("bt", [128, HEADS, 4, PAD])
        eb_raw, eb_rest = sb("eb_raw", [96, 128]), sb("eb_rest", [96, 128])
        eb = sb("eb", [96, 3, 128], BF16)
        bv_raw, bv_rest = sb("bv_raw", [3, C]), sb("bv_rest", [3, C])
        bv_parts = sb("bv_parts", [3, 3, C], BF16)
        bv_rows = sb("bv_rows", [3, 2, C])
        bv = sb("bv", [128, Q, C], BF16)
        minus_half = sb("minus_half", [ROWS, TOK])

        xin = [sb(f"xin{i}", [ROWS, A, WS, C]) for i in range(2)]
        xc1, sq1 = sb("xc1", [ROWS, WS, A, C]), sb("sq1", [ROWS, WS, A, C])
        st1 = sb("st1", [ROWS, 5, TOK])
        xt = sb("xt", [128, Q, WS, WS])
        qp, kp = sb("qp", [128, Q, N]), sb("kp", [128, Q, PAD])
        qbd = [sb(f"qbd{i}", [128, Q, HEADS, N]) for i in range(2)]
        kz = [sb(f"kz{i}", [128, Q, A, PAD]) for i in range(2)]
        vb = [sb(f"vb{i}", [128, Q, 2, HEADS, SLOT]) for i in range(2)]
        obs = sb("obs", [128, 8, 2, 2, 2, 16])
        obt = [sb(f"obt{i}", [128, 2, 8, N]) for i in range(2)]
        mx = [sb(f"mx{i}", [2 * N, 2, 4, A]) for i in range(2)]
        ms = [sb(f"ms{i}", [2 * N, 2, 2, 16], BF16) for i in range(2)]
        mr = [sb(f"mr{i}", [128, HN], BF16) for i in range(2)]
        pt = [sb(f"pt{i}", [128, 2, HEADS, N]) for i in range(2)]
        oe = [sb(f"oe{i}", [128, 4, 2, N]) for i in range(2)]
        rz = [sb(f"rz{i}", [128, 4, 2, N]) for i in range(2)]
        on = sb("on", [128, 2, Q, N])
        ym = sb("ym", [128, WS, ROWS])
        x2, xc2, sq2 = (sb(n, [ROWS, WS, A, C]) for n in ("x2", "xc2", "sq2"))
        yo = sb("yo", [ROWS, A, WS, C])
        st2 = sb("st2", [ROWS, 5, TOK])
        x2t = sb("x2t", [128, COLS])
        logits, pick1, pick2 = (sb(n, [ROWS, TOK, E]) for n in ("logits", "pick1", "pick2"))
        tmp, mixw = sb("tmp", [ROWS, TOK, E]), sb("mixw", [ROWS, TOK, E])
        top = sb("top", [ROWS, 8, TOK])
        w_parts = sb("w_parts", [ROWS, WS, 3, A * E], BF16)
        wt = sb("wt", [96, COLS], BF16)
        zt = [sb(f"zt{i}", [128, HALF]) for i in range(2)]

        ps_max, ps_scores, ps_pv, ps_small = bank("ps_max"), bank("ps_scores"), bank("ps_pv"), bank("ps_small")
        ps_pre, ps_acc, ps_rng = bank("ps_pre"), bank("ps_acc"), bank("ps_rng")

        per_unit = {
            "x_loaded": 16 * TRANSFERS, "out_stored": 16 * TRANSFERS,
            "sum1": 1, "mean1": 1, "centered1": 1, "squared1": 1, "sqsum1": 1, "var1": 1,
            "rstd1": 1, "normed1": 1,
            "sum2": 1, "mean2": 1, "centered2": 1, "squared2": 1, "sqsum2": 1, "var2": 1,
            "rstd2": 1, "normed2": 1,
            "pre_filled": PRE_FILLS, "pre_drained": PRE_FILLS,
            "q_placed": 16 * A * HEADS, "k_placed": 16 * A,
            "max_filled": Q, "max_taken": Q, "shift_rounded": GROUPS, "shift_split": GROUPS,
            "shift_turned": GROUPS, "shift_rows_ready": GROUPS,
            "scores_filled": Q, "probs_ready": Q, "pv_done": Q, "pv_drained": GROUPS,
            "sums_spread": GROUPS, "sums_inverted": GROUPS, "o_normed": GROUPS,
            "projected": 2, "acc_drained": ACC_FILLS,
            "rng_filled": RNG_FILLS, "rng_drained": RNG_FILLS,
            "top2_step": TOP2_STEPS, "gap_exp": 1, "mixed": 16,
        }
        def sem(name):
            return ctx.enter_context(nc.semaphore(name))

        x_loaded = sem("x_loaded")
        out_stored = sem("out_stored")
        sum1 = sem("sum1")
        mean1 = sem("mean1")
        centered1 = sem("centered1")
        squared1 = sem("squared1")
        sqsum1 = sem("sqsum1")
        var1 = sem("var1")
        rstd1 = sem("rstd1")
        normed1 = sem("normed1")
        sum2 = sem("sum2")
        mean2 = sem("mean2")
        centered2 = sem("centered2")
        squared2 = sem("squared2")
        sqsum2 = sem("sqsum2")
        var2 = sem("var2")
        rstd2 = sem("rstd2")
        normed2 = sem("normed2")
        pre_filled = sem("pre_filled")
        pre_drained = sem("pre_drained")
        q_placed = sem("q_placed")
        k_placed = sem("k_placed")
        max_filled = sem("max_filled")
        max_taken = sem("max_taken")
        shift_rounded = sem("shift_rounded")
        shift_split = sem("shift_split")
        shift_turned = sem("shift_turned")
        shift_rows_ready = sem("shift_rows_ready")
        scores_filled = sem("scores_filled")
        probs_ready = sem("probs_ready")
        pv_done = sem("pv_done")
        pv_drained = sem("pv_drained")
        sums_spread = sem("sums_spread")
        sums_inverted = sem("sums_inverted")
        o_normed = sem("o_normed")
        projected = sem("projected")
        acc_drained = sem("acc_drained")
        rng_filled = sem("rng_filled")
        rng_drained = sem("rng_drained")
        top2_step = sem("top2_step")
        gap_exp = sem("gap_exp")
        mixed = sem("mixed")
        zeroed = sem("zeroed")
        zeroed_odd = sem("zeroed_odd")
        weights_loaded = sem("weights_loaded")
        weight_step = sem("weight_step")
        weights_ready = sem("weights_ready")

        def upto(name, unit, i=None):
            k = per_unit[name]
            return unit.n * k + (k if i is None else i + 1)

        def over(s, n):
            return s.unsqueeze(2).to_broadcast([s.shape[0], s.shape[1], n])

        def pieces(dram, tile, unit):
            view = tile.rearrange("p j k c -> p (j k) c")
            for b in range(2):
                for r0, r1 in ROW_CUTS:
                    for c0, c1 in COL_CUTS:
                        h = (r0 + SHIFT) % SIDE
                        w = (TOK * unit.par + c0 + SHIFT) % SIDE
                        yield (view[SIDE * b + r0:SIDE * b + r1, c0:c1, :],
                               dram[unit.slab * 2 + b, h:h + r1 - r0, w:w + c1 - c0, :])

        def weight_loads():
            yield ident[:, :], c_ident
            yield identb[:, :], c_identb
            yield first3[:, :], c_first3
            yield z_sel[:, :], c_z_sel
            yield rank[:, :], c_rank
            yield mask[:, :, :].rearrange("p k n -> p (k n)"), c_mask
            yield shift_sel[:, :, :, :].rearrange("p q s m -> p (q s m)"), c_shift_sel
            yield weight_sel[:, :, :].rearrange("p e m -> p (e m)"), c_weight_sel
            for a in range(A):
                r = slice(C * a, C * a + C)
                yield wq[r, r], w_qkv[:, 0:C]
                yield wk[r, r], w_qkv[:, C:2 * C]
                yield wv[r, a % 2, a // 2, :], w_qkv[:, 2 * C:3 * C]
                yield wr[r, a, :], router_w
                yield we[r, :, a, :], expert_w.rearrange("e d c -> d e c")
                yield biases[r, 0:1], b_qkv[0:C].unsqueeze(1)
                yield biases[r, 1:2], b_qkv[C:2 * C].unsqueeze(1)
                yield biases[r, 2:3], b_proj.unsqueeze(1)
                for part in range(3):
                    yield (eb_raw[32 * part + E * a:32 * part + E * a + E, C * a:C * a + C], expert_b)
            for h in range(HEADS):
                rows = w_proj[D * h:D * h + D, :]
                for g in range(2):
                    yield w_proj_o[SLOT * h + D * g:SLOT * h + D * g + D, g, :], rows
                for b in range(2):
                    for a in range(A):
                        p0 = 64 * b + 32 * (h % 2) + D * a
                        yield w_proj_b[p0:p0 + D, b, h // 2, a, :], rows
            yield rb[:, :], router_b.unsqueeze(0).to_broadcast([ROWS, E])
            for k in range(3):
                yield bv_raw[k:k + 1, :], b_qkv[2 * C:3 * C].unsqueeze(0)

        def rel_loads():
            table = rel_table.rearrange("(r c) h -> c r h", c=2 * WS - 1)
            for g in range(2):
                for mj in range(WS):
                    for mi in range(WS):
                        row = PAD * g + mj * WS + mi
                        yield (rel_raw[row:row + 1, :, :].rearrange("p (j i) h -> p j i h", j=WS),
                               table[WS - 1 - mj:2 * WS - 1 - mj, WS - 1 - mi:2 * WS - 1 - mi, :].unsqueeze(0))

        weight_list, rel_list = list(weight_loads()), list(rel_loads())
        all_loaded = 16 * (len(weight_list) + len(rel_list))
        block = ctx.enter_context(nc.Block())

        @block.sync
        def _(sp):
            def load(v, _):
                if v.has_before(2):
                    sp.wait_ge(rng_drained, upto("rng_drained", v.before(2), 1))
                for tile, dram in pieces(x, xin[v.par], v):
                    sp.dma_start(tile, dram).then_inc(x_loaded, 16)

            def place(v, _):
                sp.wait_ge(pre_drained, upto("pre_drained", v, 5))
                if v.has_before(2):
                    sp.wait_ge(scores_filled, upto("scores_filled", v.before(2)))
                if v.number == 1:
                    sp.wait_ge(zeroed_odd, 1)
                for h in range(HEADS):
                    for a in range(A):
                        r = slice(C * a + D * h, C * a + D * h + D)
                        sp.dma_start(qbd[v.par][r, :, h, :], qp[r, :, :]).then_inc(q_placed, 16)
                for a in range(A):
                    r = slice(C * a, C * a + C)
                    sp.dma_start(kz[v.par][r, :, a, :], kp[r, :, :]).then_inc(k_placed, 16)

            def store(w, _):
                sp.wait_ge(rng_drained, upto("rng_drained", w))
                for tile, dram in pieces(out, yo, w):
                    sp.dma_start(dram, tile).then_inc(out_stored, 16)

            sp.wait_ge(zeroed, 1)
            for dst, src in weight_list:
                sp.dma_start(dst, src).then_inc(weights_loaded, 16)
            for step, unit, i in program(sp):
                if step == "load":
                    load(unit, i)
                elif step == "place":
                    place(unit, i)
                elif step == "store":
                    store(unit, i)
            sp.wait_ge(out_stored, UNITS * per_unit["out_stored"])

        @block.gpsimd
        def _(pool):
            def norm1_center(v, _):
                pool.wait_ge(mean1, upto("mean1", v))
                if v.has_before(1):
                    pool.wait_ge(pre_filled, upto("pre_filled", v.before(1), 1))
                nc.gpsimd.tensor_tensor(
                    xc1[:, :, :, :], xin[v.par].rearrange("p j k c -> p k j c"),
                    st1[:, 1, :].rearrange("p (j k) -> p k j", j=A).unsqueeze(3).to_broadcast([ROWS, WS, A, C]),
                    ALU.add).then_inc(centered1, 1)

            def norm1_scale(v, _):
                pool.wait_ge(var1, upto("var1", v))
                nc.gpsimd.tensor_tensor(st1[:, 4, :], st1[:, 3, :], minus_half[:, :], ALU.pow).then_inc(rstd1, 1)
                pool.wait_ge(rstd1, upto("rstd1", v))
                pool.wait_ge(squared1, upto("squared1", v))
                xc = xc1[:, :, :, :].rearrange("p k j c -> p (k j) c")
                nc.gpsimd.tensor_tensor(xc, xc, over(st1[:, 4, :], C), ALU.mult).then_inc(normed1, 1)

            def norm2_center(w, _):
                pool.wait_ge(mean2, upto("mean2", w))
                if w.has_before(1):
                    pool.wait_ge(rng_filled, upto("rng_filled", w.before(1)))
                nc.gpsimd.tensor_tensor(
                    xc2[:, :, :, :].rearrange("p k j c -> p (k j) c"),
                    x2[:, :, :, :].rearrange("p k j c -> p (k j) c"), over(st2[:, 1, :], C), ALU.add).then_inc(centered2, 1)

            def norm2_scale(w, _):
                pool.wait_ge(var2, upto("var2", w))
                nc.gpsimd.tensor_tensor(st2[:, 4, :], st2[:, 3, :], minus_half[:, :], ALU.pow).then_inc(rstd2, 1)
                pool.wait_ge(rstd2, upto("rstd2", w))
                pool.wait_ge(squared2, upto("squared2", w))
                xc = xc2[:, :, :, :].rearrange("p k j c -> p (k j) c")
                nc.gpsimd.tensor_tensor(xc, xc, over(st2[:, 4, :], C), ALU.mult).then_inc(normed2, 1)

            def normalise(u, g):
                pool.wait_ge(sums_inverted, upto("sums_inverted", u, g))
                pool.wait_ge(pv_drained, upto("pv_drained", u, g))
                if g == 0:
                    if u.has_before(1):
                        pool.wait_ge(projected, upto("projected", u.before(1), 1))
                nc.gpsimd.tensor_tensor(
                    on[:, :, 4 * g:4 * g + 4, :], oe[g % 2].rearrange("p q s n -> p s q n"),
                    rz[g % 2].rearrange("p q s n -> p s q n"), ALU.mult).then_inc(o_normed, 1)

            nc.gpsimd.memset(minus_half[:, :], -0.5)
            nc.gpsimd.memset(qbd[1][:, :, :, :], 0.0)
            nc.gpsimd.memset(kz[1][:, :, :, :], 0.0)
            nc.gpsimd.memset(mr[1][:, :], 0.0).then_inc(zeroed_odd, 1)
            pool.wait_ge(weights_ready, 1)
            for step, unit, i in program(pool):
                if step == "norm1_center":
                    norm1_center(unit, i)
                elif step == "norm1_scale":
                    norm1_scale(unit, i)
                elif step == "norm2_center":
                    norm2_center(unit, i)
                elif step == "norm2_scale":
                    norm2_scale(unit, i)
                elif step == "normalise":
                    normalise(unit, i)

        @block.scalar
        def _(act):
            def norm1_center(v, _):
                if v.has_before(1):
                    act.wait_ge(sqsum1, upto("sqsum1", v.before(1)))
                act.wait_ge(centered1, upto("centered1", v))
                nc.scalar.activation(sq1[:, :, :, :], xc1[:, :, :, :], ACT.Square).then_inc(squared1, 1)

            def norm2_center(w, _):
                if w.has_before(1):
                    act.wait_ge(sqsum2, upto("sqsum2", w.before(1)))
                act.wait_ge(centered2, upto("centered2", w))
                nc.scalar.activation(sq2[:, :, :, :], xc2[:, :, :, :], ACT.Square).then_inc(squared2, 1)

            def xt_drain(v, i):
                act.wait_ge(pre_filled, upto("pre_filled", v, i))
                k0, k1 = (0, 4) if i == 0 else (4, 7)
                if i == 0:
                    if v.has_before(1):
                        act.wait_ge(pre_filled, upto("pre_filled", v.before(1), 7))
                nc.scalar.copy(xt[:, :, k0:k1, :].rearrange("p q k i -> p k q i"),
                                    ps_pre[:, 0:(k1 - k0) * ROWS].rearrange("p (k q i) -> p k q i", q=Q, i=WS)).then_inc(pre_drained, 1)

            def qk_drain(v, i):
                act.wait_ge(pre_filled, upto("pre_filled", v, 2 + i))
                src = ps_pre[:, 0:HALF].rearrange("p (q n) -> p q n", n=N)
                if i < 2:
                    if v.has_before(1):
                        act.wait_ge(q_placed, upto("q_placed", v.before(1)))
                    ins = nc.scalar.activation(qp[:, 8 * i:8 * i + 8, :], src, ACT.Identity,
                                               bias=biases[:, 3:4], scale=SCALE)
                else:
                    if v.has_before(1):
                        act.wait_ge(k_placed, upto("k_placed", v.before(1)))
                    ins = nc.scalar.activation(kp[:, 8 * (i - 2):8 * (i - 2) + 8, 0:N], src, ACT.Identity,
                                               bias=biases[:, 1:2])
                ins.then_inc(pre_drained, 1)

            def v_drain(v, i):
                act.wait_ge(pre_filled, upto("pre_filled", v, 6 + i))
                if v.has_before(2):
                    act.wait_ge(pv_done, upto("pv_done", v.before(2)))
                if v.number == 1:
                    act.wait_ge(zeroed_odd, 1)
                for g in range(2):
                    r = slice(PAD * g, PAD * g + N)
                    ins = nc.scalar.copy(
                        vb[v.par][r, 8 * i:8 * i + 8, :, :, D * g:D * g + D].rearrange("p q s h d -> p (q s h) d"),
                        ps_pre[r, :].rearrange("p (t d) -> p t d", d=D))
                ins.then_inc(pre_drained, 1)

            def ob_drain(v, i):
                act.wait_ge(pre_filled, upto("pre_filled", v, 8 + i))
                if i == 0:
                    if v.has_before(1):
                        act.wait_ge(pre_filled, upto("pre_filled", v.before(1)))
                for p in range(2):
                    ins = nc.scalar.copy(obs[:, :, :, i, p, :].rearrange("p i b s -> p b i s"),
                                         ps_pre[:, 256 * p:256 * p + 256].rearrange("p (b i s) -> p b i s", b=2, s=16))
                ins.then_inc(pre_drained, 1)

            def obt_drain(v, i):
                act.wait_ge(pre_filled, upto("pre_filled", v, 10 + i))
                if i == 0:
                    if v.has_before(2):
                        act.wait_ge(projected, upto("projected", v.before(2), 1))
                nc.scalar.copy(
                    obt[v.par][:, :, 4 * i:4 * i + 4, :].rearrange("p s i n -> p i s n"),
                    ps_pre[:, :].rearrange("p (i s n) -> p i s n", s=2, n=PAD)[:, :, :, 0:N]).then_inc(pre_drained, 1)

            def shift_drain(u, g):
                act.wait_ge(shift_turned, upto("shift_turned", u, g))
                if g >= 2:
                    act.wait_ge(scores_filled, upto("scores_filled", u, 4 * (g - 2) + 3))
                else:
                    if u.has_before(1):
                        act.wait_ge(scores_filled, upto("scores_filled", u.before(1), 4 * (g + 2) + 3))
                if u.number == 0 and g == 1:
                    act.wait_ge(zeroed_odd, 1)
                nc.scalar.copy(mr[g % 2][0:32, :], ps_small[0:32, 0:HN // 2].bitcast(BF16)).then_inc(shift_rows_ready, 1)

            def exponentials(u, q):
                act.wait_ge(scores_filled, upto("scores_filled", u, q))
                if q >= 2:
                    act.wait_ge(pv_done, upto("pv_done", u, q - 2))
                else:
                    if u.has_before(1):
                        act.wait_ge(pv_done, upto("pv_done", u.before(1), q + Q - 2))
                nc.scalar.activation(pt[q % 2][:, :, :, :].rearrange("p s h n -> p (s h n)"),
                                          ps_scores[:, 0:2 * HN], ACT.Exp).then_inc(probs_ready, 1)

            def pv_drain(u, g):
                act.wait_ge(pv_done, upto("pv_done", u, 4 * g + 3))
                if g >= 2:
                    act.wait_ge(o_normed, upto("o_normed", u, g - 2))
                else:
                    if u.has_before(1):
                        act.wait_ge(o_normed, upto("o_normed", u.before(1), g + 2))
                nc.scalar.copy(oe[g % 2][:, :, :, :].rearrange("p q s n -> p (q s n)"), ps_pv[:, 0:HALF]).then_inc(pv_drained, 1)

            def y_drain(w, b):
                act.wait_ge(projected, upto("projected", w, b))
                if b == 0:
                    if w.has_before(1):
                        act.wait_ge(rng_filled, upto("rng_filled", w.before(1)))
                nc.scalar.activation(
                    ym[:, :, SIDE * b:SIDE * b + SIDE].rearrange("p k (i j) -> p i k j", j=WS),
                    ps_acc[:, 0:HALF].rearrange("p (i k j) -> p i k j", k=WS, j=WS), ACT.Identity,
                    bias=biases[:, 2:3]).then_inc(acc_drained, 1)

            def x2t_drain(w, i):
                act.wait_ge(rng_filled, upto("rng_filled", w, 2 + i))
                if i == 0:
                    if w.has_before(1):
                        act.wait_ge(mixed, upto("mixed", w.before(1)))
                c0, c1 = (0, 4 * ROWS) if i == 0 else (4 * ROWS, COLS)
                nc.scalar.copy(x2t[:, c0:c1], ps_rng[:, 0:c1 - c0]).then_inc(rng_drained, 1)

            def top2_exp(w, _):
                act.wait_ge(top2_step, upto("top2_step", w, GAP_STEP))
                nc.scalar.activation(top[:, 3, :], top[:, 2, :], ACT.Exp).then_inc(gap_exp, 1)

            def wt_drain(w, _):
                act.wait_ge(rng_filled, upto("rng_filled", w, 5))
                nc.scalar.copy(wt[:, :], ps_rng[0:96, 0:COLS // 2].bitcast(BF16)).then_inc(rng_drained, 1)

            def mix_drain(w, half):
                act.wait_ge(mixed, upto("mixed", w, E * half + E - 1))
                if half == 0:
                    act.wait_ge(rng_filled, upto("rng_filled", w, 1))
                nc.scalar.copy(ym[:, :, :].rearrange("p k r -> p (k r)")[:, HALF * half:HALF * half + HALF],
                                    ps_acc[:, 0:HALF]).then_inc(acc_drained, 1)

            act.wait_ge(zeroed, 1)
            for dst, src in rel_list:
                act.dma_start(dst, src).then_inc(weights_loaded, 16)
            act.wait_ge(weights_ready, 1)
            for step, unit, i in program(act):
                if step == "norm1_center":
                    norm1_center(unit, i)
                elif step == "norm2_center":
                    norm2_center(unit, i)
                elif step == "xt":
                    xt_drain(unit, i)
                elif step == "qk":
                    qk_drain(unit, i)
                elif step == "v":
                    v_drain(unit, i)
                elif step == "ob":
                    ob_drain(unit, i)
                elif step == "obt":
                    obt_drain(unit, i)
                elif step == "shift":
                    shift_drain(unit, i)
                elif step == "scores":
                    exponentials(unit, i)
                elif step == "pv_drain":
                    pv_drain(unit, i)
                elif step == "y":
                    y_drain(unit, i)
                elif step == "x2t":
                    x2t_drain(unit, i)
                elif step == "top2_exp":
                    top2_exp(unit, i)
                elif step == "wt":
                    wt_drain(unit, i)
                elif step == "mix_drain":
                    mix_drain(unit, i)

        @block.vector
        def _(dve):
            def norm1_center(v, _):
                dve.wait_ge(x_loaded, upto("x_loaded", v))
                if v.has_before(1):
                    dve.wait_ge(centered1, upto("centered1", v.before(1)))
                nc.vector.tensor_reduce(st1[:, 0, :], xin[v.par].rearrange("p j k c -> p (j k) c"), AX, ALU.add).then_inc(sum1, 1)
                dve.wait_ge(sum1, upto("sum1", v))
                nc.vector.tensor_scalar(st1[:, 1, :], st1[:, 0, :], -1.0 / C, None, ALU.mult).then_inc(mean1, 1)

            def norm1_scale(v, _):
                dve.wait_ge(squared1, upto("squared1", v))
                if v.has_before(1):
                    dve.wait_ge(normed1, upto("normed1", v.before(1)))
                nc.vector.tensor_reduce(st1[:, 2, :], sq1[:, :, :, :].rearrange("p k j c -> p (k j) c"), AX, ALU.add).then_inc(sqsum1, 1)
                dve.wait_ge(sqsum1, upto("sqsum1", v))
                nc.vector.tensor_scalar(st1[:, 3, :], st1[:, 2, :], 1.0 / C, LN1_EPS, ALU.mult, ALU.add).then_inc(var1, 1)

            def norm2_center(w, _):
                dve.wait_ge(rng_drained, upto("rng_drained", w, 1))
                if w.has_before(1):
                    dve.wait_ge(centered2, upto("centered2", w.before(1)))
                nc.vector.tensor_reduce(st2[:, 0, :], x2[:, :, :, :].rearrange("p k j c -> p (k j) c"), AX, ALU.add).then_inc(sum2, 1)
                dve.wait_ge(sum2, upto("sum2", w))
                nc.vector.tensor_scalar(st2[:, 1, :], st2[:, 0, :], -1.0 / C, None, ALU.mult).then_inc(mean2, 1)

            def norm2_scale(w, _):
                dve.wait_ge(squared2, upto("squared2", w))
                if w.has_before(1):
                    dve.wait_ge(normed2, upto("normed2", w.before(1)))
                nc.vector.tensor_reduce(st2[:, 2, :], sq2[:, :, :, :].rearrange("p k j c -> p (k j) c"), AX, ALU.add).then_inc(sqsum2, 1)
                dve.wait_ge(sqsum2, upto("sqsum2", w))
                nc.vector.tensor_scalar(st2[:, 3, :], st2[:, 2, :], 1.0 / C, LN2_EPS, ALU.mult, ALU.add).then_inc(var2, 1)

            def maximum(u, q):
                dve.wait_ge(max_filled, upto("max_filled", u, q))
                nc.vector.tensor_reduce(
                    mx[(q // 4) % 2][:, :, q % 4, :],
                    ps_max[0:2 * N, 0:2 * A * N].rearrange("p (s a m) -> p s a m", s=2, a=A), AX, ALU.max).then_inc(max_taken, 1)

            def split(u, g):
                m = mx[g % 2].rearrange("p s q a -> p s (q a)")
                hi, lo = ms[g % 2][:, :, 0, :], ms[g % 2][:, :, 1, :]
                dve.wait_ge(max_taken, upto("max_taken", u, 4 * g + 3))
                if g >= 2:
                    dve.wait_ge(shift_turned, upto("shift_turned", u, g - 2))
                else:
                    if u.has_before(1):
                        dve.wait_ge(shift_turned, upto("shift_turned", u.before(1), g + 2))
                nc.vector.tensor_scalar(hi, m, -1.0, None, ALU.mult).then_inc(shift_rounded, 1)
                dve.wait_ge(shift_rounded, upto("shift_rounded", u, g))
                nc.vector.scalar_tensor_tensor(out=lo, in0=m, scalar=-1.0, in1=hi, op0=ALU.mult,
                                                    op1=ALU.subtract).then_inc(shift_split, 1)

            def normalise(u, g):
                dve.wait_ge(sums_spread, upto("sums_spread", u, g))
                if g >= 2:
                    dve.wait_ge(o_normed, upto("o_normed", u, g - 2))
                else:
                    if u.has_before(1):
                        dve.wait_ge(o_normed, upto("o_normed", u.before(1), g + 2))
                nc.vector.reciprocal(rz[g % 2][:, :, :, :].rearrange("p q s n -> p (q s n)"),
                                          ps_small[:, 0:HALF]).then_inc(sums_inverted, 1)

            def residual(w, i):
                dve.wait_ge(rng_filled, upto("rng_filled", w, i))
                k0, k1 = (0, 4) if i == 0 else (4, 7)
                if i == 0:
                    if w.has_before(1):
                        dve.wait_ge(centered2, upto("centered2", w.before(1)))
                nc.vector.tensor_tensor(
                    x2[:, k0:k1, :, :], ps_rng[0:ROWS, 0:(k1 - k0) * 128].rearrange("p (k j c) -> p k j c", j=A, c=C),
                    xin[w.par][:, :, k0:k1, :].rearrange("p j k c -> p k j c"), ALU.add).then_inc(rng_drained, 1)

            def router(w, _):
                dve.wait_ge(rng_filled, upto("rng_filled", w, 4))
                nc.vector.tensor_tensor(
                    logits[:, :, :], ps_rng[0:ROWS, 0:TOK * E].rearrange("p (t e) -> p t e", e=E),
                    rb[:, :].unsqueeze(1).to_broadcast([ROWS, TOK, E]), ALU.add).then_inc(rng_drained, 1)

            at = [0]

            def link(ins, w):
                ins.then_inc(top2_step, 1)
                dve.wait_ge(top2_step, upto("top2_step", w, at[0]))
                at[0] += 1

            def largest(w, vals, m, r, pick):
                tt, V = nc.vector.tensor_tensor, nc.vector
                link(V.tensor_reduce(top[:, m, :], vals, AX, ALU.max), w)
                link(tt(tmp[:, :, :], vals, over(top[:, m, :], E), ALU.is_equal), w)
                link(tt(tmp[:, :, :], tmp[:, :, :], rank[:, :].unsqueeze(1).to_broadcast([ROWS, TOK, E]), ALU.mult), w)
                link(V.tensor_reduce(top[:, r, :], tmp[:, :, :], AX, ALU.max), w)
                link(tt(pick, tmp[:, :, :], over(top[:, r, :], E), ALU.is_equal), w)

            def top2_pick(w, _):
                at[0] = 0
                dve.wait_ge(rng_drained, upto("rng_drained", w, 4))
                largest(w, logits[:, :, :], 0, 7, pick1[:, :, :])
                link(nc.vector.scalar_tensor_tensor(out=logits[:, :, :], in0=pick1[:, :, :], scalar=BELOW_ALL,
                                                    in1=logits[:, :, :], op0=ALU.mult, op1=ALU.add), w)
                largest(w, logits[:, :, :], 1, 6, pick2[:, :, :])
                if w.has_before(1):
                    dve.wait_ge(gap_exp, upto("gap_exp", w.before(1)))
                assert at[0] == GAP_STEP
                link(nc.vector.tensor_tensor(top[:, 2, :], top[:, 1, :], top[:, 0, :], ALU.subtract), w)

            def top2_weigh(w, _):
                tt, V = nc.vector.tensor_tensor, nc.vector
                dve.wait_ge(gap_exp, upto("gap_exp", w))
                link(V.tensor_scalar(top[:, 4, :], top[:, 3, :], 1.0, None, ALU.add), w)
                link(V.reciprocal(top[:, 5, :], top[:, 4, :]), w)
                link(tt(top[:, 4, :], top[:, 3, :], top[:, 5, :], ALU.mult), w)
                link(tt(pick1[:, :, :], pick1[:, :, :], over(top[:, 5, :], E), ALU.mult), w)
                link(tt(pick2[:, :, :], pick2[:, :, :], over(top[:, 4, :], E), ALU.mult), w)
                link(tt(mixw[:, :, :], pick1[:, :, :], pick2[:, :, :], ALU.add), w)
                parts = [w_parts[:, :, k, :] for k in range(3)]
                whole = mixw[:, :, :].rearrange("p (k j) e -> p k (j e)", j=A)
                rest = tmp[:, :, :].rearrange("p (k j) e -> p k (j e)", j=A)
                if w.has_before(1):
                    dve.wait_ge(rng_filled, upto("rng_filled", w.before(1)))
                link(V.tensor_copy(parts[0], whole), w)
                link(tt(rest, whole, parts[0], ALU.subtract), w)
                link(V.tensor_copy(parts[1], rest), w)
                link(tt(parts[2], rest, parts[1], ALU.subtract), w)
                assert at[0] == TOP2_STEPS, at[0]

            def mix(w, i):
                if i == 16:
                    return
                half, e = divmod(i, E)
                dve.wait_ge(rng_filled, upto("rng_filled", w, 6 + i))
                if i >= 2:
                    dve.wait_ge(mixed, upto("mixed", w, i - 2))
                else:
                    if w.has_before(1):
                        dve.wait_ge(mixed, upto("mixed", w.before(1)))
                nc.vector.tensor_tensor(zt[i % 2][:, :], ps_rng[:, 0:HALF],
                                             x2t[:, HALF * half:HALF * half + HALF], ALU.mult).then_inc(rng_drained, 1)

            def final(w, i):
                dve.wait_ge(rng_filled, upto("rng_filled", w, 22 + i))
                k0, k1 = (0, 4) if i == 0 else (4, 7)
                if i == 0:
                    if w.has_before(1):
                        dve.wait_ge(out_stored, upto("out_stored", w.before(1)))
                nc.vector.tensor_tensor(
                    yo[:, :, k0:k1, :].rearrange("p j k c -> p k j c"),
                    ps_rng[0:ROWS, 0:(k1 - k0) * 128].rearrange("p (k j c) -> p k j c", j=A, c=C),
                    x2[:, k0:k1, :, :], ALU.add).then_inc(rng_drained, 1)

            V = nc.vector
            for t in (wq, wk, eb_raw):
                V.memset(t[:, :], 0.0)
            for t in (wr, rel_raw, bv, kp):
                V.memset(t[:, :, :], 0.0)
            for t in (we, bt):
                V.memset(t[:, :, :, :], 0.0)
            for t in vb:
                V.memset(t[:, :, :, :, :], 0.0)
            V.memset(w_proj_o[:, :, :], 0.0)
            V.memset(wv[:, :, :, :], 0.0)
            V.memset(w_proj_b[:, :, :, :, :], 0.0)
            V.memset(mr[0][:, :], 0.0)
            V.memset(qbd[0][:, :, :, :], 0.0)
            V.memset(kz[0][:, :, :, :], 0.0).then_inc(zeroed, 1)
            dve.wait_ge(zeroed, 1)
            for t in vb:
                for g in range(2):
                    V.memset(t[PAD * g:PAD * g + N, :, :, :, 16 + D * g:16 + D * g + D].rearrange(
                        "p q s h t -> p (q s h) t"), 1.0)

            dve.wait_ge(weights_loaded, all_loaded)
            count = [0]

            def chain(ins):
                ins.then_inc(weight_step, 1)
                count[0] += 1
                dve.wait_ge(weight_step, count[0])

            chain(V.tensor_scalar(biases[:, 3:4], biases[:, 0:1], SCALE, None, ALU.mult))
            for h in range(HEADS):
                for kind in range(4):
                    ins = V.tensor_tensor(bt[:, h, kind, 0:N], rel_raw[:, :, h], mask[:, kind, 0:N], ALU.add)
            chain(ins)
            chain(V.tensor_copy(eb[:, 0, :], eb_raw[:, :]))
            chain(V.tensor_tensor(eb_rest[:, :], eb_raw[:, :], eb[:, 0, :], ALU.subtract))
            chain(V.tensor_copy(eb[:, 1, :], eb_rest[:, :]))
            chain(V.tensor_tensor(eb[:, 2, :], eb_rest[:, :], eb[:, 1, :], ALU.subtract))
            chain(V.tensor_copy(bv_parts[:, 0, :], bv_raw[:, :]))
            chain(V.tensor_tensor(bv_rest[:, :], bv_raw[:, :], bv_parts[:, 0, :], ALU.subtract))
            chain(V.tensor_copy(bv_parts[:, 1, :], bv_rest[:, :]))
            chain(V.tensor_tensor(bv_parts[:, 2, :], bv_rest[:, :], bv_parts[:, 1, :], ALU.subtract))
            chain(V.tensor_scalar(bv_rows[:, 0, :], bv_parts[:, 0, :], ident[0:3, 0:1], None, ALU.mult))
            chain(V.scalar_tensor_tensor(out=bv_rows[:, 1, :], in0=bv_parts[:, 1, :], scalar=ident[0:3, 1:2],
                                        in1=bv_rows[:, 0, :], op0=ALU.mult, op1=ALU.add))
            chain(V.scalar_tensor_tensor(out=bv_rows[:, 0, :], in0=bv_parts[:, 2, :], scalar=ident[0:3, 2:3],
                                        in1=bv_rows[:, 1, :], op0=ALU.mult, op1=ALU.add))
            V.tensor_copy(bv[0:3, :, :], bv_rows[:, 0, :].unsqueeze(1).to_broadcast([3, Q, C])).then_inc(weights_ready, 1)

            for step, unit, i in program(dve):
                if step == "norm1_center":
                    norm1_center(unit, i)
                elif step == "norm1_scale":
                    norm1_scale(unit, i)
                elif step == "norm2_center":
                    norm2_center(unit, i)
                elif step == "norm2_scale":
                    norm2_scale(unit, i)
                elif step == "maximum":
                    maximum(unit, i)
                elif step == "split":
                    split(unit, i)
                elif step == "normalise":
                    normalise(unit, i)
                elif step == "back":
                    residual(unit, i)
                elif step == "router":
                    router(unit, i)
                elif step == "top2_pick":
                    top2_pick(unit, i)
                elif step == "top2_weigh":
                    top2_weigh(unit, i)
                elif step == "mix":
                    mix(unit, i)
                elif step == "final":
                    final(unit, i)

        @block.tensor
        def _(pe):
            mm = nc.tensor.matmul

            def xt_turn(v, i):
                if i or v.has_before(1):
                    pe.wait_ge(pre_drained, upto("pre_drained", v, i - 1))
                pe.wait_ge(normed1, upto("normed1", v))
                for k in range(*((0, 4) if i == 0 else (4, 7))):
                    ins = nc.tensor.transpose(ps_pre[:, (k % 4) * ROWS:(k % 4) * ROWS + ROWS],
                                              xc1[:, k, :, :].rearrange("p j c -> p (j c)"), ident[0:ROWS, 0:ROWS])
                ins.then_inc(pre_filled, 1)

            def qk(v, i):
                pe.wait_ge(pre_drained, upto("pre_drained", v, 1 + i))
                b = i % 2
                mm(ps_pre[:, 0:HALF], (wq if i < 2 else wk)[:, :],
                        xt[:, 8 * b:8 * b + 8, :, :].rearrange("p q k i -> p (q k i)"), start=True, stop=True).then_inc(pre_filled, 1)

            def v_products(v, i):
                pe.wait_ge(pre_drained, upto("pre_drained", v, 5 + i))
                mm(ps_pre[:, :], first3[:, :], bv[:, :, :].rearrange("p q c -> p (q c)"), start=True, stop=False,
                   skip_group_check=True)
                for q in range(8):
                    keys = xt[:, 8 * i + q, :, :].rearrange("p k i -> p (k i)")
                    for g in range(2):
                        ins = mm(ps_pre[PAD * g:PAD * g + N, 64 * q:64 * q + 64], keys,
                                 wv[:, g, :, :].rearrange("p s c -> p (s c)"), start=False,
                                 stop=(q == 7), skip_group_check=True)
                ins.then_inc(pre_filled, 1)

            def ob(v, i):
                pe.wait_ge(pre_drained, upto("pre_drained", v, 7 + i))
                for hh in range(2):
                    h = 2 * hh + i
                    for p in range(2):
                        for last_row in range(2):
                            kind = last_row + 2 * (v.par and p)
                            w0, w1 = (WS, WS + 1) if last_row else (0, WS)
                            dst = ps_pre[PAD * hh:PAD * hh + PAD, 256 * p:256 * p + 256].rearrange(
                                "p (b i s) -> p b i s", b=2, s=16)[:, :, w0:w1, :]
                            src = vb[v.par][:, :, p, h, 0:16].rearrange("p (b i) s -> p b i s", b=2)[:, :, w0:w1, :]
                            ins = mm(dst, bt[:, h, kind, :], src, start=True, stop=True)
                ins.then_inc(pre_filled, 1)

            def ob_turn(v, i):
                pe.wait_ge(pre_drained, upto("pre_drained", v, 9 + i))
                for k in range(4):
                    ins = nc.tensor.transpose(ps_pre[:, 128 * k:128 * k + 128],
                                              obs[:, 4 * i + k, :, :, :, :].rearrange("p b h s t -> p (b h s t)"),
                                              ident[:, :])
                ins.then_inc(pre_filled, 1)

            def max_scores(u, q):
                if q or u.has_before(1):
                    pe.wait_ge(max_taken, upto("max_taken", u, q - 1))
                if q == 0:
                    pe.wait_ge(q_placed, upto("q_placed", u))
                    pe.wait_ge(k_placed, upto("k_placed", u))
                for s in range(2):
                    ins = mm(ps_max[0:2 * N, A * N * s:A * N * s + A * N],
                             qbd[u.par][:, q, 2 * s:2 * s + 2, :].rearrange("p h n -> p (h n)"),
                             kz[u.par][:, q, :, 0:N], start=True, stop=True)
                ins.then_inc(max_filled, 1)

            def shift_turn(u, g):
                pe.wait_ge(shift_split, upto("shift_split", u, g))
                if g >= 2:
                    pe.wait_ge(sums_inverted, upto("sums_inverted", u, g - 2))
                else:
                    if u.has_before(1):
                        pe.wait_ge(sums_inverted, upto("sums_inverted", u.before(1), g + 2))
                if g or u.has_before(1):
                    pe.wait_ge(shift_rows_ready, upto("shift_rows_ready", u, g - 1))
                for s in range(2):
                    ins = nc.tensor.transpose(
                        ps_small[0:32, :].bitcast(BF16)[:, 2 * N * s:2 * N * s + 2 * N],
                        ms[g % 2][:, s, :, :].rearrange("p k r -> p (k r)"), identb[0:2 * N, 0:2 * N])
                ins.then_inc(shift_turned, 1)

            def scores(u, q):
                if q or u.has_before(1):
                    pe.wait_ge(probs_ready, upto("probs_ready", u, q - 1))
                if q % 4 == 0:
                    pe.wait_ge(shift_rows_ready, upto("shift_rows_ready", u, q // 4))
                for p in range(2):
                    dst = ps_scores[:, HN * p:HN * p + HN]
                    mm(dst, shift_sel[:, q % 4, p, :], mr[(q // 4) % 2][:, :], start=True, stop=False)
                    ins = mm(dst, kz[u.par][:, q, 2 * p:2 * p + 2, :].rearrange("p a m -> p (a m)"),
                             qbd[u.par][:, q, :, :].rearrange("p h n -> p (h n)"), start=False, stop=True)
                ins.then_inc(scores_filled, 1)

            def pv(u, q):
                pe.wait_ge(probs_ready, upto("probs_ready", u, q))
                if q % 4 == 0:
                    if q // 4 or u.has_before(1):
                        pe.wait_ge(pv_drained, upto("pv_drained", u, q // 4 - 1))
                for p in range(2):
                    c0 = (2 * (q % 4) + p) * N
                    for h in range(HEADS):
                        ins = mm(ps_pv[SLOT * h:SLOT * h + SLOT, c0:c0 + N], vb[u.par][:, q, p, h, :],
                                 pt[q % 2][:, p, h, :], start=True, stop=True)
                ins.then_inc(pv_done, 1)

            def normalise(u, g):
                pe.wait_ge(pv_drained, upto("pv_drained", u, g))
                if g < GROUPS - 1:
                    pe.wait_ge(shift_rows_ready, upto("shift_rows_ready", u, g + 1))
                elif u.number != UNITS - 1:
                    pe.wait_ge(shift_rows_ready, upto("shift_rows_ready", Unit(u.n + 1, None, None), 0))
                if g or u.has_before(1):
                    pe.wait_ge(sums_inverted, upto("sums_inverted", u, g - 1))
                mm(ps_small[:, 0:HALF], z_sel[:, :], oe[g % 2][:, :, :, :].rearrange("p q s n -> p (q s n)"),
                        start=True, stop=True).then_inc(sums_spread, 1)

            def y(w, b):
                if b or w.has_before(1):
                    pe.wait_ge(acc_drained, upto("acc_drained", w, b - 1))
                if b == 0:
                    pe.wait_ge(o_normed, upto("o_normed", w))
                for hh in range(2):
                    mm(ps_acc[:, 0:HALF], w_proj_b[:, b, hh, :, :].rearrange("p a c -> p (a c)"),
                       obt[w.par][:, hh, :, :].rearrange("p i n -> p (i n)"), start=(hh == 0), stop=False,
                       skip_group_check=True)
                for p in range(2):
                    ins = mm(ps_acc[64 * p:64 * p + 64, 0:HALF], w_proj_o[:, :, :].rearrange("p g c -> p (g c)"),
                             on[:, p, 8 * b:8 * b + 8, :].rearrange("p q n -> p (q n)"), start=False, stop=True,
                             skip_group_check=True)
                ins.then_inc(projected, 1)

            def turn_back(w, fill, i):
                if fill or w.has_before(1):
                    pe.wait_ge(rng_drained, upto("rng_drained", w, fill - 1))
                for k in range(*((0, 4) if i == 0 else (4, 7))):
                    ins = nc.tensor.transpose(ps_rng[0:ROWS, (k % 4) * 128:(k % 4) * 128 + 128], ym[:, k, :],
                                              ident[:, :])
                ins.then_inc(rng_filled, 1)

            def back(w, i):
                pe.wait_ge(acc_drained, upto("acc_drained", w, 1))
                turn_back(w, i, i)

            def x2t_turn(w, i):
                pe.wait_ge(rng_drained, upto("rng_drained", w, 1 + i))
                pe.wait_ge(normed2, upto("normed2", w))
                for k in range(*((0, 4) if i == 0 else (4, 7))):
                    ins = nc.tensor.transpose(ps_rng[:, (k % 4) * ROWS:(k % 4) * ROWS + ROWS],
                                              xc2[:, k, :, :].rearrange("p j c -> p (j c)"), ident[0:ROWS, 0:ROWS])
                ins.then_inc(rng_filled, 1)

            def router(w, _):
                pe.wait_ge(rng_drained, upto("rng_drained", w, 3))
                for k in range(WS):
                    ins = mm(ps_rng[0:ROWS, 32 * k:32 * k + 32], x2t[:, ROWS * k:ROWS * k + ROWS],
                             wr[:, :, :].rearrange("p a e -> p (a e)"), start=True, stop=True)
                ins.then_inc(rng_filled, 1)

            def wt_turn(w, _):
                pe.wait_ge(rng_drained, upto("rng_drained", w, 4))
                pe.wait_ge(top2_step, upto("top2_step", w))
                for k in range(WS):
                    ins = nc.tensor.transpose(ps_rng[0:96, :].bitcast(BF16)[:, ROWS * k:ROWS * k + ROWS],
                                              w_parts[:, k, :, :].rearrange("p t e -> p (t e)"),
                                              identb[0:ROWS, 0:ROWS])
                ins.then_inc(rng_filled, 1)

            def mix(w, i):
                if i < 16:
                    half, e = divmod(i, E)
                    pe.wait_ge(rng_drained, upto("rng_drained", w, 5 + i))
                    mm(ps_rng[:, 0:HALF], weight_sel[:, e, :], wt[:, HALF * half:HALF * half + HALF],
                            start=True, stop=True).then_inc(rng_filled, 1)
                if i == 0:
                    return
                half, e = divmod(i - 1, E)
                if e == 0:
                    pe.wait_ge(acc_drained, upto("acc_drained", w, 1 + half))
                    for k in range(3):
                        mm(ps_acc[:, 0:HALF], eb[:, k, :], wt[:, HALF * half:HALF * half + HALF],
                           start=(k == 0), stop=False)
                pe.wait_ge(rng_drained, upto("rng_drained", w, 6 + i - 1))
                ins = mm(ps_acc[:, 0:HALF], we[:, e, :, :].rearrange("p a c -> p (a c)"), zt[(i - 1) % 2][:, :],
                         start=False, stop=(e == E - 1))
                ins.then_inc(mixed, 1)

            def final(w, i):
                pe.wait_ge(acc_drained, upto("acc_drained", w, 3))
                turn_back(w, 22 + i, i)

            pe.wait_ge(weights_ready, 1)
            for step, unit, i in program(pe):
                if step == "xt":
                    xt_turn(unit, i)
                elif step == "qk":
                    qk(unit, i)
                elif step == "v":
                    v_products(unit, i)
                elif step == "ob":
                    ob(unit, i)
                elif step == "obt":
                    ob_turn(unit, i)
                elif step == "maximum":
                    max_scores(unit, i)
                elif step == "shift":
                    shift_turn(unit, i)
                elif step == "scores":
                    scores(unit, i)
                elif step == "pv":
                    pv(unit, i)
                elif step == "normalise":
                    normalise(unit, i)
                elif step == "y":
                    y(unit, i)
                elif step == "back":
                    back(unit, i)
                elif step == "x2t":
                    x2t_turn(unit, i)
                elif step == "router":
                    router(unit, i)
                elif step == "wt":
                    wt_turn(unit, i)
                elif step == "mix":
                    mix(unit, i)
                elif step == "final":
                    final(unit, i)


_INS = ["x", "L0_conv_w_qkv", "L0_conv_b_qkv", "L0_conv_w_proj", "L0_conv_b_proj", "L0_conv_rel_table",
        "L0_ffn_router_w", "L0_ffn_router_b", "L0_ffn_expert_w", "L0_ffn_expert_b"]


def kernel(**inputs):
    import ml_dtypes
    import concourse.bacc as bacc
    from concourse.bass_utils import run_bass_kernel_spmd

    nc = bacc.Bacc("TRN2", target_bir_lowering=False, num_devices=1)
    arrays, args = {}, []
    for name in _INS:
        arrays[name] = np.ascontiguousarray(inputs[name])
    for name, (a, short) in shape_constants().items():
        arrays[name] = a.astype(ml_dtypes.bfloat16) if short else a
    for name, a in arrays.items():
        args.append(nc.dram_tensor(name, a.shape, mybir.dt.from_np(a.dtype), kind="ExternalInput").ap())
    args.append(nc.dram_tensor("out", (IMAGES, SIDE, SIDE, C), F32, kind="ExternalOutput").ap())
    metaformer_block(nc, *args)
    return run_bass_kernel_spmd(nc, [arrays], core_ids=[0]).results[0]["out"]
```

```python
from contextlib import ExitStack

import numpy as np

import concourse.bass as bass
from concourse import mybir

F32 = mybir.dt.float32
F32R = mybir.dt.float32r
BF16 = mybir.dt.bfloat16
ALU = mybir.AluOpType
ACT = mybir.ActivationFunctionType
AX = mybir.AxisListType.X

IMAGES, SIDE, C = 16, 56, 32
WS, SHIFT, HEADS = 7, 3, 4
D = C // HEADS
SCALE = float(D) ** -0.5
N = WS * WS
E = 8
UNITS = 16
ROWS = 2 * SIDE
A = 4
Q = 16
TOK = A * WS
COLS = Q * N
HALF = COLS // 2
EVEN = N + 1
PAD = 64
SLOT = 32
HN = HEADS * N
GROUPS = 4
LN1_EPS, LN2_EPS = 1e-6, 1e-5
BELOW_ALL = -3.0e38
ROW_CUTS = ((0, 48), (48, 53), (53, 56))
COL_CUTS = ((0, 25), (25, 28))
TRANSFERS = 2 * len(ROW_CUTS) * len(COL_CUTS)

PRE_FILLS = 12
TOKEN_FILLS = 5
WEIGHT_FILLS = 19
AHEAD = 6
MIX_PRODUCTS = (5, 9, 13, 16)
SHIFT_STEP = 2
TOP2_STEPS = 22
GAP_STEP = 9

NORM1 = ("load", "norm1_center", "norm1_square", "norm1_scale")
PRE_ORDER = ("keep", "xt", "xt", "prepare", "qk", "qk", "qk", "qk", "place", "v", "v", "ob", "ob", "obt", "obt")
LATE = ("replicate", "wt", "mix", "mix_drain", "final", "store")
SIDE_TASKS = {
    (0, 1): [("xt", 0)], (1, 0): [("replicate", 0)], (1, 1): [("xt", 1), ("wt", 0)], (1, 2): [("y", 0)],
    (2, 0): [("y", 1), ("qk", 0), ("back", 0), ("qk", 1), ("back", 1)], (2, 1): [("keep", 0), ("norm2_center", 0)],
    (2, 2): [("mix", 0)], (3, 1): [("qk", 2)], (3, 2): [("mix", 1)],
    (4, 0): [("norm2_square", 0), ("load", 0), ("mix", 2)], (4, 1): [("qk", 3), ("norm2_scale", 0), ("mix", 3)],
    (5, 0): [("mix", 4)], (5, 1): [("place", 0), ("v", 0)], (6, 0): [("mix", 5)], (6, 2): [("mix", 6)],
    (7, 0): [("x2t", 0)], (7, 1): [("mix", 7)], (7, 2): [("x2t", 1)], (8, 0): [("mix", 8), ("router", 0)],
    (8, 1): [("mix", 9), ("mix_drain", 0), ("top2", 0), ("mix", 10)], (8, 2): [("mix", 11)],
    (9, 1): [("mix", 12), ("top2", 1), ("v", 1)], (10, 0): [("mix", 13), ("top2", 2), ("norm1_center", 0)],
    (10, 1): [("mix", 14)], (11, 0): [("top2_exp", 0), ("top2", 3), ("ob", 0), ("mix", 15)],
    (11, 1): [("top2", 4), ("norm1_square", 0)], (11, 2): [("top2", 5)], (12, 0): [("ob", 1), ("norm1_scale", 0)],
    (12, 1): [("mix", 16)], (12, 2): [("mix_drain", 1)], (13, 0): [("final", 0)], (13, 1): [("obt", 0)],
    (14, 1): [("final", 1), ("store", 0), ("obt", 1)], (14, 2): [("top2", 6)], (15, 2): [("top2", 7)],
}


class Unit:

    def __init__(self, n, slab, par, number=None):
        self.n, self.slab, self.par = n, slab, par
        self.number = number

    def has_before(self, back):
        return self.number is None or self.number >= back

    def has_after(self):
        return self.number is None or self.number < UNITS - 1

    def after(self):
        return Unit(self.n + 1, None, None)

    def before(self, back):
        return Unit(self.n - back, None, None)


def fixed(n):
    return Unit(n, n // 2, n % 2, n)


def in_loop(it, offset):
    return Unit(it * 2 + offset, it + offset // 2, offset % 2)


def macro_step(older, post, att, ahead, next_unit):
    def side(place):
        for name, i in SIDE_TASKS.get(place, ()):
            unit = (next_unit if name in NORM1 else ahead if name in PRE_ORDER else
                    older if name in LATE else post)
            if unit is not None:
                yield name, unit, i

    for s in range(Q):
        yield "scores", att, s
        yield from side((s, 0))
        unit, q = (att, s + AHEAD) if s + AHEAD < Q else (ahead, s + AHEAD - Q)
        if unit is not None:
            yield "maximum", unit, q
            if q % 4 == 3:
                yield "split", unit, q // 4
        if s % 4 == 1:
            unit = att if s > 1 else post
            if unit is not None:
                yield "invert", unit, 2 * ((s // 4 - 1) % GROUPS) + 1
        yield from side((s, 1))
        yield "pv", att, s
        if s % 4 == 0:
            unit = att if s else post
            if unit is not None:
                yield "normalise", unit, (s // 4 - 1) % GROUPS
                yield "invert", unit, 2 * ((s // 4 - 1) % GROUPS)
        yield from side((s, 2))
        if s % 4 == 3:
            yield "pv_drain", att, s // 4
        if s % 4 == SHIFT_STEP:
            g = (s // 4 + 1) % GROUPS
            if g or ahead is not None:
                yield "shift", att if g else ahead, g


def program(eng):
    unit = [fixed(n) for n in range(UNITS)] + [None, None]
    for name in NORM1:
        yield name, unit[0], 0
    for k, name in enumerate(PRE_ORDER):
        yield name, unit[0], PRE_ORDER[:k].count(name)
        if name == "keep":
            yield "load", unit[1], 0
    for name in NORM1[1:]:
        yield name, unit[1], 0
    for q in range(AHEAD):
        yield "maximum", unit[0], q
        if q == 3:
            yield "split", unit[0], 0
    yield "shift", unit[0], 0
    yield from macro_step(None, None, *unit[0:3])
    yield from macro_step(None, *unit[0:4])
    yield from macro_step(*unit[0:5])
    yield from macro_step(*unit[1:6])
    with eng.Fori(0, (UNITS - 6) // 2) as it:
        near = [in_loop(it, 2 + k) for k in range(6)]
        yield from macro_step(*near[0:5])
        yield from macro_step(*near[1:6])
    yield from macro_step(*unit[UNITS - 4:UNITS + 1])
    yield from macro_step(*unit[UNITS - 3:UNITS + 2])
    tasks = [task for place in sorted(SIDE_TASKS) for task in SIDE_TASKS[place]]
    yield "normalise", unit[UNITS - 1], GROUPS - 1
    yield "invert", unit[UNITS - 1], 2 * GROUPS - 2
    yield "invert", unit[UNITS - 1], 2 * GROUPS - 1
    for name, i in tasks:
        if name not in NORM1 + PRE_ORDER:
            yield name, unit[UNITS - 2] if name in LATE else unit[UNITS - 1], i
    for name, i in tasks:
        if name in LATE:
            yield name, unit[UNITS - 1], i


def shape_constants():
    jj, ii = np.arange(N) // WS, np.arange(N) % WS
    late = lambda t: (t >= WS - SHIFT).astype(int)
    mask = np.zeros((128, 4, PAD), np.float32)
    for kind in range(4):
        for g in range(2):
            region = late(ii) * (kind & 1) + 2 * late(jj) * ((kind >> 1) & g)
            mask[PAD * g:PAD * g + N, kind, :N] = np.where(region[:, None] != region[None, :], -100.0, 0.0)
    shift_sel = np.zeros((128, 4, 2, 2, PAD), np.float32)
    for part in range(2):
        for q in range(4):
            for a in range(A):
                shift_sel[16 * part + 4 * q + a, q, a // 2, a % 2, :N] = 1.0
    z_sel = np.zeros((128, 128), np.float32)
    for h in range(HEADS):
        for s in range(16):
            z_sel[SLOT * h + 16 + s, SLOT * h + s] = 1.0
            z_sel[SLOT * h + 16 + s, SLOT * h + 16 + s] = 1.0
    weight_sel = np.zeros((96, 2, A, 4, C), np.float32)
    for part in range(3):
        for a in range(A):
            for e in range(E):
                weight_sel[32 * part + 8 * a + e, e // 4, a, e % 4, :] = 1.0
    first3 = np.zeros((128, 128), np.float32)
    first3[:3] = 1.0
    rank = np.tile(np.arange(E, 0, -1, dtype=np.float32), (128, 1))
    return {
        "ident": np.eye(128, dtype=np.float32), "z_sel": z_sel, "mask": mask, "rank": rank,
        "identb": np.eye(128, dtype=np.float32), "first3": first3, "shift_sel": shift_sel,
        "weight_sel": weight_sel,
    }


CONST_COLS = {"ident": 128, "z_sel": 128, "mask": 4 * PAD, "rank": E}
CONST_BF16_COLS = {"identb": 128, "first3": 128, "shift_sel": 4 * 2 * 128, "weight_sel": E * 128}
WEIGHT_COLS = {"wq": 128, "wk": 128, "biases": 4, "wv": 4 * C, "w_proj_o": 2 * C, "w_proj_b": 4 * 128,
               "wr": A * E, "rb": E, "bv_raw": C, "eb_raw": 128, "we": 2 * C}


def side_by_side(parts, cols):
    whole = np.zeros((128, sum(cols.values())), np.float32)
    c0 = 0
    for name, n in cols.items():
        flat = parts[name].reshape(parts[name].shape[0], n)
        whole[:flat.shape[0], c0:c0 + n] = flat
        c0 += n
    return whole


def laid_out_weights(w_qkv, b_qkv, w_proj, b_proj, router_w, router_b, expert_w, expert_b):
    zeros = lambda *shape: np.zeros(shape, np.float32)
    wq, wk = zeros(A, C, A, C), zeros(A, C, A, C)
    wv = zeros(A, C, 2, 2, C)
    w_proj_o = zeros(HEADS, 4, D, 2, C)
    w_proj_b = zeros(2, 2, A, D, 2, 2, A, C)
    wr = zeros(A, C, A, E)
    we = expert_w.reshape(2, 4, C, C).transpose(1, 2, 0, 3)
    biases = zeros(A, C, 4)
    eb_raw = zeros(3, A, E, A, C)
    for a in range(A):
        wq[a, :, a, :] = w_qkv[:, 0:C]
        wk[a, :, a, :] = w_qkv[:, C:2 * C]
        wv[a, :, a % 2, a // 2, :] = w_qkv[:, 2 * C:3 * C]
        wr[a, :, a, :] = router_w
        eb_raw[:, a, :, a, :] = expert_b
        biases[a, :, 0], biases[a, :, 1], biases[a, :, 2] = b_qkv[0:C], b_qkv[C:2 * C], b_proj
        for b in range(2):
            for h in range(HEADS):
                w_proj_b[b, h % 2, a, :, b, h // 2, a, :] = w_proj[D * h:D * h + D]
    for g in range(2):
        for h in range(HEADS):
            w_proj_o[h, g, :, g, :] = w_proj[D * h:D * h + D]
    rows = lambda t, n: np.ascontiguousarray(t).reshape(n, -1)
    return side_by_side({
        "wq": rows(wq, 128), "wk": rows(wk, 128), "biases": rows(biases, 128), "wv": rows(wv, 128),
        "w_proj_o": rows(w_proj_o, 128), "w_proj_b": rows(w_proj_b, 128), "wr": rows(wr, 128),
        "rb": np.broadcast_to(router_b, (128, E)), "bv_raw": np.broadcast_to(b_qkv[2 * C:], (3, C)),
        "eb_raw": rows(eb_raw, 96), "we": rows(we, 128),
    }, WEIGHT_COLS)


def metaformer_block(nc, x, weights, rel_table, consts, consts_bf16, out):
    with ExitStack() as ctx:
        def sb(name, shape, dt=F32):
            return ctx.enter_context(nc.sbuf_tensor(name, shape, dt))

        def bank(name):
            return ctx.enter_context(nc.psum_tensor(name, [128, 512], F32))

        weight_tile = sb("weight_tile", [128, sum(WEIGHT_COLS.values())])
        const_tile = sb("const_tile", [128, sum(CONST_COLS.values())])
        const_bf16_tile = sb("const_bf16_tile", [128, sum(CONST_BF16_COLS.values())], BF16)
        part = {}
        for tile, cols in ((weight_tile, WEIGHT_COLS), (const_tile, CONST_COLS), (const_bf16_tile, CONST_BF16_COLS)):
            c0 = 0
            for name, n in cols.items():
                part[name] = tile[:, c0:c0 + n]
                c0 += n
        ident, z_sel, identb, first3 = part["ident"], part["z_sel"], part["identb"], part["first3"]
        mask = part["mask"].rearrange("p (k n) -> p k n", k=4)
        rank = part["rank"][0:ROWS, :]
        shift_sel = part["shift_sel"].rearrange("p (q s m) -> p q s m", q=4, s=2)
        weight_sel = part["weight_sel"][0:96, :].rearrange("p (s a m) -> p s a m", s=2, a=A)
        wq, wk = part["wq"], part["wk"]
        wv = part["wv"].rearrange("p (g s c) -> p g s c", g=2, s=2)
        w_proj_o = part["w_proj_o"].rearrange("p (g c) -> p g c", g=2)
        w_proj_b = part["w_proj_b"].rearrange("p (b s a c) -> p b s a c", b=2, s=2, a=A)
        wr = part["wr"].rearrange("p (a e) -> p a e", a=A)
        we = part["we"].rearrange("p (s c) -> p s c", s=2)
        biases = part["biases"]
        rb = part["rb"][0:ROWS, :]
        eb_raw, bv_raw = part["eb_raw"][0:96, :], part["bv_raw"][0:3, :]
        rel_raw = sb("rel_raw", [128, WS, WS, HEADS])
        bt = sb("bt", [128, HEADS, 4, PAD])
        eb_rest = sb("eb_rest", [96, 128])
        eb = sb("eb", [96, 3, 128], BF16)
        bv_rest = sb("bv_rest", [3, C])
        bv_parts = sb("bv_parts", [3, 3, C], BF16)
        bv_rows = sb("bv_rows", [3, 2, C])
        bv = sb("bv", [128, Q, C], BF16)
        minus_half = sb("minus_half", [ROWS, TOK])

        xin = sb("xin", [ROWS, A, WS, C])
        x_kept = [sb(f"x_kept{i}", [ROWS, A, WS, C]) for i in range(2)]
        xc1 = sb("xc1", [ROWS, WS, A, C])
        sq = sb("sq", [ROWS, WS, A, C])
        st1 = sb("st1", [ROWS, 5, TOK])
        xt = sb("xt", [128, Q, WS, WS])
        qp, kp = sb("qp", [128, Q, N]), sb("kp", [128, Q, PAD])
        qbd = [sb(f"qbd{i}", [128, Q, HEADS, N]) for i in range(2)]
        kz = [sb(f"kz{i}", [128, Q, A, PAD]) for i in range(2)]
        vb = [sb(f"vb{i}", [128, Q, 2, HEADS, SLOT]) for i in range(2)]
        obs = sb("obs", [128, 8, 2, 2, 2, 16])
        obt = [sb(f"obt{i}", [128, 2, 8, N]) for i in range(2)]
        mx = [sb(f"mx{i}", [2 * N, 2, 4, A]) for i in range(2)]
        ms = [sb(f"ms{i}", [2 * N, 2, 2, 16], BF16) for i in range(2)]
        mr = [sb(f"mr{i}", [128, HN], BF16) for i in range(2)]
        pt = [sb(f"pt{i}", [128, 2, HEADS, N]) for i in range(2)]
        oe = [sb(f"oe{i}", [128, 4, 2, N]) for i in range(2)]
        rz = [sb(f"rz{i}", [128, 4, 2, N]) for i in range(2)]
        on = sb("on", [128, 2, Q, N])
        ym = sb("ym", [128, WS, ROWS])
        x2 = [sb(f"x2_{i}", [ROWS, A, WS, C]) for i in range(2)]
        xc2 = sb("xc2", [ROWS, WS, A, C])
        st2 = sb("st2", [ROWS, 5, TOK])
        x2t = sb("x2t", [128, COLS])
        logits, pick1, pick2 = (sb(n, [ROWS, TOK, E]) for n in ("logits", "pick1", "pick2"))
        tmp, mixw = sb("tmp", [ROWS, TOK, E]), sb("mixw", [ROWS, TOK, E])
        top = sb("top", [ROWS, 8, TOK])
        w_parts = sb("w_parts", [ROWS, WS, 3, A * E], BF16)
        wt = sb("wt", [96, COLS], BF16)
        x4 = sb("x4", [128, A, COLS])
        zt = sb("zt", [128, A, HALF])

        ps_max, ps_scores, ps_pv, ps_small = bank("ps_max"), bank("ps_scores"), bank("ps_pv"), bank("ps_small")
        ps_pre, ps_acc = bank("ps_pre"), bank("ps_acc")
        ps_token, ps_weight = bank("ps_token"), bank("ps_weight")

        per_unit = {
            "x_loaded": 16 * TRANSFERS, "x_kept_ready": 16, "out_stored": 16 * TRANSFERS,
            "sum1": 1, "mean1": 1, "centered1": 1, "squared1": 1, "sqsum1": 1, "var1": 1,
            "rstd1": 1, "normed1": 1,
            "sum2": 1, "mean2": 1, "centered2": 1, "squared2": 1, "sqsum2": 1, "var2": 1,
            "rstd2": 1, "normed2": 1,
            "pre_filled": PRE_FILLS, "pre_drained": PRE_FILLS,
            "q_placed": 16 * A * HEADS, "k_placed": 16 * A,
            "max_filled": Q, "max_taken": Q, "shift_rounded": GROUPS, "shift_split": GROUPS,
            "shift_turned": GROUPS, "shift_rows_ready": GROUPS,
            "scores_filled": Q, "probs_ready": Q, "pv_done": Q, "pv_drained": GROUPS,
            "sums_spread": GROUPS, "sums_inverted": 2 * GROUPS, "o_normed": 2 * GROUPS,
            "projected": 2, "y_drained": 2, "sum_drained": 2,
            "token_filled": TOKEN_FILLS, "token_drained": TOKEN_FILLS,
            "weight_filled": WEIGHT_FILLS, "weight_drained": WEIGHT_FILLS,
            "top2_step": TOP2_STEPS, "gap_exp": 1, "x4_ready": 16 * 4 * A, "mixed": 4,
        }
        def sem(name):
            return ctx.enter_context(nc.semaphore(name))

        x_loaded = sem("x_loaded")
        x_kept_ready = sem("x_kept_ready")
        out_stored = sem("out_stored")
        sum1 = sem("sum1")
        mean1 = sem("mean1")
        centered1 = sem("centered1")
        squared1 = sem("squared1")
        sqsum1 = sem("sqsum1")
        var1 = sem("var1")
        rstd1 = sem("rstd1")
        normed1 = sem("normed1")
        sum2 = sem("sum2")
        mean2 = sem("mean2")
        centered2 = sem("centered2")
        squared2 = sem("squared2")
        sqsum2 = sem("sqsum2")
        var2 = sem("var2")
        rstd2 = sem("rstd2")
        normed2 = sem("normed2")
        pre_filled = sem("pre_filled")
        pre_drained = sem("pre_drained")
        q_placed = sem("q_placed")
        k_placed = sem("k_placed")
        max_filled = sem("max_filled")
        max_taken = sem("max_taken")
        shift_rounded = sem("shift_rounded")
        shift_split = sem("shift_split")
        shift_turned = sem("shift_turned")
        shift_rows_ready = sem("shift_rows_ready")
        scores_filled = sem("scores_filled")
        probs_ready = sem("probs_ready")
        pv_done = sem("pv_done")
        pv_drained = sem("pv_drained")
        sums_spread = sem("sums_spread")
        sums_inverted = sem("sums_inverted")
        o_normed = sem("o_normed")
        projected = sem("projected")
        y_drained = sem("y_drained")
        sum_drained = sem("sum_drained")
        token_filled = sem("token_filled")
        token_drained = sem("token_drained")
        weight_filled = sem("weight_filled")
        weight_drained = sem("weight_drained")
        top2_step = sem("top2_step")
        gap_exp = sem("gap_exp")
        x4_ready = sem("x4_ready")
        mixed = sem("mixed")
        zeroed = sem("zeroed")
        zeroed_even = sem("zeroed_even")
        zeroed_odd = sem("zeroed_odd")
        odd_v_zeroed = sem("odd_v_zeroed")
        consts_loaded = sem("consts_loaded")
        weights_loaded = sem("weights_loaded")
        rel_zeroed = sem("rel_zeroed")
        rel_loaded = sem("rel_loaded")
        weight_step = sem("weight_step")
        weights_ready = sem("weights_ready")

        def upto(name, unit, i=None):
            k = per_unit[name]
            return unit.n * k + (k if i is None else i + 1)

        def over(s, n):
            return s.unsqueeze(2).to_broadcast([s.shape[0], s.shape[1], n])

        def pieces(dram, tile, unit):
            view = tile.rearrange("p j k c -> p (j k) c")
            for b in range(2):
                for r0, r1 in ROW_CUTS:
                    for c0, c1 in COL_CUTS:
                        h = (r0 + SHIFT) % SIDE
                        w = (TOK * unit.par + c0 + SHIFT) % SIDE
                        yield (view[SIDE * b + r0:SIDE * b + r1, c0:c1, :],
                               dram[unit.slab * 2 + b, h:h + r1 - r0, w:w + c1 - c0, :])

        def rel_loads():
            line = (2 * WS - 1) * HEADS
            for g in range(2):
                for mj in range(WS):
                    row = PAD * g + mj * WS
                    yield (rel_raw[row:row + WS, :, :, :].rearrange("p i j h -> p i (j h)"),
                           bass.AP(rel_table.tensor, rel_table.offset + mj * HEADS, [[line, WS], [line, WS], [1, WS * HEADS]]))

        rel_list = list(rel_loads())
        block = ctx.enter_context(nc.Block())

        @block.sync
        def _(sp):
            def load(v, _):
                if v.has_before(1):
                    sp.wait_ge(centered1, upto("centered1", v.before(1)))
                    sp.wait_ge(x_kept_ready, upto("x_kept_ready", v.before(1)))
                for tile, dram in pieces(x, xin, v):
                    sp.dma_start(tile, dram).then_inc(x_loaded, 16)

            def keep(v, _):
                sp.wait_ge(x_loaded, upto("x_loaded", v))
                if v.has_before(2):
                    sp.wait_ge(token_drained, upto("token_drained", v.before(2), 1))
                sp.dma_start(x_kept[v.par].rearrange("p j k c -> p (j k c)"),
                             xin.rearrange("p j k c -> p (j k c)")).then_inc(x_kept_ready, 16)

            def place(v, _):
                sp.wait_ge(pre_drained, upto("pre_drained", v, 5))
                if v.has_before(2):
                    sp.wait_ge(scores_filled, upto("scores_filled", v.before(2)))
                if v.number == 0:
                    sp.wait_ge(zeroed, 1)
                    sp.wait_ge(zeroed_even, 1)
                if v.number == 1:
                    sp.wait_ge(zeroed_odd, 1)
                for h in range(HEADS):
                    for a in range(A):
                        r = slice(C * a + D * h, C * a + D * h + D)
                        sp.dma_start(qbd[v.par][r, :, h, :], qp[r, :, :]).then_inc(q_placed, 16)
                for a in range(A):
                    r = slice(C * a, C * a + C)
                    sp.dma_start(kz[v.par][r, :, a, :], kp[r, :, :]).then_inc(k_placed, 16)

            def replicate(w, _):
                sp.wait_ge(token_drained, upto("token_drained", w, 3))
                if w.has_before(1):
                    sp.wait_ge(mixed, upto("mixed", w.before(1)))
                for a in range(A):
                    for e in range(4):
                        sp.dma_start(x4[C * e:C * e + C, a, :], x2t[C * a:C * a + C, :]).then_inc(x4_ready, 16)

            def store(w, _):
                sp.wait_ge(weight_drained, upto("weight_drained", w))
                for tile, dram in pieces(out, x2[w.par], w):
                    sp.dma_start(dram, tile).then_inc(out_stored, 16)

            for step, unit, i in program(sp):
                if step == "load":
                    load(unit, i)
                elif step == "keep":
                    keep(unit, i)
                elif step == "place":
                    place(unit, i)
                elif step == "replicate":
                    replicate(unit, i)
                elif step == "store":
                    store(unit, i)
            sp.wait_ge(out_stored, UNITS * per_unit["out_stored"])

        @block.gpsimd
        def _(pool):
            def norm1_center(v, _):
                pool.wait_ge(mean1, upto("mean1", v))
                if v.has_before(1):
                    pool.wait_ge(pre_filled, upto("pre_filled", v.before(1), 1))
                nc.gpsimd.tensor_tensor(
                    xc1[:, :, :, :], xin.rearrange("p j k c -> p k j c"),
                    st1[:, 1, :].rearrange("p (j k) -> p k j", j=A).unsqueeze(3).to_broadcast([ROWS, WS, A, C]),
                    ALU.add).then_inc(centered1, 1)

            def norm1_scale(v, _):
                pool.wait_ge(var1, upto("var1", v))
                nc.gpsimd.tensor_tensor(st1[:, 4, :], st1[:, 3, :], minus_half[:, :], ALU.pow).then_inc(rstd1, 1)
                pool.wait_ge(rstd1, upto("rstd1", v))
                pool.wait_ge(squared1, upto("squared1", v))
                xc = xc1[:, :, :, :].rearrange("p k j c -> p (k j) c")
                nc.gpsimd.tensor_tensor(xc, xc, over(st1[:, 4, :], C), ALU.mult).then_inc(normed1, 1)

            def norm2_center(w, _):
                pool.wait_ge(mean2, upto("mean2", w))
                if w.has_before(1):
                    pool.wait_ge(token_filled, upto("token_filled", w.before(1), 3))
                nc.gpsimd.tensor_tensor(
                    xc2[:, :, :, :], x2[w.par].rearrange("p j k c -> p k j c"),
                    st2[:, 1, :].rearrange("p (j k) -> p k j", j=A).unsqueeze(3).to_broadcast([ROWS, WS, A, C]),
                    ALU.add).then_inc(centered2, 1)

            def norm2_scale(w, _):
                pool.wait_ge(var2, upto("var2", w))
                nc.gpsimd.tensor_tensor(st2[:, 4, :], st2[:, 3, :], minus_half[:, :], ALU.pow).then_inc(rstd2, 1)
                pool.wait_ge(rstd2, upto("rstd2", w))
                pool.wait_ge(squared2, upto("squared2", w))
                xc = xc2[:, :, :, :].rearrange("p k j c -> p (k j) c")
                nc.gpsimd.tensor_tensor(xc, xc, over(st2[:, 4, :], C), ALU.mult).then_inc(normed2, 1)

            def invert(u, i):
                g, half = divmod(i, 2)
                quads = slice(2 * half, 2 * half + 2)
                pool.wait_ge(sums_inverted, upto("sums_inverted", u, i))
                pool.wait_ge(pv_drained, upto("pv_drained", u, g))
                if i == 0:
                    if u.has_before(1):
                        pool.wait_ge(projected, upto("projected", u.before(1), 1))
                nc.gpsimd.tensor_tensor(
                    on[:, :, 4 * g + 2 * half:4 * g + 2 * half + 2, :], oe[g % 2][:, quads, :, :].rearrange("p q s n -> p s q n"),
                    rz[g % 2][:, quads, :, :].rearrange("p q s n -> p s q n"), ALU.mult).then_inc(o_normed, 1)

            nc.gpsimd.memset(minus_half[:, :], -0.5)
            nc.gpsimd.memset(qbd[0][:, :, :, :], 0.0)
            nc.gpsimd.memset(kz[0][:, :, :, :], 0.0).then_inc(zeroed_even, 1)
            for step, unit, i in program(pool):
                if step == "norm1_center":
                    norm1_center(unit, i)
                elif step == "norm1_scale":
                    norm1_scale(unit, i)
                elif step == "norm2_center":
                    norm2_center(unit, i)
                elif step == "norm2_scale":
                    norm2_scale(unit, i)
                elif step == "invert":
                    invert(unit, i)
                elif step == "place" and unit.number == 0:
                    nc.gpsimd.memset(qbd[1][:, :, :, :], 0.0)
                    nc.gpsimd.memset(kz[1][:, :, :, :], 0.0)
                    nc.gpsimd.memset(mr[1][:, :], 0.0).then_inc(zeroed_odd, 1)

        @block.scalar
        def _(act):
            def norm1_square(v, _):
                if v.has_before(3):
                    act.wait_ge(sqsum2, upto("sqsum2", v.before(3)))
                else:
                    if v.has_before(1):
                        act.wait_ge(sqsum1, upto("sqsum1", v.before(1)))
                act.wait_ge(centered1, upto("centered1", v))
                nc.scalar.activation(sq[:, :, :, :], xc1[:, :, :, :], ACT.Square).then_inc(squared1, 1)

            def norm2_square(w, _):
                if w.number is None or w.number + 2 < UNITS:
                    act.wait_ge(sqsum1, upto("sqsum1", Unit(w.n + 2, None, None)))
                else:
                    act.wait_ge(sqsum2, upto("sqsum2", w.before(1)))
                act.wait_ge(centered2, upto("centered2", w))
                nc.scalar.activation(sq[:, :, :, :], xc2[:, :, :, :], ACT.Square).then_inc(squared2, 1)

            def xt_drain(v, i):
                act.wait_ge(pre_filled, upto("pre_filled", v, i))
                k0, k1 = (0, 4) if i == 0 else (4, 7)
                if i == 0:
                    if v.has_before(1):
                        act.wait_ge(pre_filled, upto("pre_filled", v.before(1), 7))
                nc.scalar.copy(xt[:, :, k0:k1, :].rearrange("p q k i -> p k q i"),
                                    ps_pre[:, 0:(k1 - k0) * ROWS].rearrange("p (k q i) -> p k q i", q=Q, i=WS)).then_inc(pre_drained, 1)

            def qk_drain(v, i):
                act.wait_ge(pre_filled, upto("pre_filled", v, 2 + i))
                src = ps_pre[:, 0:HALF].rearrange("p (q n) -> p q n", n=N)
                if i < 2:
                    if v.has_before(1):
                        act.wait_ge(q_placed, upto("q_placed", v.before(1)))
                    ins = nc.scalar.activation(qp[:, 8 * i:8 * i + 8, :], src, ACT.Identity,
                                               bias=biases[:, 3:4], scale=SCALE)
                else:
                    if v.has_before(1):
                        act.wait_ge(k_placed, upto("k_placed", v.before(1)))
                    ins = nc.scalar.activation(kp[:, 8 * (i - 2):8 * (i - 2) + 8, 0:N], src, ACT.Identity,
                                               bias=biases[:, 1:2])
                ins.then_inc(pre_drained, 1)

            def v_drain(v, i):
                act.wait_ge(pre_filled, upto("pre_filled", v, 6 + i))
                if v.has_before(2):
                    act.wait_ge(pv_done, upto("pv_done", v.before(2)))
                if v.number == 1:
                    act.wait_ge(odd_v_zeroed, 2)
                for g in range(2):
                    r = slice(PAD * g, PAD * g + N)
                    ins = nc.scalar.copy(
                        vb[v.par][r, 8 * i:8 * i + 8, :, :, D * g:D * g + D].rearrange("p q s h d -> p (q s h) d"),
                        ps_pre[r, :].rearrange("p (t d) -> p t d", d=D))
                ins.then_inc(pre_drained, 1)

            def ob_drain(v, i):
                act.wait_ge(pre_filled, upto("pre_filled", v, 8 + i))
                if i == 0:
                    if v.has_before(1):
                        act.wait_ge(pre_filled, upto("pre_filled", v.before(1)))
                for p in range(2):
                    ins = nc.scalar.copy(obs[:, :, :, i, p, :].rearrange("p i b s -> p b i s"),
                                         ps_pre[:, 256 * p:256 * p + 256].rearrange("p (b i s) -> p b i s", b=2, s=16))
                ins.then_inc(pre_drained, 1)

            def obt_drain(v, i):
                act.wait_ge(pre_filled, upto("pre_filled", v, 10 + i))
                if i == 0:
                    if v.has_before(2):
                        act.wait_ge(projected, upto("projected", v.before(2), 1))
                nc.scalar.copy(
                    obt[v.par][:, :, 4 * i:4 * i + 4, :].rearrange("p s i n -> p i s n"),
                    ps_pre[:, :].rearrange("p (i s n) -> p i s n", s=2, n=PAD)[:, :, :, 0:N]).then_inc(pre_drained, 1)

            def shift_drain(u, g):
                act.wait_ge(shift_turned, upto("shift_turned", u, g))
                if g >= 2:
                    act.wait_ge(scores_filled, upto("scores_filled", u, 4 * (g - 2) + 3))
                else:
                    if u.has_before(1):
                        act.wait_ge(scores_filled, upto("scores_filled", u.before(1), 4 * (g + 2) + 3))
                if u.number == 0 and g == 1:
                    act.wait_ge(zeroed_odd, 1)
                nc.scalar.copy(mr[g % 2][0:32, :], ps_small[0:32, 0:HN // 2].bitcast(BF16)).then_inc(shift_rows_ready, 1)

            def exponentials(u, q):
                act.wait_ge(scores_filled, upto("scores_filled", u, q))
                if q >= 2:
                    act.wait_ge(pv_done, upto("pv_done", u, q - 2))
                else:
                    if u.has_before(1):
                        act.wait_ge(pv_done, upto("pv_done", u.before(1), q + Q - 2))
                nc.scalar.activation(pt[q % 2][:, :, :, :].rearrange("p s h n -> p (s h n)"),
                                          ps_scores[:, 0:2 * HN], ACT.Exp).then_inc(probs_ready, 1)

            def pv_drain(u, g):
                act.wait_ge(pv_done, upto("pv_done", u, 4 * g + 3))
                if g >= 2:
                    act.wait_ge(o_normed, upto("o_normed", u, 2 * (g - 2) + 1))
                else:
                    if u.has_before(1):
                        act.wait_ge(o_normed, upto("o_normed", u.before(1), 2 * (g + 2) + 1))
                nc.scalar.copy(oe[g % 2][:, :, :, :].rearrange("p q s n -> p (q s n)"), ps_pv[:, 0:HALF]).then_inc(pv_drained, 1)

            def y_drain(w, b):
                act.wait_ge(projected, upto("projected", w, b))
                if b == 0:
                    if w.has_before(2):
                        act.wait_ge(weight_filled, upto("weight_filled", w.before(2)))
                    elif w.has_before(1):
                        act.wait_ge(token_filled, upto("token_filled", w.before(1), 1))
                nc.scalar.activation(
                    ym[:, :, SIDE * b:SIDE * b + SIDE].rearrange("p k (i j) -> p i k j", j=WS),
                    ps_acc[:, 0:HALF].rearrange("p (i k j) -> p i k j", k=WS, j=WS), ACT.Identity,
                    bias=biases[:, 2:3]).then_inc(y_drained, 1)

            def x2t_drain(w, i):
                act.wait_ge(token_filled, upto("token_filled", w, 2 + i))
                if i == 0:
                    if w.has_before(1):
                        act.wait_ge(x4_ready, upto("x4_ready", w.before(1)))
                c0, c1 = (0, 4 * ROWS) if i == 0 else (4 * ROWS, COLS)
                nc.scalar.copy(x2t[:, c0:c1], ps_token[:, 0:c1 - c0]).then_inc(token_drained, 1)

            def top2_exp(w, _):
                act.wait_ge(top2_step, upto("top2_step", w, GAP_STEP))
                nc.scalar.activation(top[:, 3, :], top[:, 2, :], ACT.Exp).then_inc(gap_exp, 1)

            def wt_drain(w, _):
                act.wait_ge(weight_filled, upto("weight_filled", w, 0))
                nc.scalar.copy(wt[:, :], ps_weight[0:96, 0:COLS // 2].bitcast(BF16)).then_inc(weight_drained, 1)

            def mix_drain(w, half):
                act.wait_ge(mixed, upto("mixed", w, 2 * half + 1))
                if half == 0:
                    if w.has_after():
                        act.wait_ge(token_filled, upto("token_filled", w.after(), 1))
                    else:
                        act.wait_ge(weight_filled, upto("weight_filled", w.before(1)))
                nc.scalar.copy(ym[:, :, :].rearrange("p k r -> p (k r)")[:, HALF * half:HALF * half + HALF],
                                    ps_acc[:, 0:HALF]).then_inc(sum_drained, 1)

            act.dma_start(const_tile[:, :], consts).then_inc(consts_loaded, 16)
            act.dma_start(weight_tile[:, :], weights).then_inc(weights_loaded, 16)
            act.dma_start(const_bf16_tile[:, :], consts_bf16).then_inc(weights_loaded, 16)
            act.wait_ge(rel_zeroed, 1)
            for dst, src in rel_list:
                act.dma_start(dst, src).then_inc(rel_loaded, 16)
            for step, unit, i in program(act):
                if step == "norm1_square":
                    norm1_square(unit, i)
                elif step == "norm2_square":
                    norm2_square(unit, i)
                elif step == "prepare" and unit.number == 0:
                    act.wait_ge(weights_ready, 1)
                elif step == "xt":
                    xt_drain(unit, i)
                elif step == "qk":
                    qk_drain(unit, i)
                elif step == "v":
                    v_drain(unit, i)
                elif step == "ob":
                    ob_drain(unit, i)
                elif step == "obt":
                    obt_drain(unit, i)
                elif step == "shift":
                    shift_drain(unit, i)
                elif step == "scores":
                    exponentials(unit, i)
                elif step == "pv_drain":
                    pv_drain(unit, i)
                elif step == "y":
                    y_drain(unit, i)
                elif step == "x2t":
                    x2t_drain(unit, i)
                elif step == "top2_exp":
                    top2_exp(unit, i)
                elif step == "wt":
                    wt_drain(unit, i)
                elif step == "mix_drain":
                    mix_drain(unit, i)

        @block.vector
        def _(dve):
            def norm1_center(v, _):
                dve.wait_ge(x_loaded, upto("x_loaded", v))
                if v.has_before(1):
                    dve.wait_ge(centered1, upto("centered1", v.before(1)))
                nc.vector.tensor_reduce(st1[:, 0, :], xin.rearrange("p j k c -> p (j k) c"), AX, ALU.add).then_inc(sum1, 1)
                dve.wait_ge(sum1, upto("sum1", v))
                nc.vector.tensor_scalar(st1[:, 1, :], st1[:, 0, :], -1.0 / C, None, ALU.mult).then_inc(mean1, 1)

            def norm1_scale(v, _):
                dve.wait_ge(squared1, upto("squared1", v))
                if v.has_before(1):
                    dve.wait_ge(normed1, upto("normed1", v.before(1)))
                nc.vector.tensor_reduce(st1[:, 2, :], sq[:, :, :, :].rearrange("p k j c -> p (k j) c"), AX, ALU.add).then_inc(sqsum1, 1)
                dve.wait_ge(sqsum1, upto("sqsum1", v))
                nc.vector.tensor_scalar(st1[:, 3, :], st1[:, 2, :], 1.0 / C, LN1_EPS, ALU.mult, ALU.add).then_inc(var1, 1)

            def norm2_center(w, _):
                dve.wait_ge(token_drained, upto("token_drained", w, 1))
                if w.has_before(1):
                    dve.wait_ge(centered2, upto("centered2", w.before(1)))
                nc.vector.tensor_reduce(st2[:, 0, :], x2[w.par].rearrange("p j k c -> p (j k) c"), AX, ALU.add).then_inc(sum2, 1)
                dve.wait_ge(sum2, upto("sum2", w))
                nc.vector.tensor_scalar(st2[:, 1, :], st2[:, 0, :], -1.0 / C, None, ALU.mult).then_inc(mean2, 1)

            def norm2_scale(w, _):
                dve.wait_ge(squared2, upto("squared2", w))
                if w.has_before(1):
                    dve.wait_ge(normed2, upto("normed2", w.before(1)))
                nc.vector.tensor_reduce(st2[:, 2, :], sq[:, :, :, :].rearrange("p k j c -> p (k j) c"), AX, ALU.add).then_inc(sqsum2, 1)
                dve.wait_ge(sqsum2, upto("sqsum2", w))
                nc.vector.tensor_scalar(st2[:, 3, :], st2[:, 2, :], 1.0 / C, LN2_EPS, ALU.mult, ALU.add).then_inc(var2, 1)

            def maximum(u, q):
                dve.wait_ge(max_filled, upto("max_filled", u, q))
                nc.vector.tensor_reduce(
                    mx[(q // 4) % 2][:, :, q % 4, :],
                    ps_max[0:2 * N, 0:2 * A * EVEN].rearrange("p (s a m) -> p s a m", s=2, a=A)[:, :, :, 0:N], AX, ALU.max).then_inc(max_taken, 1)

            def split(u, g):
                m = mx[g % 2].rearrange("p s q a -> p s (q a)")
                hi, lo = ms[g % 2][:, :, 0, :], ms[g % 2][:, :, 1, :]
                dve.wait_ge(max_taken, upto("max_taken", u, 4 * g + 3))
                if g >= 2:
                    dve.wait_ge(shift_turned, upto("shift_turned", u, g - 2))
                else:
                    if u.has_before(1):
                        dve.wait_ge(shift_turned, upto("shift_turned", u.before(1), g + 2))
                nc.vector.tensor_scalar(hi, m, -1.0, None, ALU.mult).then_inc(shift_rounded, 1)
                dve.wait_ge(shift_rounded, upto("shift_rounded", u, g))
                nc.vector.scalar_tensor_tensor(out=lo, in0=m, scalar=-1.0, in1=hi, op0=ALU.mult,
                                                    op1=ALU.subtract).then_inc(shift_split, 1)

            def invert(u, i):
                g, half = divmod(i, 2)
                dve.wait_ge(sums_spread, upto("sums_spread", u, g))
                if half == 0:
                    if g >= 2:
                        dve.wait_ge(o_normed, upto("o_normed", u, 2 * (g - 2) + 1))
                    else:
                        if u.has_before(1):
                            dve.wait_ge(o_normed, upto("o_normed", u.before(1), 2 * (g + 2) + 1))
                nc.vector.reciprocal(rz[g % 2][:, 2 * half:2 * half + 2, :, :].rearrange("p q s n -> p (q s n)"),
                                     ps_small[:, HALF // 2 * half:HALF // 2 * half + HALF // 2]).then_inc(sums_inverted, 1)

            def residual(w, i):
                dve.wait_ge(token_filled, upto("token_filled", w, i))
                dve.wait_ge(x_kept_ready, upto("x_kept_ready", w))
                k0, k1 = (0, 4) if i == 0 else (4, 7)
                if i == 0:
                    if w.has_before(2):
                        dve.wait_ge(out_stored, upto("out_stored", w.before(2)))
                nc.vector.tensor_tensor(
                    x2[w.par][:, :, k0:k1, :].rearrange("p j k c -> p k j c"),
                    ps_token[0:ROWS, 0:(k1 - k0) * 128].rearrange("p (k j c) -> p k j c", j=A, c=C),
                    x_kept[w.par][:, :, k0:k1, :].rearrange("p j k c -> p k j c"), ALU.add).then_inc(token_drained, 1)

            def router(w, _):
                dve.wait_ge(token_filled, upto("token_filled", w, 4))
                nc.vector.tensor_tensor(
                    logits[:, :, :], ps_token[0:ROWS, 0:TOK * E].rearrange("p (t e) -> p t e", e=E),
                    rb[:, :].unsqueeze(1).to_broadcast([ROWS, TOK, E]), ALU.add).then_inc(token_drained, 1)

            at = [0]

            def link(ins, w):
                ins.then_inc(top2_step, 1)
                dve.wait_ge(top2_step, upto("top2_step", w, at[0]))
                at[0] += 1

            def at_largest(w, vals, m):
                link(nc.vector.tensor_reduce(top[:, m, :], vals, AX, ALU.max), w)
                link(nc.vector.tensor_tensor(tmp[:, :, :], vals, over(top[:, m, :], E), ALU.is_equal), w)
                link(nc.vector.tensor_tensor(tmp[:, :, :], tmp[:, :, :],
                                             rank[:, :].unsqueeze(1).to_broadcast([ROWS, TOK, E]), ALU.mult), w)

            def first_of_them(w, r, pick):
                link(nc.vector.tensor_reduce(top[:, r, :], tmp[:, :, :], AX, ALU.max), w)
                link(nc.vector.tensor_tensor(pick, tmp[:, :, :], over(top[:, r, :], E), ALU.is_equal), w)

            def top2(w, i):
                tt, V = nc.vector.tensor_tensor, nc.vector
                if i == 0:
                    at[0] = 0
                    dve.wait_ge(token_drained, upto("token_drained", w, 4))
                    at_largest(w, logits[:, :, :], 0)
                elif i == 1:
                    first_of_them(w, 7, pick1[:, :, :])
                    link(V.scalar_tensor_tensor(out=logits[:, :, :], in0=pick1[:, :, :], scalar=BELOW_ALL,
                                                in1=logits[:, :, :], op0=ALU.mult, op1=ALU.add), w)
                elif i == 2:
                    at_largest(w, logits[:, :, :], 1)
                    if w.has_before(1):
                        dve.wait_ge(gap_exp, upto("gap_exp", w.before(1)))
                    assert at[0] == GAP_STEP
                    link(tt(top[:, 2, :], top[:, 1, :], top[:, 0, :], ALU.subtract), w)
                elif i == 3:
                    first_of_them(w, 6, pick2[:, :, :])
                elif i == 4:
                    dve.wait_ge(gap_exp, upto("gap_exp", w))
                    link(V.tensor_scalar(top[:, 4, :], top[:, 3, :], 1.0, None, ALU.add), w)
                    link(V.reciprocal(top[:, 5, :], top[:, 4, :]), w)
                    link(tt(top[:, 4, :], top[:, 3, :], top[:, 5, :], ALU.mult), w)
                elif i == 5:
                    link(tt(pick1[:, :, :], pick1[:, :, :], over(top[:, 5, :], E), ALU.mult), w)
                    link(tt(pick2[:, :, :], pick2[:, :, :], over(top[:, 4, :], E), ALU.mult), w)
                    link(tt(mixw[:, :, :], pick1[:, :, :], pick2[:, :, :], ALU.add), w)
                else:
                    parts = [w_parts[:, :, k, :] for k in range(3)]
                    whole = mixw[:, :, :].rearrange("p (k j) e -> p k (j e)", j=A)
                    rest = tmp[:, :, :].rearrange("p (k j) e -> p k (j e)", j=A)
                    if i == 6:
                        if w.has_before(1):
                            dve.wait_ge(weight_filled, upto("weight_filled", w.before(1), 0))
                        link(V.tensor_copy(parts[0], whole), w)
                        link(tt(rest, whole, parts[0], ALU.subtract), w)
                    else:
                        link(V.tensor_copy(parts[1], rest), w)
                        link(tt(parts[2], rest, parts[1], ALU.subtract), w)
                        assert at[0] == TOP2_STEPS, at[0]

            def mix(w, i):
                if i == 16:
                    return
                half, eh, a = i // E, i // A % 2, i % A
                dve.wait_ge(weight_filled, upto("weight_filled", w, 1 + i))
                if i == 0:
                    dve.wait_ge(x4_ready, upto("x4_ready", w))
                if eh == 0 and half:
                    dve.wait_ge(mixed, upto("mixed", w, 0))
                elif eh == 0:
                    if w.has_before(1):
                        dve.wait_ge(mixed, upto("mixed", w.before(1), 2))
                tokens = x4[:, a, HALF * half:HALF * half + HALF]
                nc.vector.tensor_tensor(tokens if eh else zt[:, a, :], ps_weight[:, 0:HALF], tokens,
                                        ALU.mult).then_inc(weight_drained, 1)

            def final(w, i):
                dve.wait_ge(weight_filled, upto("weight_filled", w, 17 + i))
                k0, k1 = (0, 4) if i == 0 else (4, 7)
                tokens = x2[w.par][:, :, k0:k1, :].rearrange("p j k c -> p k j c")
                nc.vector.tensor_tensor(
                    tokens, ps_weight[0:ROWS, 0:(k1 - k0) * 128].rearrange("p (k j c) -> p k j c", j=A, c=C),
                    tokens, ALU.add).then_inc(weight_drained, 1)

            V = nc.vector

            def ones(buf):
                for g in range(2):
                    ins = V.memset(buf[PAD * g:PAD * g + N, :, :, :, 16 + D * g:16 + D * g + D].rearrange(
                        "p q s h t -> p (q s h) t"), 1.0)
                return ins

            count = [0]

            def chain(ins):
                ins.then_inc(weight_step, 1)
                count[0] += 1
                dve.wait_ge(weight_step, count[0])

            def prepare():
                dve.wait_ge(weights_loaded, 32)
                dve.wait_ge(consts_loaded, 16)
                chain(V.tensor_scalar(biases[:, 3:4], biases[:, 0:1], SCALE, None, ALU.mult))
                chain(V.tensor_copy(eb[:, 0, :], eb_raw))
                chain(V.tensor_tensor(eb_rest[:, :], eb_raw, eb[:, 0, :], ALU.subtract))
                chain(V.tensor_copy(eb[:, 1, :], eb_rest[:, :]))
                chain(V.tensor_tensor(eb[:, 2, :], eb_rest[:, :], eb[:, 1, :], ALU.subtract))
                chain(V.tensor_copy(bv_parts[:, 0, :], bv_raw))
                chain(V.tensor_tensor(bv_rest[:, :], bv_raw, bv_parts[:, 0, :], ALU.subtract))
                chain(V.tensor_copy(bv_parts[:, 1, :], bv_rest[:, :]))
                chain(V.tensor_tensor(bv_parts[:, 2, :], bv_rest[:, :], bv_parts[:, 1, :], ALU.subtract))
                chain(V.tensor_scalar(bv_rows[:, 0, :], bv_parts[:, 0, :], ident[0:3, 0:1], None, ALU.mult))
                chain(V.scalar_tensor_tensor(out=bv_rows[:, 1, :], in0=bv_parts[:, 1, :], scalar=ident[0:3, 1:2],
                                            in1=bv_rows[:, 0, :], op0=ALU.mult, op1=ALU.add))
                chain(V.scalar_tensor_tensor(out=bv_rows[:, 0, :], in0=bv_parts[:, 2, :], scalar=ident[0:3, 2:3],
                                            in1=bv_rows[:, 1, :], op0=ALU.mult, op1=ALU.add))
                chain(V.tensor_copy(bv[0:3, :, :], bv_rows[:, 0, :].unsqueeze(1).to_broadcast([3, Q, C])))
                dve.wait_ge(rel_loaded, 16 * len(rel_list))
                for h in range(HEADS):
                    for kind in range(4):
                        ins = V.tensor_tensor(
                            bt[:, h, kind, 0:N].rearrange("p (j i) -> p j i", j=WS),
                            rel_raw[:, ::-1, ::-1, h].rearrange("p i j -> p j i"),
                            mask[:, kind, 0:N].rearrange("p (j i) -> p j i", j=WS), ALU.add)
                ins.then_inc(weights_ready, 1)

            V.memset(rel_raw[:, :, :, :], 0.0).then_inc(rel_zeroed, 1)
            V.memset(bv[:, :, :], 0.0)
            V.memset(bt[:, :, :, :], 0.0)
            V.memset(kp[:, :, :], 0.0)
            V.memset(mr[0][:, :], 0.0)
            V.memset(vb[0][:, :, :, :, :], 0.0).then_inc(zeroed, 1)
            dve.wait_ge(zeroed, 1)
            ones(vb[0])
            for step, unit, i in program(dve):
                if step == "norm1_center":
                    norm1_center(unit, i)
                elif step == "norm1_scale":
                    norm1_scale(unit, i)
                elif step == "norm2_center":
                    norm2_center(unit, i)
                elif step == "norm2_scale":
                    norm2_scale(unit, i)
                elif step == "prepare" and unit.number == 0:
                    prepare()
                elif step == "place" and unit.number == 0:
                    V.memset(vb[1][:, :, :, :, :], 0.0).then_inc(odd_v_zeroed, 1)
                    dve.wait_ge(odd_v_zeroed, 1)
                    ones(vb[1]).then_inc(odd_v_zeroed, 1)
                elif step == "maximum":
                    maximum(unit, i)
                elif step == "split":
                    split(unit, i)
                elif step == "invert":
                    invert(unit, i)
                elif step == "back":
                    residual(unit, i)
                elif step == "router":
                    router(unit, i)
                elif step == "top2":
                    top2(unit, i)
                elif step == "mix":
                    mix(unit, i)
                elif step == "final":
                    final(unit, i)

        @block.tensor
        def _(pe):
            mm = nc.tensor.matmul

            def xt_turn(v, i):
                if i or v.has_before(1):
                    pe.wait_ge(pre_drained, upto("pre_drained", v, i - 1))
                pe.wait_ge(normed1, upto("normed1", v))
                for k in range(*((0, 4) if i == 0 else (4, 7))):
                    ins = nc.tensor.transpose(ps_pre[:, (k % 4) * ROWS:(k % 4) * ROWS + ROWS],
                                              xc1[:, k, :, :].rearrange("p j c -> p (j c)"), ident[0:ROWS, 0:ROWS])
                ins.then_inc(pre_filled, 1)

            def qk(v, i):
                pe.wait_ge(pre_drained, upto("pre_drained", v, 1 + i))
                b = i % 2
                mm(ps_pre[:, 0:HALF], (wq if i < 2 else wk)[:, :],
                        xt[:, 8 * b:8 * b + 8, :, :].rearrange("p q k i -> p (q k i)"), start=True, stop=True).then_inc(pre_filled, 1)

            def v_products(v, i):
                pe.wait_ge(pre_drained, upto("pre_drained", v, 5 + i))
                mm(ps_pre[:, :], first3[:, :], bv[:, :, :].rearrange("p q c -> p (q c)"), start=True, stop=False,
                   skip_group_check=True)
                for q in range(8):
                    keys = xt[:, 8 * i + q, :, :].rearrange("p k i -> p (k i)")
                    for g in range(2):
                        ins = mm(ps_pre[PAD * g:PAD * g + N, 64 * q:64 * q + 64], keys,
                                 wv[:, g, :, :].rearrange("p s c -> p (s c)"), start=False,
                                 stop=(q == 7), skip_group_check=True)
                ins.then_inc(pre_filled, 1)

            def ob(v, i):
                pe.wait_ge(pre_drained, upto("pre_drained", v, 7 + i))
                for hh in range(2):
                    h = 2 * hh + i
                    for p in range(2):
                        for last_row in range(2):
                            kind = last_row + 2 * (v.par and p)
                            w0, w1 = (WS, WS + 1) if last_row else (0, WS)
                            dst = ps_pre[PAD * hh:PAD * hh + PAD, 256 * p:256 * p + 256].rearrange(
                                "p (b i s) -> p b i s", b=2, s=16)[:, :, w0:w1, :]
                            src = vb[v.par][:, :, p, h, 0:16].rearrange("p (b i) s -> p b i s", b=2)[:, :, w0:w1, :]
                            ins = mm(dst, bt[:, h, kind, :], src, start=True, stop=True)
                ins.then_inc(pre_filled, 1)

            def ob_turn(v, i):
                pe.wait_ge(pre_drained, upto("pre_drained", v, 9 + i))
                for k in range(4):
                    ins = nc.tensor.transpose(ps_pre[:, 128 * k:128 * k + 128],
                                              obs[:, 4 * i + k, :, :, :, :].rearrange("p b h s t -> p (b h s t)"),
                                              ident[:, :])
                ins.then_inc(pre_filled, 1)

            def max_scores(u, q):
                if q or u.has_before(1):
                    pe.wait_ge(max_taken, upto("max_taken", u, q - 1))
                if q == 0:
                    pe.wait_ge(q_placed, upto("q_placed", u))
                    pe.wait_ge(k_placed, upto("k_placed", u))
                for s in range(2):
                    ins = mm(ps_max[0:2 * N, A * EVEN * s:A * EVEN * s + A * EVEN],
                             qbd[u.par][:, q, 2 * s:2 * s + 2, :].rearrange("p h n -> p (h n)").bitcast(F32R),
                             kz[u.par][:, q, :, 0:EVEN].bitcast(F32R), start=True, stop=True)
                ins.then_inc(max_filled, 1)

            def shift_turn(u, g):
                pe.wait_ge(shift_split, upto("shift_split", u, g))
                if g >= 2:
                    pe.wait_ge(sums_inverted, upto("sums_inverted", u, 2 * (g - 2) + 1))
                else:
                    if u.has_before(1):
                        pe.wait_ge(sums_inverted, upto("sums_inverted", u.before(1), 2 * (g + 2) + 1))
                if g or u.has_before(1):
                    pe.wait_ge(shift_rows_ready, upto("shift_rows_ready", u, g - 1))
                for s in range(2):
                    ins = nc.tensor.transpose(
                        ps_small[0:32, :].bitcast(BF16)[:, 2 * N * s:2 * N * s + 2 * N],
                        ms[g % 2][:, s, :, :].rearrange("p k r -> p (k r)"), identb[0:2 * N, 0:2 * N])
                ins.then_inc(shift_turned, 1)

            def scores(u, q):
                if q or u.has_before(1):
                    pe.wait_ge(probs_ready, upto("probs_ready", u, q - 1))
                if q % 4 == 0:
                    pe.wait_ge(shift_rows_ready, upto("shift_rows_ready", u, q // 4))
                for p in range(2):
                    dst = ps_scores[:, HN * p:HN * p + HN]
                    mm(dst, shift_sel[:, q % 4, p, :], mr[(q // 4) % 2][:, :], start=True, stop=False)
                    ins = mm(dst, kz[u.par][:, q, 2 * p:2 * p + 2, :].rearrange("p a m -> p (a m)"),
                             qbd[u.par][:, q, :, :].rearrange("p h n -> p (h n)"), start=False, stop=True)
                ins.then_inc(scores_filled, 1)

            def pv(u, q):
                pe.wait_ge(probs_ready, upto("probs_ready", u, q))
                if q % 4 == 0:
                    if q // 4 or u.has_before(1):
                        pe.wait_ge(pv_drained, upto("pv_drained", u, q // 4 - 1))
                for p in range(2):
                    c0 = (2 * (q % 4) + p) * N
                    for h in range(HEADS):
                        ins = mm(ps_pv[SLOT * h:SLOT * h + SLOT, c0:c0 + N], vb[u.par][:, q, p, h, :],
                                 pt[q % 2][:, p, h, :], start=True, stop=True)
                ins.then_inc(pv_done, 1)

            def normalise(u, g):
                pe.wait_ge(pv_drained, upto("pv_drained", u, g))
                if g < GROUPS - 1:
                    pe.wait_ge(shift_rows_ready, upto("shift_rows_ready", u, g + 1))
                elif u.number != UNITS - 1:
                    pe.wait_ge(shift_rows_ready, upto("shift_rows_ready", u.after(), 0))
                if g or u.has_before(1):
                    pe.wait_ge(sums_inverted, upto("sums_inverted", u, 2 * g - 1))
                mm(ps_small[:, 0:HALF], z_sel[:, :], oe[g % 2][:, :, :, :].rearrange("p q s n -> p (q s n)"),
                        start=True, stop=True).then_inc(sums_spread, 1)

            def y(w, b):
                if b:
                    pe.wait_ge(y_drained, upto("y_drained", w, 0))
                elif w.has_before(2):
                    pe.wait_ge(sum_drained, upto("sum_drained", w.before(2)))
                elif w.has_before(1):
                    pe.wait_ge(y_drained, upto("y_drained", w.before(1)))
                for hh in range(2):
                    mm(ps_acc[:, 0:HALF], w_proj_b[:, b, hh, :, :].rearrange("p a c -> p (a c)"),
                       obt[w.par][:, hh, :, :].rearrange("p i n -> p (i n)"), start=(hh == 0), stop=False,
                       skip_group_check=True)
                if b == 0:
                    pe.wait_ge(o_normed, upto("o_normed", w))
                for p in range(2):
                    ins = mm(ps_acc[64 * p:64 * p + 64, 0:HALF], w_proj_o[:, :, :].rearrange("p g c -> p (g c)"),
                             on[:, p, 8 * b:8 * b + 8, :].rearrange("p q n -> p (q n)"), start=False, stop=True,
                             skip_group_check=True)
                ins.then_inc(projected, 1)

            def turn_back(bank, i):
                for k in range(*((0, 4) if i == 0 else (4, 7))):
                    ins = nc.tensor.transpose(bank[0:ROWS, (k % 4) * 128:(k % 4) * 128 + 128], ym[:, k, :],
                                              ident[:, :])
                return ins

            def back(w, i):
                pe.wait_ge(y_drained, upto("y_drained", w))
                if i or w.has_before(1):
                    pe.wait_ge(token_drained, upto("token_drained", w, i - 1))
                turn_back(ps_token, i).then_inc(token_filled, 1)

            def x2t_turn(w, i):
                pe.wait_ge(token_drained, upto("token_drained", w, 1 + i))
                pe.wait_ge(normed2, upto("normed2", w))
                for k in range(*((0, 4) if i == 0 else (4, 7))):
                    ins = nc.tensor.transpose(ps_token[:, (k % 4) * ROWS:(k % 4) * ROWS + ROWS],
                                              xc2[:, k, :, :].rearrange("p j c -> p (j c)"), ident[0:ROWS, 0:ROWS])
                ins.then_inc(token_filled, 1)

            def router(w, _):
                pe.wait_ge(token_drained, upto("token_drained", w, 3))
                for k in range(WS):
                    ins = mm(ps_token[0:ROWS, 32 * k:32 * k + 32], x2t[:, ROWS * k:ROWS * k + ROWS],
                             wr[:, :, :].rearrange("p a e -> p (a e)"), start=True, stop=True)
                ins.then_inc(token_filled, 1)

            def wt_turn(w, _):
                if w.has_before(1):
                    pe.wait_ge(weight_drained, upto("weight_drained", w.before(1)))
                pe.wait_ge(top2_step, upto("top2_step", w))
                for k in range(WS):
                    ins = nc.tensor.transpose(ps_weight[0:96, :].bitcast(BF16)[:, ROWS * k:ROWS * k + ROWS],
                                              w_parts[:, k, :, :].rearrange("p t e -> p (t e)"),
                                              identb[0:ROWS, 0:ROWS])
                ins.then_inc(weight_filled, 1)

            def mix(w, i):
                if i < 16:
                    half, eh, a = i // E, i // A % 2, i % A
                    pe.wait_ge(weight_drained, upto("weight_drained", w, i))
                    mm(ps_weight[:, 0:HALF], weight_sel[:, eh, a, :], wt[:, HALF * half:HALF * half + HALF],
                            start=True, stop=True).then_inc(weight_filled, 1)
                if i not in MIX_PRODUCTS:
                    return
                half, eh = divmod(MIX_PRODUCTS.index(i), 2)
                if eh == 0:
                    if half:
                        pe.wait_ge(sum_drained, upto("sum_drained", w, 0))
                    elif w.has_after():
                        pe.wait_ge(y_drained, upto("y_drained", w.after()))
                    else:
                        pe.wait_ge(sum_drained, upto("sum_drained", w.before(1)))
                    for k in range(3):
                        mm(ps_acc[:, 0:HALF], eb[:, k, :], wt[:, HALF * half:HALF * half + HALF],
                           start=(k == 0), stop=False, skip_group_check=True)
                pe.wait_ge(weight_drained, upto("weight_drained", w, E * half + A * eh + A))
                for a in range(A):
                    tokens = x4[:, a, HALF * half:HALF * half + HALF] if eh else zt[:, a, :]
                    ins = mm(ps_acc[C * a:C * a + C, 0:HALF], we[:, eh, :], tokens, start=False, stop=(eh == 1),
                             skip_group_check=True)
                ins.then_inc(mixed, 1)

            def final(w, i):
                pe.wait_ge(sum_drained, upto("sum_drained", w))
                pe.wait_ge(weight_drained, upto("weight_drained", w, 16 + i))
                turn_back(ps_weight, i).then_inc(weight_filled, 1)

            pe.wait_ge(consts_loaded, 16)
            for step, unit, i in program(pe):
                if step == "xt":
                    xt_turn(unit, i)
                elif step == "prepare" and unit.number == 0:
                    pe.wait_ge(weights_ready, 1)
                elif step == "qk":
                    qk(unit, i)
                elif step == "v":
                    v_products(unit, i)
                elif step == "ob":
                    ob(unit, i)
                elif step == "obt":
                    ob_turn(unit, i)
                elif step == "maximum":
                    max_scores(unit, i)
                elif step == "shift":
                    shift_turn(unit, i)
                elif step == "scores":
                    scores(unit, i)
                elif step == "pv":
                    pv(unit, i)
                elif step == "normalise":
                    normalise(unit, i)
                elif step == "y":
                    y(unit, i)
                elif step == "back":
                    back(unit, i)
                elif step == "x2t":
                    x2t_turn(unit, i)
                elif step == "router":
                    router(unit, i)
                elif step == "wt":
                    wt_turn(unit, i)
                elif step == "mix":
                    mix(unit, i)
                elif step == "final":
                    final(unit, i)


def kernel(x, L0_conv_w_qkv, L0_conv_b_qkv, L0_conv_w_proj, L0_conv_b_proj, L0_conv_rel_table,
           L0_ffn_router_w, L0_ffn_router_b, L0_ffn_expert_w, L0_ffn_expert_b):
    import ml_dtypes
    import concourse.bacc as bacc
    from concourse.bass_utils import run_bass_kernel_spmd

    given = [np.asarray(t) for t in (L0_conv_w_qkv, L0_conv_b_qkv, L0_conv_w_proj, L0_conv_b_proj, L0_ffn_router_w,
                                     L0_ffn_router_b, L0_ffn_expert_w, L0_ffn_expert_b)]
    constants = shape_constants()
    arrays = {
        "x": np.ascontiguousarray(x),
        "weights": laid_out_weights(*given),
        "rel_table": np.ascontiguousarray(np.asarray(L0_conv_rel_table)[::-1]),
        "consts": side_by_side(constants, CONST_COLS),
        "consts_bf16": side_by_side(constants, CONST_BF16_COLS).astype(ml_dtypes.bfloat16),
    }
    nc = bacc.Bacc("TRN2", target_bir_lowering=False, num_devices=1)
    args = [nc.dram_tensor(name, a.shape, mybir.dt.from_np(a.dtype), kind="ExternalInput").ap()
            for name, a in arrays.items()]
    args.append(nc.dram_tensor("out", (IMAGES, SIDE, SIDE, C), F32, kind="ExternalOutput").ap())
    metaformer_block(nc, *args)
    return run_bass_kernel_spmd(nc, [arrays], core_ids=[0]).results[0]["out"]
```

```python
from contextlib import ExitStack

import numpy as np

import concourse.bass as bass
from concourse import mybir

F32 = mybir.dt.float32
F32R = mybir.dt.float32r
BF16 = mybir.dt.bfloat16
ALU = mybir.AluOpType
ACT = mybir.ActivationFunctionType
AX = mybir.AxisListType.X

IMAGES, SIDE, C = 16, 56, 32
WS, SHIFT, HEADS = 7, 3, 4
D = C // HEADS
SCALE = float(D) ** -0.5
N = WS * WS
E = 8
UNITS = 16
ROWS = 2 * SIDE
A = 4
Q = 16
TOK = A * WS
COLS = Q * N
HALF = COLS // 2
EVEN = N + 1
PAD = 64
SLOT = 32
HN = HEADS * N
GROUPS = 4
LN1_EPS, LN2_EPS = 1e-6, 1e-5
BELOW_ALL = -3.0e38
ROW_CUTS = ((0, 48), (48, 53), (53, 56))
COL_CUTS = ((0, 25), (25, 28))
TRANSFERS = 2 * len(ROW_CUTS) * len(COL_CUTS)

PRE_FILLS = 12
TOKEN_FILLS = 5
WEIGHT_FILLS = 19
AHEAD = 6
MIX_PRODUCTS = (5, 9, 13, 16)
SHIFT_STEP = 2
TOP2_STEPS = 22
PROBS_STEP = 15
GAP_STEP = 9

NORM1 = ("load", "norm1_center", "norm1_square", "norm1_scale")
PRE_ORDER = ("keep", "xt", "xt", "prepare", "qk", "qk", "qk", "qk", "place", "v", "v", "ob", "ob", "obt", "obt")
LATE = ("replicate", "wt", "mix", "mix_drain", "final", "store")
SIDE_TASKS = {
    (0, 0): [("replicate", 0)], (0, 1): [("xt", 0)], (1, 2): [("wt", 0), ("y", 0), ("y", 1), ("back", 0)],
    (2, 0): [("back", 1)], (2, 1): [("keep", 0), ("xt", 1), ("load", 0)], (2, 2): [("qk", 0), ("norm2_center", 0)],
    (3, 0): [("norm2_square", 0)], (3, 1): [("qk", 1)], (3, 2): [("place", 0)],
    (4, 1): [("mix", 0), ("mix", 1), ("qk", 2)], (4, 2): [("norm2_scale", 0)], (5, 0): [("mix", 2)],
    (5, 1): [("qk", 3)], (6, 0): [("mix", 3), ("v", 0)], (6, 1): [("mix", 4)],
    (6, 2): [("mix", 5), ("mix", 6), ("mix", 7)], (7, 0): [("mix", 8)], (7, 1): [("mix", 9)],
    (7, 2): [("norm1_center", 0), ("mix_drain", 0), ("mix", 10)], (8, 1): [("x2t", 0), ("mix", 11), ("x2t", 1)],
    (8, 2): [("mix", 12)], (9, 0): [("router", 0)], (9, 1): [("norm1_square", 0), ("mix", 13)],
    (10, 0): [("v", 1), ("top2", 0), ("norm1_scale", 0), ("mix", 14)],
    (10, 2): [("mix", 15), ("top2", 1), ("top2", 2)], (11, 1): [("ob", 0)],
    (12, 0): [("mix", 16), ("top2_exp", 0), ("top2", 3)], (13, 1): [("top2", 4), ("mix_drain", 1), ("ob", 1)],
    (14, 0): [("top2", 5)], (14, 1): [("final", 0)], (14, 2): [("final", 1), ("obt", 0), ("top2", 6)],
    (15, 0): [("store", 0)], (15, 1): [("obt", 1), ("top2", 7)],
}


PROLOGUE = tuple((0, name) for name in NORM1 + ("keep",)) + ((1, "load"),) + tuple(
    (0, name) for name in ("xt", "xt", "prepare", "qk", "qk", "qk", "qk", "place", "v", "v")) + (
    (1, "norm1_center"), (0, "ob"), (0, "ob"), (1, "norm1_square"), (0, "obt"), (0, "obt"), (1, "norm1_scale")) + tuple(
    (0, "maximum") for _ in range(AHEAD))
TAIL = ((1, 1), (0, 3), (1, 1), (0, 1), (1, 1), (0, 2), (1, 1), (0, 1), (1, 1), (0, 5), (1, 1), (0, 6), (1, 1),
        (0, 5), (1, 4), (0, 1), (1, 8), (2, 24))




class Unit:

    def __init__(self, n, slab, par, number=None):
        self.n, self.slab, self.par = n, slab, par
        self.number = number

    def has_before(self, back):
        return self.number is None or self.number >= back

    def has_after(self):
        return self.number is None or self.number < UNITS - 1

    def after(self):
        return Unit(self.n + 1, None, None)

    def before(self, back):
        return Unit(self.n - back, None, None)


def fixed(n):
    return Unit(n, n // 2, n % 2, n)


def in_loop(it, offset):
    return Unit(it * 2 + offset, it + offset // 2, offset % 2)


def macro_step(older, post, att, ahead, next_unit):
    def side(place):
        for name, i in SIDE_TASKS.get(place, ()):
            unit = (next_unit if name in NORM1 else ahead if name in PRE_ORDER else
                    older if name in LATE else post)
            if unit is not None:
                yield name, unit, i

    for s in range(Q):
        yield "scores", att, s
        yield from side((s, 0))
        unit, q = (att, s + AHEAD) if s + AHEAD < Q else (ahead, s + AHEAD - Q)
        if unit is not None:
            yield "maximum", unit, q
            if q % 4 == 3:
                yield "split", unit, q // 4
        if s % 4 == 1:
            unit = att if s > 1 else post
            if unit is not None:
                yield "invert", unit, 2 * ((s // 4 - 1) % GROUPS) + 1
        yield from side((s, 1))
        yield "pv", att, s
        if s % 4 == SHIFT_STEP:
            g = (s // 4 + 1) % GROUPS
            if g or ahead is not None:
                yield "shift", att if g else ahead, g
        if s % 4 == 0:
            unit = att if s else post
            if unit is not None:
                yield "spread_sums", unit, (s // 4 - 1) % GROUPS
                yield "invert", unit, 2 * ((s // 4 - 1) % GROUPS)
        yield from side((s, 2))
        if s % 4 == 3:
            yield "pv_drain", att, s // 4


def program(eng):
    unit = [fixed(n) for n in range(UNITS)] + [None, None]
    seen = []
    for n, name in PROLOGUE:
        k = seen.count((n, name))
        seen.append((n, name))
        yield name, unit[n], k
        if name == "maximum" and k == 3:
            yield "split", unit[0], 0
    yield "shift", unit[0], 0
    yield from macro_step(None, None, *unit[0:3])
    yield from macro_step(None, *unit[0:4])
    yield from macro_step(*unit[0:5])
    yield from macro_step(*unit[1:6])
    with eng.Fori(0, (UNITS - 6) // 2) as it:
        near = [in_loop(it, 2 + k) for k in range(6)]
        yield from macro_step(*near[0:5])
        yield from macro_step(*near[1:6])
    yield from macro_step(*unit[UNITS - 4:UNITS + 1])
    yield from macro_step(*unit[UNITS - 3:UNITS + 2])
    tasks = [task for place in sorted(SIDE_TASKS) for task in SIDE_TASKS[place]]
    yield "spread_sums", unit[UNITS - 1], GROUPS - 1
    yield "invert", unit[UNITS - 1], 2 * GROUPS - 2
    yield "invert", unit[UNITS - 1], 2 * GROUPS - 1
    late = [task for task in tasks if task[0] in LATE]
    rest = [task for task in tasks if task[0] not in NORM1 + PRE_ORDER + LATE]
    chains = [[(name, unit[UNITS - 2], i) for name, i in late], [(name, unit[UNITS - 1], i) for name, i in rest],
              [(name, unit[UNITS - 1], i) for name, i in late]]
    for chain, count in TAIL:
        for _ in range(count):
            yield chains[chain].pop(0)
    assert not any(chains)


def shape_constants():
    jj, ii = np.arange(N) // WS, np.arange(N) % WS
    late = lambda t: (t >= WS - SHIFT).astype(int)
    mask = np.zeros((128, 4, PAD), np.float32)
    for kind in range(4):
        for g in range(2):
            region = late(ii) * (kind & 1) + 2 * late(jj) * ((kind >> 1) & g)
            mask[PAD * g:PAD * g + N, kind, :N] = np.where(region[:, None] != region[None, :], -100.0, 0.0)
    shift_sel = np.zeros((128, 4, 2, 2, PAD), np.float32)
    for part in range(2):
        for q in range(4):
            for a in range(A):
                shift_sel[16 * part + 4 * q + a, q, a // 2, a % 2, :N] = 1.0
    weight_sel = np.zeros((96, 2, A, 4, C), np.float32)
    for part in range(3):
        for a in range(A):
            for e in range(E):
                weight_sel[32 * part + 8 * a + e, e // 4, a, e % 4, :] = 1.0
    first3 = np.zeros((128, 128), np.float32)
    first3[:3] = 1.0
    rank = np.tile(np.arange(E, 0, -1, dtype=np.float32), (128, 1))
    return {
        "ident": np.eye(128, dtype=np.float32), "mask": mask, "rank": rank,
        "identb": np.eye(128, dtype=np.float32), "first3": first3, "shift_sel": shift_sel,
        "weight_sel": weight_sel,
    }


CONST_COLS = {"ident": 128, "mask": 4 * PAD, "rank": E}
CONST_BF16_COLS = {"identb": 128, "first3": 128, "shift_sel": 4 * 2 * 128, "weight_sel": E * 128}
WEIGHT_COLS = {"wq": 128, "wk": 128, "biases": 4, "wv": 4 * C, "w_proj_o": 2 * C, "w_proj_b": 4 * 128,
               "wr": A * E, "rb": E, "bv_raw": C, "eb_raw": 128, "we": 2 * C}


def side_by_side(parts, cols):
    whole = np.zeros((128, sum(cols.values())), np.float32)
    c0 = 0
    for name, n in cols.items():
        flat = parts[name].reshape(parts[name].shape[0], n)
        whole[:flat.shape[0], c0:c0 + n] = flat
        c0 += n
    return whole


def laid_out_weights(w_qkv, b_qkv, w_proj, b_proj, router_w, router_b, expert_w, expert_b):
    zeros = lambda *shape: np.zeros(shape, np.float32)
    wq, wk = zeros(A, C, A, C), zeros(A, C, A, C)
    wv = zeros(A, C, 2, 2, C)
    w_proj_o = zeros(HEADS, 4, D, 2, C)
    w_proj_b = zeros(2, 2, A, D, 2, 2, A, C)
    wr = zeros(A, C, A, E)
    we = expert_w.reshape(2, 4, C, C).transpose(1, 2, 0, 3)
    biases = zeros(A, C, 4)
    eb_raw = zeros(3, A, E, A, C)
    for a in range(A):
        wq[a, :, a, :] = w_qkv[:, 0:C]
        wk[a, :, a, :] = w_qkv[:, C:2 * C]
        wv[a, :, a % 2, a // 2, :] = w_qkv[:, 2 * C:3 * C]
        wr[a, :, a, :] = router_w
        eb_raw[:, a, :, a, :] = expert_b
        biases[a, :, 0], biases[a, :, 1], biases[a, :, 2] = b_qkv[0:C], b_qkv[C:2 * C], b_proj
        for b in range(2):
            for h in range(HEADS):
                w_proj_b[b, h % 2, a, :, b, h // 2, a, :] = w_proj[D * h:D * h + D]
    for g in range(2):
        for h in range(HEADS):
            w_proj_o[h, g, :, g, :] = w_proj[D * h:D * h + D]
    rows = lambda t, n: np.ascontiguousarray(t).reshape(n, -1)
    return side_by_side({
        "wq": rows(wq, 128), "wk": rows(wk, 128), "biases": rows(biases, 128), "wv": rows(wv, 128),
        "w_proj_o": rows(w_proj_o, 128), "w_proj_b": rows(w_proj_b, 128), "wr": rows(wr, 128),
        "rb": np.broadcast_to(router_b, (128, E)), "bv_raw": np.broadcast_to(b_qkv[2 * C:], (3, C)),
        "eb_raw": rows(eb_raw, 96), "we": rows(we, 128),
    }, WEIGHT_COLS)


def metaformer_block(nc, x, weights, rel_table, consts, consts_bf16, out):
    with ExitStack() as ctx:
        def sb(name, shape, dt=F32):
            return ctx.enter_context(nc.sbuf_tensor(name, shape, dt))

        def bank(name):
            return ctx.enter_context(nc.psum_tensor(name, [128, 512], F32))

        weight_tile = sb("weight_tile", [128, sum(WEIGHT_COLS.values())])
        const_tile = sb("const_tile", [128, sum(CONST_COLS.values())])
        const_bf16_tile = sb("const_bf16_tile", [128, sum(CONST_BF16_COLS.values())], BF16)
        part = {}
        for tile, cols in ((weight_tile, WEIGHT_COLS), (const_tile, CONST_COLS), (const_bf16_tile, CONST_BF16_COLS)):
            c0 = 0
            for name, n in cols.items():
                part[name] = tile[:, c0:c0 + n]
                c0 += n
        ident, identb, first3 = part["ident"], part["identb"], part["first3"]
        mask = part["mask"].rearrange("p (k n) -> p k n", k=4)
        rank = part["rank"][0:ROWS, :]
        shift_sel = part["shift_sel"].rearrange("p (q s m) -> p q s m", q=4, s=2)
        weight_sel = part["weight_sel"][0:96, :].rearrange("p (s a m) -> p s a m", s=2, a=A)
        wq, wk = part["wq"], part["wk"]
        wv = part["wv"].rearrange("p (g s c) -> p g s c", g=2, s=2)
        w_proj_o = part["w_proj_o"].rearrange("p (g c) -> p g c", g=2)
        w_proj_b = part["w_proj_b"].rearrange("p (b s a c) -> p b s a c", b=2, s=2, a=A)
        wr = part["wr"].rearrange("p (a e) -> p a e", a=A)
        we = part["we"].rearrange("p (s c) -> p s c", s=2)
        biases = part["biases"]
        rb = part["rb"][0:ROWS, :]
        eb_raw, bv_raw = part["eb_raw"][0:96, :], part["bv_raw"][0:3, :]
        rel_raw = sb("rel_raw", [128, WS, WS, HEADS])
        bt = sb("bt", [128, HEADS, 4, PAD])
        eb_rest = sb("eb_rest", [96, 128])
        eb = sb("eb", [96, 3, 128], BF16)
        bv_rest = sb("bv_rest", [3, C])
        bv_parts = sb("bv_parts", [3, 3, C], BF16)
        bv_rows = sb("bv_rows", [3, 2, C])
        bv = sb("bv", [128, Q, C], BF16)
        minus_half, minus_1_c, plus_1_c, eps1, eps2 = (
            sb(n, [ROWS, TOK]) for n in ("minus_half", "minus_1_c", "plus_1_c", "eps1", "eps2"))

        xin = sb("xin", [ROWS, A, WS, C])
        x_kept = [sb(f"x_kept{i}", [ROWS, A, WS, C]) for i in range(2)]
        xc1 = sb("xc1", [ROWS, WS, A, C])
        sq = sb("sq", [ROWS, WS, A, C])
        st1 = sb("st1", [ROWS, 5, TOK])
        xt = sb("xt", [128, Q, WS, WS])
        qp, kp = sb("qp", [128, Q, N]), sb("kp", [128, Q, PAD])
        qbd = [sb(f"qbd{i}", [128, Q, HEADS, N]) for i in range(2)]
        kz = [sb(f"kz{i}", [128, Q, A, PAD]) for i in range(2)]
        vb = [sb(f"vb{i}", [128, Q, 2, HEADS, SLOT]) for i in range(2)]
        obs = sb("obs", [128, 8, 2, 2, 2, 16])
        obt = [sb(f"obt{i}", [128, 2, 8, N]) for i in range(2)]
        mx = [sb(f"mx{i}", [2 * N, 2, 4, A]) for i in range(2)]
        ms = [sb(f"ms{i}", [2 * N, 2, 2, 16], BF16) for i in range(2)]
        mr = [sb(f"mr{i}", [128, HN], BF16) for i in range(2)]
        pt = [sb(f"pt{i}", [128, 2, HEADS, N]) for i in range(2)]
        oe = [sb(f"oe{i}", [128, 4, 2, N]) for i in range(2)]
        rz = [sb(f"rz{i}", [128, 4, 2, N]) for i in range(2)]
        on = sb("on", [128, 2, Q, N])
        waited = sb("waited", [1, 1])
        ym = sb("ym", [128, WS, ROWS])
        x2 = [sb(f"x2_{i}", [ROWS, A, WS, C]) for i in range(2)]
        xc2 = sb("xc2", [ROWS, WS, A, C])
        st2 = sb("st2", [ROWS, 5, TOK])
        x2t = sb("x2t", [128, COLS])
        logits, pick1, pick2 = (sb(n, [ROWS, TOK, E]) for n in ("logits", "pick1", "pick2"))
        tmp, mixw, mix_rest = (sb(n, [ROWS, TOK, E]) for n in ("tmp", "mixw", "mix_rest"))
        top = sb("top", [ROWS, 8, TOK])
        w_parts = sb("w_parts", [ROWS, WS, 3, A * E], BF16)
        wt = sb("wt", [96, COLS], BF16)
        x4 = sb("x4", [128, A, COLS])
        zt = sb("zt", [128, A, HALF])

        ps_max, ps_scores, ps_pv = bank("ps_max"), bank("ps_scores"), bank("ps_pv")
        ps_pre, ps_acc = bank("ps_pre"), bank("ps_acc")
        ps_token, ps_weight = bank("ps_token"), [bank(f"ps_weight{i}") for i in range(2)]

        per_unit = {
            "x_loaded": 16 * TRANSFERS, "x_kept_ready": 16, "out_stored": 16 * TRANSFERS,
            "sum1": 1, "mean1": 1, "centered1": 1, "squared1": 1, "sqsum1": 1, "meansq1": 1, "var1": 1,
            "rstd1": 1, "normed1": 1,
            "sum2": 1, "mean2": 1, "centered2": 1, "squared2": 1, "sqsum2": 1, "meansq2": 1, "var2": 1,
            "rstd2": 1, "normed2": 1,
            "pre_filled": PRE_FILLS, "pre_drained": PRE_FILLS,
            "q_placed": 16 * A * HEADS, "k_placed": 16 * A,
            "max_filled": Q, "max_taken": Q, "shift_rounded": GROUPS, "shift_split": GROUPS,
            "shift_turned": GROUPS, "shift_rows_ready": GROUPS,
            "scores_filled": Q, "probs_ready": Q, "pv_done": Q, "pv_drained": GROUPS,
            "sums_spread": GROUPS, "sums_inverted": 2 * GROUPS, "o_normed": 2 * GROUPS,
            "projected": 2, "y_drained": 2, "sum_drained": 2,
            "token_filled": TOKEN_FILLS, "token_drained": TOKEN_FILLS,
            "weight_filled": WEIGHT_FILLS, "weight_drained": WEIGHT_FILLS,
            "top2_step": TOP2_STEPS, "gap_exp": 1, "x4_first": 16 * A, "x4_ready": 16 * 3, "mixed": 4,
        }
        def sem(name):
            return ctx.enter_context(nc.semaphore(name))

        x_loaded = sem("x_loaded")
        x_kept_ready = sem("x_kept_ready")
        out_stored = sem("out_stored")
        sum1 = sem("sum1")
        mean1 = sem("mean1")
        centered1 = sem("centered1")
        squared1 = sem("squared1")
        sqsum1 = sem("sqsum1")
        meansq1 = sem("meansq1")
        var1 = sem("var1")
        rstd1 = sem("rstd1")
        normed1 = sem("normed1")
        sum2 = sem("sum2")
        mean2 = sem("mean2")
        centered2 = sem("centered2")
        squared2 = sem("squared2")
        sqsum2 = sem("sqsum2")
        meansq2 = sem("meansq2")
        var2 = sem("var2")
        rstd2 = sem("rstd2")
        normed2 = sem("normed2")
        pre_filled = sem("pre_filled")
        pre_drained = sem("pre_drained")
        q_placed = sem("q_placed")
        k_placed = sem("k_placed")
        max_filled = sem("max_filled")
        max_taken = sem("max_taken")
        shift_rounded = sem("shift_rounded")
        shift_split = sem("shift_split")
        shift_turned = sem("shift_turned")
        shift_rows_ready = sem("shift_rows_ready")
        scores_filled = sem("scores_filled")
        probs_ready = sem("probs_ready")
        pv_done = sem("pv_done")
        pv_drained = sem("pv_drained")
        sums_spread = sem("sums_spread")
        sums_inverted = sem("sums_inverted")
        o_normed = sem("o_normed")
        projected = sem("projected")
        y_drained = sem("y_drained")
        sum_drained = sem("sum_drained")
        token_filled = sem("token_filled")
        token_drained = sem("token_drained")
        weight_filled = sem("weight_filled")
        weight_drained = sem("weight_drained")
        top2_step = sem("top2_step")
        gap_exp = sem("gap_exp")
        x4_first = sem("x4_first")
        x4_ready = sem("x4_ready")
        mixed = sem("mixed")
        zeroed = sem("zeroed")
        zeroed_even = sem("zeroed_even")
        zeroed_odd = sem("zeroed_odd")
        odd_v_zeroed = sem("odd_v_zeroed")
        consts_loaded = sem("consts_loaded")
        weights_loaded = sem("weights_loaded")
        rel_zeroed = sem("rel_zeroed")
        rel_loaded = sem("rel_loaded")
        weight_step = sem("weight_step")
        weights_ready = sem("weights_ready")

        def upto(name, unit, i=None):
            k = per_unit[name]
            return unit.n * k + (k if i is None else i + 1)

        def over(s, n):
            return s.unsqueeze(2).to_broadcast([s.shape[0], s.shape[1], n])

        def pieces(dram, tile, unit):
            view = tile.rearrange("p j k c -> p (j k) c")
            for b in range(2):
                for r0, r1 in ROW_CUTS:
                    for c0, c1 in COL_CUTS:
                        h = (r0 + SHIFT) % SIDE
                        w = (TOK * unit.par + c0 + SHIFT) % SIDE
                        yield (view[SIDE * b + r0:SIDE * b + r1, c0:c1, :],
                               dram[unit.slab * 2 + b, h:h + r1 - r0, w:w + c1 - c0, :])

        def rel_loads():
            line = (2 * WS - 1) * HEADS
            for g in range(2):
                for mj in range(WS):
                    row = PAD * g + mj * WS
                    yield (rel_raw[row:row + WS, :, :, :].rearrange("p i j h -> p i (j h)"),
                           bass.AP(rel_table.tensor, rel_table.offset + mj * HEADS, [[line, WS], [line, WS], [1, WS * HEADS]]))

        rel_list = list(rel_loads())

        def pre_bank(v, fill):
            return ps_token if v.number == 0 and fill % 2 else ps_pre

        def pre_free(v, fill):
            operands = (-1, -1, 1, 1, 1, 1, 1, 1, 7, 7, 9, 9)[fill]
            return max(operands, fill - 2) if v.number == 0 else fill - 1

        def max_bank(u, q):
            return ps_token if u.number == 0 and q < AHEAD and q % 2 else ps_max

        block = ctx.enter_context(nc.Block())

        @block.sync
        def _(sp):
            def load(v, _):
                if v.has_before(1):
                    sp.wait_ge(centered1, upto("centered1", v.before(1)))
                    sp.wait_ge(x_kept_ready, upto("x_kept_ready", v.before(1)))
                for tile, dram in pieces(x, xin, v):
                    sp.dma_start(tile, dram).then_inc(x_loaded, 16)

            def keep(v, _):
                sp.wait_ge(x_loaded, upto("x_loaded", v))
                if v.has_before(2):
                    sp.wait_ge(token_drained, upto("token_drained", v.before(2), 1))
                sp.dma_start(x_kept[v.par].rearrange("p j k c -> p (j k c)"),
                             xin.rearrange("p j k c -> p (j k c)")).then_inc(x_kept_ready, 16)

            def place(v, _):
                sp.wait_ge(pre_drained, upto("pre_drained", v, 3))
                if v.has_before(2):
                    sp.wait_ge(scores_filled, upto("scores_filled", v.before(2)))
                if v.number == 0:
                    sp.wait_ge(zeroed, 1)
                    sp.wait_ge(zeroed_even, 1)
                if v.number == 1:
                    sp.wait_ge(zeroed_odd, 1)
                for h in range(HEADS):
                    for a in range(A):
                        r = slice(C * a + D * h, C * a + D * h + D)
                        sp.dma_start(qbd[v.par][r, :, h, :], qp[r, :, :]).then_inc(q_placed, 16)
                sp.wait_ge(pre_drained, upto("pre_drained", v, 5))
                for a in range(A):
                    r = slice(C * a, C * a + C)
                    sp.dma_start(kz[v.par][r, :, a, :], kp[r, :, :]).then_inc(k_placed, 16)

            def replicate(w, _):
                sp.wait_ge(token_drained, upto("token_drained", w, 3))
                if w.has_before(1):
                    sp.wait_ge(mixed, upto("mixed", w.before(1)))
                for a in range(A):
                    sp.dma_start(x4[0:C, a, :], x2t[C * a:C * a + C, :]).then_inc(x4_first, 16)
                sp.wait_ge(x4_first, upto("x4_first", w))
                for e in range(1, 4):
                    sp.dma_start(x4[C * e:C * e + C, :, :].rearrange("p a t -> p (a t)"),
                                 x4[0:C, :, :].rearrange("p a t -> p (a t)")).then_inc(x4_ready, 16)

            def store(w, _):
                sp.wait_ge(weight_drained, upto("weight_drained", w))
                for tile, dram in pieces(out, x2[w.par], w):
                    sp.dma_start(dram, tile).then_inc(out_stored, 16)

            for step, unit, i in program(sp):
                if step == "load":
                    load(unit, i)
                    if unit.number == 0:
                        sp.wait_ge(rel_zeroed, 1)
                        for dst, src in rel_list:
                            sp.dma_start(dst, src).then_inc(rel_loaded, 16)
                elif step == "keep":
                    keep(unit, i)
                elif step == "place":
                    place(unit, i)
                elif step == "replicate":
                    replicate(unit, i)
                elif step == "store":
                    store(unit, i)
            sp.wait_ge(out_stored, UNITS * per_unit["out_stored"])

        @block.gpsimd
        def _(pool):
            def norm1_center(v, _):
                pool.wait_ge(sum1, upto("sum1", v))
                nc.gpsimd.tensor_tensor(st1[:, 1, :], st1[:, 0, :], minus_1_c[:, :], ALU.mult).then_inc(mean1, 1)
                pool.wait_ge(mean1, upto("mean1", v))
                if v.has_before(1):
                    pool.wait_ge(pre_filled, upto("pre_filled", v.before(1), 1))
                nc.gpsimd.tensor_tensor(
                    xc1[:, :, :, :], xin.rearrange("p j k c -> p k j c"),
                    st1[:, 1, :].rearrange("p (j k) -> p k j", j=A).unsqueeze(3).to_broadcast([ROWS, WS, A, C]),
                    ALU.add).then_inc(centered1, 1)

            def norm1_scale(v, _):
                pool.wait_ge(sqsum1, upto("sqsum1", v))
                nc.gpsimd.tensor_tensor(st1[:, 3, :], st1[:, 2, :], plus_1_c[:, :], ALU.mult).then_inc(meansq1, 1)
                pool.wait_ge(meansq1, upto("meansq1", v))
                nc.gpsimd.tensor_tensor(st1[:, 3, :], st1[:, 3, :], eps1[:, :], ALU.add).then_inc(var1, 1)
                pool.wait_ge(var1, upto("var1", v))
                nc.gpsimd.tensor_tensor(st1[:, 4, :], st1[:, 3, :], minus_half[:, :], ALU.pow).then_inc(rstd1, 1)
                pool.wait_ge(rstd1, upto("rstd1", v))
                pool.wait_ge(squared1, upto("squared1", v))
                xc = xc1[:, :, :, :].rearrange("p k j c -> p (k j) c")
                nc.gpsimd.tensor_tensor(xc, xc, over(st1[:, 4, :], C), ALU.mult).then_inc(normed1, 1)

            def norm2_center(w, _):
                pool.wait_ge(sum2, upto("sum2", w))
                nc.gpsimd.tensor_tensor(st2[:, 1, :], st2[:, 0, :], minus_1_c[:, :], ALU.mult).then_inc(mean2, 1)
                pool.wait_ge(mean2, upto("mean2", w))
                if w.has_before(1):
                    pool.wait_ge(token_filled, upto("token_filled", w.before(1), 3))
                nc.gpsimd.tensor_tensor(
                    xc2[:, :, :, :], x2[w.par].rearrange("p j k c -> p k j c"),
                    st2[:, 1, :].rearrange("p (j k) -> p k j", j=A).unsqueeze(3).to_broadcast([ROWS, WS, A, C]),
                    ALU.add).then_inc(centered2, 1)

            def norm2_scale(w, _):
                pool.wait_ge(sqsum2, upto("sqsum2", w))
                nc.gpsimd.tensor_tensor(st2[:, 3, :], st2[:, 2, :], plus_1_c[:, :], ALU.mult).then_inc(meansq2, 1)
                pool.wait_ge(meansq2, upto("meansq2", w))
                nc.gpsimd.tensor_tensor(st2[:, 3, :], st2[:, 3, :], eps2[:, :], ALU.add).then_inc(var2, 1)
                pool.wait_ge(var2, upto("var2", w))
                nc.gpsimd.tensor_tensor(st2[:, 4, :], st2[:, 3, :], minus_half[:, :], ALU.pow).then_inc(rstd2, 1)
                pool.wait_ge(rstd2, upto("rstd2", w))
                pool.wait_ge(squared2, upto("squared2", w))
                xc = xc2[:, :, :, :].rearrange("p k j c -> p (k j) c")
                nc.gpsimd.tensor_tensor(xc, xc, over(st2[:, 4, :], C), ALU.mult).then_inc(normed2, 1)

            def invert(u, i):
                g, half = divmod(i, 2)
                quads = slice(2 * half, 2 * half + 2)
                pool.wait_ge(sums_inverted, upto("sums_inverted", u, i))
                if i == 0:
                    if u.has_before(1):
                        pool.wait_ge(projected, upto("projected", u.before(1), 1))
                nc.gpsimd.tensor_tensor(
                    on[:, :, 4 * g + 2 * half:4 * g + 2 * half + 2, :], oe[g % 2][:, quads, :, :].rearrange("p q s n -> p s q n"),
                    rz[g % 2][:, quads, :, :].rearrange("p q s n -> p s q n"), ALU.mult).then_inc(o_normed, 1)

            at = [0]

            def link(ins, w):
                ins.then_inc(top2_step, 1)
                pool.wait_ge(top2_step, upto("top2_step", w, at[0]))
                at[0] += 1

            def top2(w, i):
                tt = nc.gpsimd.tensor_tensor
                if i == 5:
                    at[0] = PROBS_STEP
                    pool.wait_ge(top2_step, upto("top2_step", w, PROBS_STEP - 1))
                    link(tt(pick1[:, :, :], pick1[:, :, :], over(top[:, 5, :], E), ALU.mult), w)
                    link(tt(pick2[:, :, :], pick2[:, :, :], over(top[:, 4, :], E), ALU.mult), w)
                    link(tt(mixw[:, :, :], pick1[:, :, :], pick2[:, :, :], ALU.add), w)
                    return
                parts = [w_parts[:, :, k, :] for k in range(3)]
                view = lambda t: t[:, :, :].rearrange("p (k j) e -> p k (j e)", j=A)
                whole, rest = view(mixw), view(mix_rest)
                if i == 6:
                    if w.has_before(1):
                        pool.wait_ge(weight_filled, upto("weight_filled", w.before(1), 0))
                    link(tt(parts[0], view(pick1), view(pick2), ALU.add), w)
                    link(tt(rest, whole, parts[0], ALU.subtract), w)
                else:
                    link(tt(parts[1], whole, parts[0], ALU.subtract), w)
                    link(tt(parts[2], rest, parts[1], ALU.subtract), w)
                    assert at[0] == TOP2_STEPS, at[0]

            for tile, value in ((minus_half, -0.5), (minus_1_c, -1.0 / C), (plus_1_c, 1.0 / C), (eps1, LN1_EPS),
                                (eps2, LN2_EPS)):
                nc.gpsimd.memset(tile[:, :], value)
            nc.gpsimd.memset(qbd[0][:, :, :, :], 0.0)
            nc.gpsimd.memset(kz[0][:, :, :, :], 0.0).then_inc(zeroed_even, 1)
            pool.wait_ge(zeroed_even, 1)
            for step, unit, i in program(pool):
                if step == "norm1_center":
                    norm1_center(unit, i)
                elif step == "norm1_scale":
                    norm1_scale(unit, i)
                elif step == "norm2_center":
                    norm2_center(unit, i)
                elif step == "norm2_scale":
                    norm2_scale(unit, i)
                elif step == "invert":
                    invert(unit, i)
                elif step == "top2" and i >= 5:
                    top2(unit, i)
                elif step == "place" and unit.number == 0:
                    nc.gpsimd.memset(qbd[1][:, :, :, :], 0.0)
                    nc.gpsimd.memset(kz[1][:, :, :, :], 0.0)
                    nc.gpsimd.memset(mr[1][:, :], 0.0).then_inc(zeroed_odd, 1)

        @block.scalar
        def _(act):
            def norm1_square(v, _):
                if v.has_before(3):
                    act.wait_ge(sqsum2, upto("sqsum2", v.before(3)))
                else:
                    if v.has_before(1):
                        act.wait_ge(sqsum1, upto("sqsum1", v.before(1)))
                act.wait_ge(centered1, upto("centered1", v))
                nc.scalar.activation(sq[:, :, :, :], xc1[:, :, :, :], ACT.Square).then_inc(squared1, 1)

            def norm2_square(w, _):
                if w.number is None or w.number + 2 < UNITS:
                    act.wait_ge(sqsum1, upto("sqsum1", Unit(w.n + 2, None, None)))
                else:
                    act.wait_ge(sqsum2, upto("sqsum2", w.before(1)))
                act.wait_ge(centered2, upto("centered2", w))
                nc.scalar.activation(sq[:, :, :, :], xc2[:, :, :, :], ACT.Square).then_inc(squared2, 1)

            def xt_drain(v, i):
                act.wait_ge(pre_filled, upto("pre_filled", v, i))
                k0, k1 = (0, 4) if i == 0 else (4, 7)
                if i == 0:
                    if v.has_before(1):
                        act.wait_ge(pre_filled, upto("pre_filled", v.before(1), 7))
                nc.scalar.copy(xt[:, :, k0:k1, :].rearrange("p q k i -> p k q i"),
                                    pre_bank(v, i)[:, 0:(k1 - k0) * ROWS].rearrange("p (k q i) -> p k q i", q=Q, i=WS)).then_inc(pre_drained, 1)

            def qk_drain(v, i):
                act.wait_ge(pre_filled, upto("pre_filled", v, 2 + i))
                src = pre_bank(v, 2 + i)[:, 0:HALF].rearrange("p (q n) -> p q n", n=N)
                if i < 2:
                    if v.has_before(1):
                        act.wait_ge(q_placed, upto("q_placed", v.before(1)))
                    ins = nc.scalar.activation(qp[:, 8 * i:8 * i + 8, :], src, ACT.Identity,
                                               bias=biases[:, 3:4], scale=SCALE)
                else:
                    if v.has_before(1):
                        act.wait_ge(k_placed, upto("k_placed", v.before(1)))
                    ins = nc.scalar.activation(kp[:, 8 * (i - 2):8 * (i - 2) + 8, 0:N], src, ACT.Identity,
                                               bias=biases[:, 1:2])
                ins.then_inc(pre_drained, 1)

            def v_drain(v, i):
                act.wait_ge(pre_filled, upto("pre_filled", v, 6 + i))
                if v.has_before(2):
                    act.wait_ge(pv_done, upto("pv_done", v.before(2)))
                if v.number == 1:
                    act.wait_ge(odd_v_zeroed, 2)
                for g in range(2):
                    r = slice(PAD * g, PAD * g + N)
                    ins = nc.scalar.copy(
                        vb[v.par][r, 8 * i:8 * i + 8, :, :, D * g:D * g + D].rearrange("p q s h d -> p (q s h) d"),
                        pre_bank(v, 6 + i)[r, :].rearrange("p (t d) -> p t d", d=D))
                ins.then_inc(pre_drained, 1)

            def ob_drain(v, i):
                act.wait_ge(pre_filled, upto("pre_filled", v, 8 + i))
                if i == 0:
                    if v.has_before(1):
                        act.wait_ge(pre_filled, upto("pre_filled", v.before(1)))
                for p in range(2):
                    ins = nc.scalar.copy(obs[:, :, :, i, p, :].rearrange("p i b s -> p b i s"),
                                         pre_bank(v, 8 + i)[:, 256 * p:256 * p + 256].rearrange("p (b i s) -> p b i s", b=2, s=16))
                ins.then_inc(pre_drained, 1)

            def obt_drain(v, i):
                act.wait_ge(pre_filled, upto("pre_filled", v, 10 + i))
                if i == 0:
                    if v.has_before(2):
                        act.wait_ge(projected, upto("projected", v.before(2), 1))
                nc.scalar.copy(
                    obt[v.par][:, :, 4 * i:4 * i + 4, :].rearrange("p s i n -> p i s n"),
                    pre_bank(v, 10 + i)[:, :].rearrange("p (i s n) -> p i s n", s=2, n=PAD)[:, :, :, 0:N]).then_inc(pre_drained, 1)

            def shift_drain(u, g):
                act.wait_ge(shift_turned, upto("shift_turned", u, g))
                if g >= 2:
                    act.wait_ge(scores_filled, upto("scores_filled", u, 4 * (g - 2) + 3))
                else:
                    if u.has_before(1):
                        act.wait_ge(scores_filled, upto("scores_filled", u.before(1), 4 * (g + 2) + 3))
                if u.number == 0 and g == 1:
                    act.wait_ge(zeroed_odd, 1)
                nc.scalar.copy(mr[g % 2][0:32, :], ps_scores[0:32, 0:HN // 2].bitcast(BF16)).then_inc(shift_rows_ready, 1)

            def exponentials(u, q):
                act.wait_ge(scores_filled, upto("scores_filled", u, q))
                nc.scalar.activation(pt[q % 2][:, :, :, :].rearrange("p s h n -> p (s h n)"),
                                          ps_scores[:, 0:2 * HN], ACT.Exp).then_inc(probs_ready, 1)

            def pv_drain(u, g):
                act.wait_ge(pv_done, upto("pv_done", u, 4 * g + 3))
                if g >= 2:
                    act.wait_ge(o_normed, upto("o_normed", u, 2 * (g - 2) + 1))
                else:
                    if u.has_before(1):
                        act.wait_ge(o_normed, upto("o_normed", u.before(1), 2 * (g + 2) + 1))
                nc.scalar.copy(oe[g % 2][:, :, :, :].rearrange("p q s n -> p (q s n)"), ps_pv[:, 0:HALF]).then_inc(pv_drained, 1)

            def y_drain(w, b):
                act.wait_ge(projected, upto("projected", w, b))
                if b == 0:
                    if w.has_before(2):
                        act.wait_ge(weight_filled, upto("weight_filled", w.before(2)))
                    elif w.has_before(1):
                        act.wait_ge(token_filled, upto("token_filled", w.before(1), 1))
                nc.scalar.activation(
                    ym[:, :, SIDE * b:SIDE * b + SIDE].rearrange("p k (i j) -> p i k j", j=WS),
                    ps_acc[:, 0:HALF].rearrange("p (i k j) -> p i k j", k=WS, j=WS), ACT.Identity,
                    bias=biases[:, 2:3]).then_inc(y_drained, 1)

            def x2t_drain(w, i):
                act.wait_ge(token_filled, upto("token_filled", w, 2 + i))
                if i == 0:
                    if w.has_before(1):
                        act.wait_ge(x4_ready, upto("x4_ready", w.before(1)))
                c0, c1 = (0, 4 * ROWS) if i == 0 else (4 * ROWS, COLS)
                nc.scalar.copy(x2t[:, c0:c1], ps_token[:, 0:c1 - c0]).then_inc(token_drained, 1)

            def top2_exp(w, _):
                act.wait_ge(top2_step, upto("top2_step", w, GAP_STEP))
                nc.scalar.activation(top[:, 3, :], top[:, 2, :], ACT.Exp).then_inc(gap_exp, 1)

            def wt_drain(w, _):
                act.wait_ge(weight_filled, upto("weight_filled", w, 0))
                nc.scalar.copy(wt[:, :], ps_weight[0][0:96, 0:COLS // 2].bitcast(BF16)).then_inc(weight_drained, 1)

            def mix_drain(w, half):
                act.wait_ge(mixed, upto("mixed", w, 2 * half + 1))
                if half == 0:
                    if w.has_after():
                        act.wait_ge(token_filled, upto("token_filled", w.after(), 1))
                    else:
                        act.wait_ge(weight_filled, upto("weight_filled", w.before(1)))
                nc.scalar.copy(ym[:, :, :].rearrange("p k r -> p (k r)")[:, HALF * half:HALF * half + HALF],
                                    ps_acc[:, 0:HALF]).then_inc(sum_drained, 1)

            act.dma_start(const_tile[:, :], consts).then_inc(consts_loaded, 16)
            act.dma_start(weight_tile[:, :], weights).then_inc(weights_loaded, 16)
            act.dma_start(const_bf16_tile[:, :], consts_bf16).then_inc(weights_loaded, 16)
            for step, unit, i in program(act):
                if step == "norm1_square":
                    norm1_square(unit, i)
                elif step == "norm2_square":
                    norm2_square(unit, i)
                elif step == "prepare" and unit.number == 0:
                    act.wait_ge(weights_ready, 1)
                elif step == "xt":
                    xt_drain(unit, i)
                elif step == "qk":
                    qk_drain(unit, i)
                elif step == "v":
                    v_drain(unit, i)
                elif step == "ob":
                    ob_drain(unit, i)
                elif step == "obt":
                    obt_drain(unit, i)
                elif step == "shift":
                    shift_drain(unit, i)
                elif step == "scores":
                    exponentials(unit, i)
                elif step == "pv_drain":
                    pv_drain(unit, i)
                elif step == "y":
                    y_drain(unit, i)
                elif step == "x2t":
                    x2t_drain(unit, i)
                elif step == "top2_exp":
                    top2_exp(unit, i)
                elif step == "wt":
                    wt_drain(unit, i)
                elif step == "mix_drain":
                    mix_drain(unit, i)

        @block.vector
        def _(dve):
            def norm1_center(v, _):
                dve.wait_ge(x_loaded, upto("x_loaded", v))
                if v.has_before(1):
                    dve.wait_ge(centered1, upto("centered1", v.before(1)))
                nc.vector.tensor_reduce(st1[:, 0, :], xin.rearrange("p j k c -> p (j k) c"), AX, ALU.add).then_inc(sum1, 1)

            def norm1_scale(v, _):
                dve.wait_ge(squared1, upto("squared1", v))
                if v.has_before(1):
                    dve.wait_ge(normed1, upto("normed1", v.before(1)))
                nc.vector.tensor_reduce(st1[:, 2, :], sq[:, :, :, :].rearrange("p k j c -> p (k j) c"), AX, ALU.add).then_inc(sqsum1, 1)

            def norm2_center(w, _):
                dve.wait_ge(token_drained, upto("token_drained", w, 1))
                if w.has_before(1):
                    dve.wait_ge(centered2, upto("centered2", w.before(1)))
                nc.vector.tensor_reduce(st2[:, 0, :], x2[w.par].rearrange("p j k c -> p (j k) c"), AX, ALU.add).then_inc(sum2, 1)

            def norm2_scale(w, _):
                dve.wait_ge(squared2, upto("squared2", w))
                if w.has_before(1):
                    dve.wait_ge(normed2, upto("normed2", w.before(1)))
                nc.vector.tensor_reduce(st2[:, 2, :], sq[:, :, :, :].rearrange("p k j c -> p (k j) c"), AX, ALU.add).then_inc(sqsum2, 1)

            def maximum(u, q):
                dve.wait_ge(max_filled, upto("max_filled", u, q))
                nc.vector.tensor_reduce(
                    mx[(q // 4) % 2][:, :, q % 4, :],
                    max_bank(u, q)[0:2 * N, 0:2 * A * EVEN].rearrange("p (s a m) -> p s a m", s=2, a=A)[:, :, :, 0:N], AX, ALU.max).then_inc(max_taken, 1)

            def split(u, g):
                m = mx[g % 2].rearrange("p s q a -> p s (q a)")
                hi, lo = ms[g % 2][:, :, 0, :], ms[g % 2][:, :, 1, :]
                dve.wait_ge(max_taken, upto("max_taken", u, 4 * g + 3))
                if g >= 2:
                    dve.wait_ge(shift_turned, upto("shift_turned", u, g - 2))
                else:
                    if u.has_before(1):
                        dve.wait_ge(shift_turned, upto("shift_turned", u.before(1), g + 2))
                nc.vector.tensor_scalar(hi, m, -1.0, None, ALU.mult).then_inc(shift_rounded, 1)
                dve.wait_ge(shift_rounded, upto("shift_rounded", u, g))
                nc.vector.scalar_tensor_tensor(out=lo, in0=m, scalar=-1.0, in1=hi, op0=ALU.mult,
                                                    op1=ALU.subtract).then_inc(shift_split, 1)

            def spread_sums(u, g):
                dve.wait_ge(pv_drained, upto("pv_drained", u, g))
                if g >= 2:
                    dve.wait_ge(o_normed, upto("o_normed", u, 2 * (g - 2) + 1))
                else:
                    if u.has_before(1):
                        dve.wait_ge(o_normed, upto("o_normed", u.before(1), 2 * (g + 2) + 1))
                nc.vector.memset(waited[:, :], 0.0)
                nc.vector.stream_shuffle(rz[g % 2][:, :, :, :].rearrange("p q s n -> p (q s n)"),
                                         oe[g % 2][:, :, :, :].rearrange("p q s n -> p (q s n)"),
                                         [16 + k % 16 for k in range(SLOT)]).then_inc(sums_spread, 1)

            def invert(u, i):
                g, half = divmod(i, 2)
                if half == 0:
                    dve.wait_ge(sums_spread, upto("sums_spread", u, g))
                sums = rz[g % 2][:, 2 * half:2 * half + 2, :, :].rearrange("p q s n -> p (q s n)")
                nc.vector.reciprocal(sums, sums).then_inc(sums_inverted, 1)

            def residual(w, i):
                dve.wait_ge(token_filled, upto("token_filled", w, i))
                if i == 0:
                    dve.wait_ge(x_kept_ready, upto("x_kept_ready", w))
                k0, k1 = (0, 4) if i == 0 else (4, 7)
                if i == 0:
                    if w.has_before(2):
                        dve.wait_ge(out_stored, upto("out_stored", w.before(2)))
                nc.vector.tensor_tensor(
                    x2[w.par][:, :, k0:k1, :].rearrange("p j k c -> p k j c"),
                    ps_token[0:ROWS, 0:(k1 - k0) * 128].rearrange("p (k j c) -> p k j c", j=A, c=C),
                    x_kept[w.par][:, :, k0:k1, :].rearrange("p j k c -> p k j c"), ALU.add).then_inc(token_drained, 1)

            def router(w, _):
                dve.wait_ge(token_filled, upto("token_filled", w, 4))
                nc.vector.tensor_tensor(
                    logits[:, :, :], ps_token[0:ROWS, 0:TOK * E].rearrange("p (t e) -> p t e", e=E),
                    rb[:, :].unsqueeze(1).to_broadcast([ROWS, TOK, E]), ALU.add).then_inc(token_drained, 1)

            at = [0]

            def link(ins, w):
                ins.then_inc(top2_step, 1)
                dve.wait_ge(top2_step, upto("top2_step", w, at[0]))
                at[0] += 1

            def at_largest(w, vals, m):
                link(nc.vector.tensor_reduce(top[:, m, :], vals, AX, ALU.max), w)
                link(nc.vector.tensor_tensor(tmp[:, :, :], vals, over(top[:, m, :], E), ALU.is_equal), w)
                link(nc.vector.tensor_tensor(tmp[:, :, :], tmp[:, :, :],
                                             rank[:, :].unsqueeze(1).to_broadcast([ROWS, TOK, E]), ALU.mult), w)

            def first_of_them(w, r, pick):
                link(nc.vector.tensor_reduce(top[:, r, :], tmp[:, :, :], AX, ALU.max), w)
                link(nc.vector.tensor_tensor(pick, tmp[:, :, :], over(top[:, r, :], E), ALU.is_equal), w)

            def top2(w, i):
                tt, V = nc.vector.tensor_tensor, nc.vector
                if i == 0:
                    at[0] = 0
                    dve.wait_ge(token_drained, upto("token_drained", w, 4))
                    if w.has_before(1):
                        dve.wait_ge(top2_step, upto("top2_step", w.before(1)))
                    at_largest(w, logits[:, :, :], 0)
                elif i == 1:
                    first_of_them(w, 7, pick1[:, :, :])
                    link(V.scalar_tensor_tensor(out=logits[:, :, :], in0=pick1[:, :, :], scalar=BELOW_ALL,
                                                in1=logits[:, :, :], op0=ALU.mult, op1=ALU.add), w)
                elif i == 2:
                    at_largest(w, logits[:, :, :], 1)
                    if w.has_before(1):
                        dve.wait_ge(gap_exp, upto("gap_exp", w.before(1)))
                    assert at[0] == GAP_STEP
                    link(tt(top[:, 2, :], top[:, 1, :], top[:, 0, :], ALU.subtract), w)
                elif i == 3:
                    first_of_them(w, 6, pick2[:, :, :])
                else:
                    dve.wait_ge(gap_exp, upto("gap_exp", w))
                    link(V.tensor_scalar(top[:, 4, :], top[:, 3, :], 1.0, None, ALU.add), w)
                    link(V.reciprocal(top[:, 5, :], top[:, 4, :]), w)
                    link(tt(top[:, 4, :], top[:, 3, :], top[:, 5, :], ALU.mult), w)
                    assert at[0] == PROBS_STEP

            def mix(w, i):
                if i == 16:
                    return
                half, eh, a = i // E, i // A % 2, i % A
                dve.wait_ge(weight_filled, upto("weight_filled", w, 1 + i))
                if i == 0:
                    dve.wait_ge(x4_ready, upto("x4_ready", w))
                if eh == 0 and half:
                    dve.wait_ge(mixed, upto("mixed", w, 0))
                elif eh == 0:
                    if w.has_before(1):
                        dve.wait_ge(mixed, upto("mixed", w.before(1), 2))
                tokens = x4[:, a, HALF * half:HALF * half + HALF]
                nc.vector.tensor_tensor(tokens if eh else zt[:, a, :], ps_weight[(1 + i) % 2][:, 0:HALF], tokens,
                                        ALU.mult).then_inc(weight_drained, 1)

            def final(w, i):
                dve.wait_ge(weight_filled, upto("weight_filled", w, 17 + i))
                k0, k1 = (0, 4) if i == 0 else (4, 7)
                tokens = x2[w.par][:, :, k0:k1, :].rearrange("p j k c -> p k j c")
                nc.vector.tensor_tensor(
                    tokens, ps_weight[(17 + i) % 2][0:ROWS, 0:(k1 - k0) * 128].rearrange("p (k j c) -> p k j c", j=A, c=C),
                    tokens, ALU.add).then_inc(weight_drained, 1)

            V = nc.vector

            def ones(buf):
                for g in range(2):
                    ins = V.memset(buf[PAD * g:PAD * g + N, :, :, :, 16 + D * g:16 + D * g + D].rearrange(
                        "p q s h t -> p (q s h) t"), 1.0)
                return ins

            count = [0]

            def chain(ins):
                ins.then_inc(weight_step, 1)
                count[0] += 1
                dve.wait_ge(weight_step, count[0])

            def prepare():
                dve.wait_ge(weights_loaded, 32)
                dve.wait_ge(consts_loaded, 16)
                chain(V.tensor_scalar(biases[:, 3:4], biases[:, 0:1], SCALE, None, ALU.mult))
                chain(V.tensor_copy(eb[:, 0, :], eb_raw))
                chain(V.tensor_tensor(eb_rest[:, :], eb_raw, eb[:, 0, :], ALU.subtract))
                chain(V.tensor_copy(eb[:, 1, :], eb_rest[:, :]))
                chain(V.tensor_tensor(eb[:, 2, :], eb_rest[:, :], eb[:, 1, :], ALU.subtract))
                chain(V.tensor_copy(bv_parts[:, 0, :], bv_raw))
                chain(V.tensor_tensor(bv_rest[:, :], bv_raw, bv_parts[:, 0, :], ALU.subtract))
                chain(V.tensor_copy(bv_parts[:, 1, :], bv_rest[:, :]))
                chain(V.tensor_tensor(bv_parts[:, 2, :], bv_rest[:, :], bv_parts[:, 1, :], ALU.subtract))
                chain(V.tensor_scalar(bv_rows[:, 0, :], bv_parts[:, 0, :], ident[0:3, 0:1], None, ALU.mult))
                chain(V.scalar_tensor_tensor(out=bv_rows[:, 1, :], in0=bv_parts[:, 1, :], scalar=ident[0:3, 1:2],
                                            in1=bv_rows[:, 0, :], op0=ALU.mult, op1=ALU.add))
                chain(V.scalar_tensor_tensor(out=bv_rows[:, 0, :], in0=bv_parts[:, 2, :], scalar=ident[0:3, 2:3],
                                            in1=bv_rows[:, 1, :], op0=ALU.mult, op1=ALU.add))
                chain(V.tensor_copy(bv[0:3, :, :], bv_rows[:, 0, :].unsqueeze(1).to_broadcast([3, Q, C])))
                dve.wait_ge(rel_loaded, 16 * len(rel_list))
                for h in range(HEADS):
                    for kind in range(4):
                        ins = V.tensor_tensor(
                            bt[:, h, kind, 0:N].rearrange("p (j i) -> p j i", j=WS),
                            rel_raw[:, ::-1, ::-1, h].rearrange("p i j -> p j i"),
                            mask[:, kind, 0:N].rearrange("p (j i) -> p j i", j=WS), ALU.add)
                ins.then_inc(weights_ready, 1)

            V.memset(rel_raw[:, :, :, :], 0.0).then_inc(rel_zeroed, 1)
            V.memset(bv[:, :, :], 0.0)
            V.memset(bt[:, :, :, :], 0.0)
            V.memset(kp[:, :, :], 0.0)
            V.memset(mr[0][:, :], 0.0)
            V.memset(vb[0][:, :, :, :, :], 0.0).then_inc(zeroed, 1)
            dve.wait_ge(zeroed, 1)
            ones(vb[0])
            for step, unit, i in program(dve):
                if step == "norm1_center":
                    norm1_center(unit, i)
                elif step == "norm1_scale":
                    norm1_scale(unit, i)
                elif step == "norm2_center":
                    norm2_center(unit, i)
                elif step == "norm2_scale":
                    norm2_scale(unit, i)
                elif step == "prepare" and unit.number == 0:
                    prepare()
                elif step == "place" and unit.number == 0:
                    V.memset(vb[1][:, :, :, :, :], 0.0).then_inc(odd_v_zeroed, 1)
                    dve.wait_ge(odd_v_zeroed, 1)
                    ones(vb[1]).then_inc(odd_v_zeroed, 1)
                elif step == "maximum":
                    maximum(unit, i)
                elif step == "split":
                    split(unit, i)
                elif step == "spread_sums":
                    spread_sums(unit, i)
                elif step == "invert":
                    invert(unit, i)
                elif step == "back":
                    residual(unit, i)
                elif step == "router":
                    router(unit, i)
                elif step == "top2" and i < 5:
                    top2(unit, i)
                elif step == "mix":
                    mix(unit, i)
                elif step == "final":
                    final(unit, i)

        @block.tensor
        def _(pe):
            mm = nc.tensor.matmul

            def xt_turn(v, i):
                if v.has_before(1):
                    pe.wait_ge(pre_drained, upto("pre_drained", v, i - 1))
                pe.wait_ge(normed1, upto("normed1", v))
                for k in range(*((0, 4) if i == 0 else (4, 7))):
                    ins = nc.tensor.transpose(pre_bank(v, i)[:, (k % 4) * ROWS:(k % 4) * ROWS + ROWS],
                                              xc1[:, k, :, :].rearrange("p j c -> p (j c)"), ident[0:ROWS, 0:ROWS])
                ins.then_inc(pre_filled, 1)

            def qk(v, i):
                pe.wait_ge(pre_drained, upto("pre_drained", v, pre_free(v, 2 + i)))
                b = i % 2
                mm(pre_bank(v, 2 + i)[:, 0:HALF], (wq if i < 2 else wk)[:, :],
                        xt[:, 8 * b:8 * b + 8, :, :].rearrange("p q k i -> p (q k i)"), start=True, stop=True).then_inc(pre_filled, 1)

            def v_products(v, i):
                pe.wait_ge(pre_drained, upto("pre_drained", v, pre_free(v, 6 + i)))
                bank = pre_bank(v, 6 + i)
                mm(bank[:, :], first3[:, :], bv[:, :, :].rearrange("p q c -> p (q c)"), start=True, stop=False,
                   skip_group_check=True)
                for q in range(8):
                    keys = xt[:, 8 * i + q, :, :].rearrange("p k i -> p (k i)")
                    for g in range(2):
                        ins = mm(bank[PAD * g:PAD * g + N, 64 * q:64 * q + 64], keys,
                                 wv[:, g, :, :].rearrange("p s c -> p (s c)"), start=False,
                                 stop=(q == 7), skip_group_check=True)
                ins.then_inc(pre_filled, 1)

            def ob(v, i):
                pe.wait_ge(pre_drained, upto("pre_drained", v, pre_free(v, 8 + i)))
                for hh in range(2):
                    h = 2 * hh + i
                    for p in range(2):
                        for last_row in range(2):
                            kind = last_row + 2 * (v.par and p)
                            w0, w1 = (WS, WS + 1) if last_row else (0, WS)
                            dst = pre_bank(v, 8 + i)[PAD * hh:PAD * hh + PAD, 256 * p:256 * p + 256].rearrange(
                                "p (b i s) -> p b i s", b=2, s=16)[:, :, w0:w1, :]
                            src = vb[v.par][:, :, p, h, 0:16].rearrange("p (b i) s -> p b i s", b=2)[:, :, w0:w1, :]
                            ins = mm(dst, bt[:, h, kind, :], src, start=True, stop=True)
                ins.then_inc(pre_filled, 1)

            def ob_turn(v, i):
                pe.wait_ge(pre_drained, upto("pre_drained", v, pre_free(v, 10 + i)))
                for k in range(4):
                    ins = nc.tensor.transpose(pre_bank(v, 10 + i)[:, 128 * k:128 * k + 128],
                                              obs[:, 4 * i + k, :, :, :, :].rearrange("p b h s t -> p (b h s t)"),
                                              ident[:, :])
                ins.then_inc(pre_filled, 1)

            def max_scores(u, q):
                if u.number == 0 and q < AHEAD:
                    if q >= 2:
                        pe.wait_ge(max_taken, upto("max_taken", u, q - 2))
                    elif q == 1:
                        pe.wait_ge(pre_drained, upto("pre_drained", u))
                else:
                    pe.wait_ge(max_taken, upto("max_taken", u, q - 1))
                if q == 0:
                    pe.wait_ge(q_placed, upto("q_placed", u))
                    pe.wait_ge(k_placed, upto("k_placed", u))
                for s in range(2):
                    ins = mm(max_bank(u, q)[0:2 * N, A * EVEN * s:A * EVEN * s + A * EVEN],
                             qbd[u.par][:, q, 2 * s:2 * s + 2, :].rearrange("p h n -> p (h n)").bitcast(F32R),
                             kz[u.par][:, q, :, 0:EVEN].bitcast(F32R), start=True, stop=True)
                ins.then_inc(max_filled, 1)

            def shift_turn(u, g):
                pe.wait_ge(shift_split, upto("shift_split", u, g))
                for s in range(2):
                    ins = nc.tensor.transpose(
                        ps_scores[0:32, :].bitcast(BF16)[:, 2 * N * s:2 * N * s + 2 * N],
                        ms[g % 2][:, s, :, :].rearrange("p k r -> p (k r)"), identb[0:2 * N, 0:2 * N])
                ins.then_inc(shift_turned, 1)

            def scores(u, q):
                if q % 4 == SHIFT_STEP + 1:
                    if q + 1 < Q:
                        pe.wait_ge(shift_rows_ready, upto("shift_rows_ready", u, q // 4 + 1))
                    elif u.has_after():
                        pe.wait_ge(shift_rows_ready, upto("shift_rows_ready", u.after(), 0))
                elif q == 0:
                    pe.wait_ge(shift_rows_ready, upto("shift_rows_ready", u, 0))
                for p in range(2):
                    dst = ps_scores[:, HN * p:HN * p + HN]
                    mm(dst, shift_sel[:, q % 4, p, :], mr[(q // 4) % 2][:, :], start=True, stop=False)
                    ins = mm(dst, kz[u.par][:, q, 2 * p:2 * p + 2, :].rearrange("p a m -> p (a m)"),
                             qbd[u.par][:, q, :, :].rearrange("p h n -> p (h n)"), start=False, stop=True)
                ins.then_inc(scores_filled, 1)

            def pv(u, q):
                pe.wait_ge(probs_ready, upto("probs_ready", u, q))
                if q % 4 == 0:
                    if q // 4 or u.has_before(1):
                        pe.wait_ge(pv_drained, upto("pv_drained", u, q // 4 - 1))
                for p in range(2):
                    c0 = (2 * (q % 4) + p) * N
                    for h in range(HEADS):
                        ins = mm(ps_pv[SLOT * h:SLOT * h + SLOT, c0:c0 + N], vb[u.par][:, q, p, h, :],
                                 pt[q % 2][:, p, h, :], start=True, stop=True)
                ins.then_inc(pv_done, 1)

            def y(w, b):
                if b:
                    pe.wait_ge(y_drained, upto("y_drained", w, 0))
                elif w.has_before(2):
                    pe.wait_ge(sum_drained, upto("sum_drained", w.before(2)))
                elif w.has_before(1):
                    pe.wait_ge(y_drained, upto("y_drained", w.before(1)))
                for hh in range(2):
                    mm(ps_acc[:, 0:HALF], w_proj_b[:, b, hh, :, :].rearrange("p a c -> p (a c)"),
                       obt[w.par][:, hh, :, :].rearrange("p i n -> p (i n)"), start=(hh == 0), stop=False,
                       skip_group_check=True)
                if b == 0:
                    pe.wait_ge(o_normed, upto("o_normed", w))
                for p in range(2):
                    ins = mm(ps_acc[64 * p:64 * p + 64, 0:HALF], w_proj_o[:, :, :].rearrange("p g c -> p (g c)"),
                             on[:, p, 8 * b:8 * b + 8, :].rearrange("p q n -> p (q n)"), start=False, stop=True,
                             skip_group_check=True)
                ins.then_inc(projected, 1)

            def turn_back(bank, i):
                for k in range(*((0, 4) if i == 0 else (4, 7))):
                    ins = nc.tensor.transpose(bank[0:ROWS, (k % 4) * 128:(k % 4) * 128 + 128], ym[:, k, :],
                                              ident[:, :])
                return ins

            def back(w, i):
                pe.wait_ge(y_drained, upto("y_drained", w))
                if i or w.has_before(1):
                    pe.wait_ge(token_drained, upto("token_drained", w, i - 1))
                turn_back(ps_token, i).then_inc(token_filled, 1)

            def x2t_turn(w, i):
                pe.wait_ge(token_drained, upto("token_drained", w, 1 + i))
                pe.wait_ge(normed2, upto("normed2", w))
                for k in range(*((0, 4) if i == 0 else (4, 7))):
                    ins = nc.tensor.transpose(ps_token[:, (k % 4) * ROWS:(k % 4) * ROWS + ROWS],
                                              xc2[:, k, :, :].rearrange("p j c -> p (j c)"), ident[0:ROWS, 0:ROWS])
                ins.then_inc(token_filled, 1)

            def router(w, _):
                pe.wait_ge(token_drained, upto("token_drained", w, 3))
                for k in range(WS):
                    ins = mm(ps_token[0:ROWS, 32 * k:32 * k + 32], x2t[:, ROWS * k:ROWS * k + ROWS],
                             wr[:, :, :].rearrange("p a e -> p (a e)"), start=True, stop=True)
                ins.then_inc(token_filled, 1)

            def wt_turn(w, _):
                if w.has_before(1):
                    pe.wait_ge(weight_drained, upto("weight_drained", w.before(1)))
                pe.wait_ge(top2_step, upto("top2_step", w))
                for k in range(WS):
                    ins = nc.tensor.transpose(ps_weight[0][0:96, :].bitcast(BF16)[:, ROWS * k:ROWS * k + ROWS],
                                              w_parts[:, k, :, :].rearrange("p t e -> p (t e)"),
                                              identb[0:ROWS, 0:ROWS])
                ins.then_inc(weight_filled, 1)

            def mix(w, i):
                if i < 16:
                    half, eh, a = i // E, i // A % 2, i % A
                    if i < 2:
                        pe.wait_ge(weight_drained, upto("weight_drained", w, 0))
                    else:
                        pe.wait_ge(weight_drained, upto("weight_drained", w, i - 1))
                    mm(ps_weight[(1 + i) % 2][:, 0:HALF], weight_sel[:, eh, a, :], wt[:, HALF * half:HALF * half + HALF],
                            start=True, stop=True).then_inc(weight_filled, 1)
                if i not in MIX_PRODUCTS:
                    return
                half, eh = divmod(MIX_PRODUCTS.index(i), 2)
                if eh == 0:
                    if half:
                        pe.wait_ge(sum_drained, upto("sum_drained", w, 0))
                    elif w.has_after():
                        pe.wait_ge(y_drained, upto("y_drained", w.after()))
                    else:
                        pe.wait_ge(sum_drained, upto("sum_drained", w.before(1)))
                    for k in range(3):
                        mm(ps_acc[:, 0:HALF], eb[:, k, :], wt[:, HALF * half:HALF * half + HALF],
                           start=(k == 0), stop=False, skip_group_check=True)
                pe.wait_ge(weight_drained, upto("weight_drained", w, E * half + A * eh + A))
                for a in range(A):
                    tokens = x4[:, a, HALF * half:HALF * half + HALF] if eh else zt[:, a, :]
                    ins = mm(ps_acc[C * a:C * a + C, 0:HALF], we[:, eh, :], tokens, start=False, stop=(eh == 1),
                             skip_group_check=True)
                ins.then_inc(mixed, 1)

            def final(w, i):
                pe.wait_ge(sum_drained, upto("sum_drained", w))
                pe.wait_ge(weight_drained, upto("weight_drained", w, 15 + i))
                turn_back(ps_weight[(17 + i) % 2], i).then_inc(weight_filled, 1)

            pe.wait_ge(consts_loaded, 16)
            for step, unit, i in program(pe):
                if step == "xt":
                    xt_turn(unit, i)
                elif step == "prepare" and unit.number == 0:
                    pe.wait_ge(weights_ready, 1)
                elif step == "qk":
                    qk(unit, i)
                elif step == "v":
                    v_products(unit, i)
                elif step == "ob":
                    ob(unit, i)
                elif step == "obt":
                    ob_turn(unit, i)
                elif step == "maximum":
                    max_scores(unit, i)
                elif step == "shift":
                    shift_turn(unit, i)
                elif step == "scores":
                    scores(unit, i)
                elif step == "pv":
                    pv(unit, i)
                elif step == "y":
                    y(unit, i)
                elif step == "back":
                    back(unit, i)
                elif step == "x2t":
                    x2t_turn(unit, i)
                elif step == "router":
                    router(unit, i)
                elif step == "wt":
                    wt_turn(unit, i)
                elif step == "mix":
                    mix(unit, i)
                elif step == "final":
                    final(unit, i)


def kernel(x, L0_conv_w_qkv, L0_conv_b_qkv, L0_conv_w_proj, L0_conv_b_proj, L0_conv_rel_table,
           L0_ffn_router_w, L0_ffn_router_b, L0_ffn_expert_w, L0_ffn_expert_b):
    import ml_dtypes
    import concourse.bacc as bacc
    from concourse.bass_utils import run_bass_kernel_spmd

    given = [np.asarray(t) for t in (L0_conv_w_qkv, L0_conv_b_qkv, L0_conv_w_proj, L0_conv_b_proj, L0_ffn_router_w,
                                     L0_ffn_router_b, L0_ffn_expert_w, L0_ffn_expert_b)]
    constants = shape_constants()
    arrays = {
        "x": np.ascontiguousarray(x),
        "weights": laid_out_weights(*given),
        "rel_table": np.ascontiguousarray(np.asarray(L0_conv_rel_table)[::-1]),
        "consts": side_by_side(constants, CONST_COLS),
        "consts_bf16": side_by_side(constants, CONST_BF16_COLS).astype(ml_dtypes.bfloat16),
    }
    nc = bacc.Bacc("TRN2", target_bir_lowering=False, num_devices=1)
    args = [nc.dram_tensor(name, a.shape, mybir.dt.from_np(a.dtype), kind="ExternalInput").ap()
            for name, a in arrays.items()]
    args.append(nc.dram_tensor("out", (IMAGES, SIDE, SIDE, C), F32, kind="ExternalOutput").ap())
    metaformer_block(nc, *args)
    return run_bass_kernel_spmd(nc, [arrays], core_ids=[0]).results[0]["out"]
```
